# Optimizing a Trainium2 kernel written in Bass

```python
import numpy as np
import jax
import jax.numpy as jnp

def _softmax(x, axis=-1):
    return jax.nn.softmax(x, axis=axis)

def _gelu(x):
    return jax.nn.gelu(x, approximate=True)

def _silu(x):
    return jax.nn.silu(x)

def _sigmoid(x):
    return jax.nn.sigmoid(x)

def _layernorm(x, axis=-1, eps=1e-05):
    m = jnp.mean(x, axis=axis, keepdims=True)
    v = jnp.var(x, axis=axis, keepdims=True)
    return (x - m) / jnp.sqrt(v + eps)

def _scatter_add(tgt, idx, src, axis=0):
    return tgt.at[idx].add(src)

def _segment_sum(src, seg, n):
    return jax.ops.segment_sum(src, seg, n)
kernel_name = 'mk_adaln_d2_jaxref_r8_429ca6'

def setup_inputs(seed: int=0):
    np.random.seed(seed)
    _w = jnp.asarray

    def _L0_attn_setup():
        import jax, jax.numpy as jnp
        import numpy as np
        DIM = 128
        HEADS = 16
        HEAD_DIM = DIM // HEADS
        COLLAPSE_THRESHOLD = 0.27
        SHARPNESS = 15.0
        LN_EPS = 1e-05
        NORM_EPS = 1e-12

        def _layernorm(x, gamma, beta):
            mu = jnp.mean(x, axis=-1, keepdims=True)
            var = jnp.mean(jnp.square(x - mu), axis=-1, keepdims=True)
            return (x - mu) * jax.lax.rsqrt(var + LN_EPS) * gamma + beta

        def _l2_normalize(x):
            n = jnp.sqrt(jnp.sum(jnp.square(x), axis=-1, keepdims=True))
            return x / jnp.maximum(n, NORM_EPS)
        key = jax.random.key(seed)
        ks = jax.random.split(key, 9)
        B, T = (2, 256)
        s = 1.0 / np.sqrt(DIM)
        sh = 1.0 / np.sqrt(HEAD_DIM)
        return {'x': jax.random.normal(ks[0], (B, T, DIM), dtype=jnp.float32), 'w_q': jax.random.normal(ks[1], (DIM, DIM), dtype=jnp.float32) * s, 'w_k': jax.random.normal(ks[2], (DIM, DIM), dtype=jnp.float32) * s, 'w_v': jax.random.normal(ks[3], (DIM, DIM), dtype=jnp.float32) * s, 'g_q': jax.random.normal(ks[4], (HEAD_DIM,), dtype=jnp.float32) * sh, 'g_k': jax.random.normal(ks[5], (HEAD_DIM,), dtype=jnp.float32) * sh, 'w_o': jax.random.normal(ks[6], (DIM, DIM), dtype=jnp.float32) * s, 'b_o': jnp.zeros((DIM,), dtype=jnp.float32), 'gamma': jnp.ones((DIM,), dtype=jnp.float32), 'beta': jnp.zeros((DIM,), dtype=jnp.float32)}
    _L0_attn_in = _L0_attn_setup()

    def _L0_ffn_setup():
        import jax, jax.numpy as jnp
        import numpy as np
        DM = 128
        NEXPERTS = 32
        EXPERTSETS = 4
        EXPERTSIZE = 32
        BATCH, SEQ = (4, 256)
        key = jax.random.key(seed)
        k0, k1, k2, k3 = jax.random.split(key, 4)
        scale = 0.02
        x = jax.random.normal(k0, (BATCH, SEQ, DM), jnp.float32)
        controller = jax.random.normal(k1, (DM, NEXPERTS, EXPERTSETS), jnp.float32) * scale
        f1 = jax.random.normal(k2, (DM, NEXPERTS, EXPERTSETS, EXPERTSIZE), jnp.float32) * scale
        bias = jnp.zeros((NEXPERTS, EXPERTSETS, EXPERTSIZE), jnp.float32)
        f2 = jax.random.normal(k3, (NEXPERTS, EXPERTSETS, EXPERTSIZE, DM), jnp.float32) * scale
        return {'x': x, 'controller': controller, 'f1': f1, 'bias': bias, 'f2': f2}
    _L0_ffn_in = _L0_ffn_setup()
    _L0_c = _w((lambda *s: np.random.randn(*s).astype(np.float32) * 0.05)(32, 128))
    _L0_wmod = _w((lambda *s: np.random.randn(*s).astype(np.float32) * 0.05)(128, 6 * 128) * 128 ** (-0.5))

    def _L1_attn_setup():
        import jax, jax.numpy as jnp
        import numpy as np
        D_MODEL = 128
        HEADS = 16
        D_K = D_MODEL // HEADS
        ROPE_BASE = 10000.0

        def _rope(x, pos_offset=0):
            S, d = (x.shape[-2], x.shape[-1])
            inv_freq = 1.0 / ROPE_BASE ** (jnp.arange(0, d, 2, dtype=jnp.float32) / d)
            pos = jnp.arange(S, dtype=jnp.float32) + pos_offset
            ang = pos[:, None] * inv_freq[None, :]
            cos, sin = (jnp.cos(ang), jnp.sin(ang))
            x1, x2 = (x[..., :d // 2], x[..., d // 2:])
            return jnp.concatenate([x1 * cos - x2 * sin, x1 * sin + x2 * cos], axis=-1)
        key = jax.random.key(seed)
        ks = jax.random.split(key, 5)
        B, S = (2, 256)
        x = jax.random.normal(ks[0], (B, S, D_MODEL), dtype=jnp.float32)
        w = lambda k: jax.random.normal(k, (D_MODEL, D_MODEL), dtype=jnp.float32) * 0.02
        z = jnp.zeros((D_MODEL,), dtype=jnp.float32)
        return {'x': x, 'Wq': w(ks[1]), 'bq': z, 'Wk': w(ks[2]), 'bk': z, 'Wv': w(ks[3]), 'bv': z, 'Wo': w(ks[4]), 'bo': z}
    _L1_attn_in = _L1_attn_setup()

    def _L1_ffn_setup():
        import jax, jax.numpy as jnp
        import numpy as np
        D_IN, D_HID = (128, 512)

        def _ternary(key, shape):
            return jax.random.randint(key, shape, -1, 2).astype(jnp.float32)

        def _tlin(x, w, s):
            return jnp.einsum('bsi,oi->bso', x, w) * s
        key = jax.random.key(seed)
        ks = jax.random.split(key, 12)
        inv = lambda fan: 1.0 / np.sqrt(fan).astype(np.float32)
        return {'x': jax.random.normal(ks[0], (4, 256, D_IN), dtype=jnp.float32), 'w1_w': _ternary(ks[1], (D_HID, D_IN)), 'w1_s': jax.random.uniform(ks[2], (D_HID,), dtype=jnp.float32) * inv(D_IN), 'w2_w': _ternary(ks[3], (D_HID, D_IN)), 'w2_s': jax.random.uniform(ks[4], (D_HID,), dtype=jnp.float32) * inv(D_IN), 'h1_w': _ternary(ks[5], (D_HID, D_HID)), 'h1_s': jax.random.uniform(ks[6], (D_HID,), dtype=jnp.float32) * inv(D_HID), 'h2_w': _ternary(ks[7], (D_HID, D_HID)), 'h2_s': jax.random.uniform(ks[8], (D_HID,), dtype=jnp.float32) * inv(D_HID), 'w3_w': _ternary(ks[9], (D_IN, D_HID)), 'w3_s': jax.random.uniform(ks[10], (D_IN,), dtype=jnp.float32) * inv(D_HID)}
    _L1_ffn_in = _L1_ffn_setup()
    _L1_c = _w((lambda *s: np.random.randn(*s).astype(np.float32) * 0.05)(32, 128))
    _L1_wmod = _w((lambda *s: np.random.randn(*s).astype(np.float32) * 0.05)(128, 6 * 128) * 128 ** (-0.5))
    _d = {'L0_attn_x': _L0_attn_in['x'], 'L0_attn_w_q': _L0_attn_in['w_q'], 'L0_attn_w_k': _L0_attn_in['w_k'], 'L0_attn_w_v': _L0_attn_in['w_v'], 'L0_attn_g_q': _L0_attn_in['g_q'], 'L0_attn_g_k': _L0_attn_in['g_k'], 'L0_attn_w_o': _L0_attn_in['w_o'], 'L0_attn_b_o': _L0_attn_in['b_o'], 'L0_attn_gamma': _L0_attn_in['gamma'], 'L0_attn_beta': _L0_attn_in['beta'], 'L0_ffn_controller': _L0_ffn_in['controller'], 'L0_ffn_f1': _L0_ffn_in['f1'], 'L0_ffn_bias': _L0_ffn_in['bias'], 'L0_ffn_f2': _L0_ffn_in['f2'], 'L0_c': _L0_c, 'L0_wmod': _L0_wmod, 'L1_attn_Wq': _L1_attn_in['Wq'], 'L1_attn_bq': _L1_attn_in['bq'], 'L1_attn_Wk': _L1_attn_in['Wk'], 'L1_attn_bk': _L1_attn_in['bk'], 'L1_attn_Wv': _L1_attn_in['Wv'], 'L1_attn_bv': _L1_attn_in['bv'], 'L1_attn_Wo': _L1_attn_in['Wo'], 'L1_attn_bo': _L1_attn_in['bo'], 'L1_ffn_w1_w': _L1_ffn_in['w1_w'], 'L1_ffn_w1_s': _L1_ffn_in['w1_s'], 'L1_ffn_w2_w': _L1_ffn_in['w2_w'], 'L1_ffn_w2_s': _L1_ffn_in['w2_s'], 'L1_ffn_h1_w': _L1_ffn_in['h1_w'], 'L1_ffn_h1_s': _L1_ffn_in['h1_s'], 'L1_ffn_h2_w': _L1_ffn_in['h2_w'], 'L1_ffn_h2_s': _L1_ffn_in['h2_s'], 'L1_ffn_w3_w': _L1_ffn_in['w3_w'], 'L1_ffn_w3_s': _L1_ffn_in['w3_s'], 'L1_c': _L1_c, 'L1_wmod': _L1_wmod}
    _x0 = _d['L0_attn_x']
    _d['L0_attn_x'] = jax.random.normal(jax.random.fold_in(jax.random.key(seed), 1), (32, 256, 128), dtype=_x0.dtype)
    del _x0
    return _d

def reference(L0_attn_x, L0_attn_w_q, L0_attn_w_k, L0_attn_w_v, L0_attn_g_q, L0_attn_g_k, L0_attn_w_o, L0_attn_b_o, L0_attn_gamma, L0_attn_beta, L0_ffn_controller, L0_ffn_f1, L0_ffn_bias, L0_ffn_f2, L0_c, L0_wmod, L1_attn_Wq, L1_attn_bq, L1_attn_Wk, L1_attn_bk, L1_attn_Wv, L1_attn_bv, L1_attn_Wo, L1_attn_bo, L1_ffn_w1_w, L1_ffn_w1_s, L1_ffn_w2_w, L1_ffn_w2_s, L1_ffn_h1_w, L1_ffn_h1_s, L1_ffn_h2_w, L1_ffn_h2_s, L1_ffn_w3_w, L1_ffn_w3_s, L1_c, L1_wmod):

    def _L0_attn_ref(x, w_q, w_k, w_v, g_q, g_k, w_o, b_o, gamma, beta):
        import jax, jax.numpy as jnp
        import numpy as np
        DIM = 128
        HEADS = 16
        HEAD_DIM = DIM // HEADS
        COLLAPSE_THRESHOLD = 0.27
        SHARPNESS = 15.0
        LN_EPS = 1e-05
        NORM_EPS = 1e-12

        def _layernorm(x, gamma, beta):
            mu = jnp.mean(x, axis=-1, keepdims=True)
            var = jnp.mean(jnp.square(x - mu), axis=-1, keepdims=True)
            return (x - mu) * jax.lax.rsqrt(var + LN_EPS) * gamma + beta

        def _l2_normalize(x):
            n = jnp.sqrt(jnp.sum(jnp.square(x), axis=-1, keepdims=True))
            return x / jnp.maximum(n, NORM_EPS)
        B, T, D = x.shape
        x_norm = _layernorm(x, gamma, beta)
        q = (x_norm @ w_q).reshape(B, T, HEADS, HEAD_DIM).transpose(0, 2, 1, 3)
        k = (x_norm @ w_k).reshape(B, T, HEADS, HEAD_DIM).transpose(0, 2, 1, 3)
        v = (x @ w_v).reshape(B, T, HEADS, HEAD_DIM).transpose(0, 2, 1, 3)
        q = _l2_normalize(q)
        k = _l2_normalize(k)
        align = jnp.einsum('bhqd,bhkd->bhqk', q, k)
        resonance = 0.5 + 0.5 * jnp.tanh((align - COLLAPSE_THRESHOLD) * SHARPNESS)
        gate_q = 0.25 + 0.75 * jax.nn.sigmoid(jnp.einsum('bhtd,d->bht', q, g_q))
        gate_k = 0.25 + 0.75 * jax.nn.sigmoid(jnp.einsum('bhtd,d->bht', k, g_k))
        modulation = resonance * gate_q[..., :, None] * gate_k[..., None, :]
        fused = jnp.einsum('bhqk,bhkd->bhqd', modulation, v)
        fused = fused.transpose(0, 2, 1, 3).reshape(B, T, HEADS * HEAD_DIM)
        return fused @ w_o + b_o

    def _L0_ffn_ref(x, controller, f1, bias, f2):
        import jax, jax.numpy as jnp
        import numpy as np
        DM = 128
        NEXPERTS = 32
        EXPERTSETS = 4
        EXPERTSIZE = 32
        BATCH, SEQ = (4, 256)
        B, L, d = x.shape
        t = controller.shape[1]
        g = L // t
        grouped = x.reshape(B, g, t, d)
        logits = jnp.einsum('bgtd,des->bgtes', grouped, controller)
        tie = jnp.linspace(0.0, 1e-06, t, dtype=logits.dtype).reshape(t, 1, 1)
        logits = logits + tie
        perm = (logits == jnp.max(logits, axis=-3, keepdims=True)).astype(x.dtype)
        perm = jax.lax.stop_gradient(perm)
        dispatched = jnp.einsum('bgtd,bgtes->bgesd', grouped, perm)
        inner = jax.nn.relu(jnp.einsum('bgesd,desf->bgesf', dispatched, f1) + bias)
        intermediate = jnp.einsum('bgesf,esfd->bgesd', inner, f2)
        out = jnp.einsum('bgesd,bgtes->bgtd', intermediate, perm)
        return out.reshape(B, L, d)

    def _L1_attn_ref(x, Wq, bq, Wk, bk, Wv, bv, Wo, bo):
        import jax, jax.numpy as jnp
        import numpy as np
        D_MODEL = 128
        HEADS = 16
        D_K = D_MODEL // HEADS
        ROPE_BASE = 10000.0

        def _rope(x, pos_offset=0):
            S, d = (x.shape[-2], x.shape[-1])
            inv_freq = 1.0 / ROPE_BASE ** (jnp.arange(0, d, 2, dtype=jnp.float32) / d)
            pos = jnp.arange(S, dtype=jnp.float32) + pos_offset
            ang = pos[:, None] * inv_freq[None, :]
            cos, sin = (jnp.cos(ang), jnp.sin(ang))
            x1, x2 = (x[..., :d // 2], x[..., d // 2:])
            return jnp.concatenate([x1 * cos - x2 * sin, x1 * sin + x2 * cos], axis=-1)
        B, S, _ = x.shape

        def split_heads(t):
            return t.reshape(B, S, HEADS, D_K).transpose(0, 2, 1, 3)
        q = split_heads(x @ Wq + bq)
        k = split_heads(x @ Wk + bk)
        v = split_heads(x @ Wv + bv)
        q = _rope(q, pos_offset=0)
        k = _rope(k, pos_offset=0)
        scores = jnp.einsum('bhqd,bhkd->bhqk', q, k) / np.sqrt(D_K).astype(np.float32)
        probs = jax.nn.softmax(scores, axis=-1)
        attn = jnp.einsum('bhqk,bhkd->bhqd', probs, v)
        out = attn.transpose(0, 2, 1, 3).reshape(B, S, D_MODEL)
        return out @ Wo + bo

    def _L1_ffn_ref(x, w1_w, w1_s, w2_w, w2_s, h1_w, h1_s, h2_w, h2_s, w3_w, w3_s):
        import jax, jax.numpy as jnp
        import numpy as np
        D_IN, D_HID = (128, 512)

        def _ternary(key, shape):
            return jax.random.randint(key, shape, -1, 2).astype(jnp.float32)

        def _tlin(x, w, s):
            return jnp.einsum('bsi,oi->bso', x, w) * s
        h = jax.nn.silu(_tlin(x, w1_w, w1_s)) * _tlin(x, w2_w, w2_s)
        h = jax.nn.gelu(_tlin(h, h1_w, h1_s), approximate=False)
        h = jax.nn.gelu(_tlin(h, h2_w, h2_s), approximate=False)
        return _tlin(h, w3_w, w3_s)
    x = L0_attn_x
    mod = (_silu(L0_c) @ L0_wmod).reshape(L0_c.shape[0], 6, 1, -1)
    sa, ca, ga, sb, cb, gb = (mod[:, 0], mod[:, 1], mod[:, 2], mod[:, 3], mod[:, 4], mod[:, 5])
    ga = (2 * (ga >= 0) - 1) * jnp.maximum(jnp.abs(ga), 0.25)
    gb = (2 * (gb >= 0) - 1) * jnp.maximum(jnp.abs(gb), 0.25)
    h = _layernorm(x, axis=-1) * (1 + ca) + sa
    x = x + ga * _L0_attn_ref(h, L0_attn_w_q, L0_attn_w_k, L0_attn_w_v, L0_attn_g_q, L0_attn_g_k, L0_attn_w_o, L0_attn_b_o, L0_attn_gamma, L0_attn_beta)
    h = _layernorm(x, axis=-1) * (1 + cb) + sb
    x = x + gb * _L0_ffn_ref(h, L0_ffn_controller, L0_ffn_f1, L0_ffn_bias, L0_ffn_f2)
    mod = (_silu(L1_c) @ L1_wmod).reshape(L1_c.shape[0], 6, 1, -1)
    sa, ca, ga, sb, cb, gb = (mod[:, 0], mod[:, 1], mod[:, 2], mod[:, 3], mod[:, 4], mod[:, 5])
    ga = (2 * (ga >= 0) - 1) * jnp.maximum(jnp.abs(ga), 0.25)
    gb = (2 * (gb >= 0) - 1) * jnp.maximum(jnp.abs(gb), 0.25)
    h = _layernorm(x, axis=-1) * (1 + ca) + sa
    x = x + ga * _L1_attn_ref(h, L1_attn_Wq, L1_attn_bq, L1_attn_Wk, L1_attn_bk, L1_attn_Wv, L1_attn_bv, L1_attn_Wo, L1_attn_bo)
    h = _layernorm(x, axis=-1) * (1 + cb) + sb
    x = x + gb * _L1_ffn_ref(h, L1_ffn_w1_w, L1_ffn_w1_s, L1_ffn_w2_w, L1_ffn_w2_s, L1_ffn_h1_w, L1_ffn_h1_s, L1_ffn_h2_w, L1_ffn_h2_s, L1_ffn_w3_w, L1_ffn_w3_s)
    return x

_drawn_inputs = setup_inputs


def setup_inputs(seed=0):
    import zlib

    import numpy as np

    out = dict(_drawn_inputs(seed))
    spreads = {'L0_attn_b_o': (0.0, 0.1),
     'L0_attn_gamma': (1.0, 0.2),
     'L0_attn_beta': (0.0, 0.1),
     'L0_ffn_bias': (0.0, 0.1),
     'L1_attn_bq': (0.0, 0.1),
     'L1_attn_bk': (0.0, 0.1),
     'L1_attn_bv': (0.0, 0.1),
     'L1_attn_bo': (0.0, 0.1)}
    factors = {}
    for name, (base, spread) in spreads.items():
        noise = np.random.default_rng([zlib.crc32(name.encode()), seed]).standard_normal(out[name].shape)
        drawn = base * np.exp(spread * noise) if base else spread * noise
        out[name] = jnp.asarray(drawn.astype(out[name].dtype))
    for name, factor in factors.items():
        out[name] = (out[name] * factor).astype(out[name].dtype)
    return out
```

```python
from contextlib import ExitStack

import numpy as np

import concourse.bass as bass
from concourse import mybir

F32 = mybir.dt.float32
F32R = mybir.dt.float32r
F16 = mybir.dt.float16
I32 = mybir.dt.int32
ALU = mybir.AluOpType
ACT = mybir.ActivationFunctionType
AX = mybir.AxisListType

P = 128
B = 32
T = 256
D = 128
TT = T // P
H = 16
HD = D // H
G = 4
MOD = 6 * D
LN_EPS = 1e-5
CHUNKS = 8
UNIT = 257
UNIT_PAD = 260

ROW_CA0, ROW_SA0, ROW_GA0, ROW_GABO0, ROW_CB0, ROW_SB0, ROW_GB0, ROW_GA1, ROW_GABO1 = range(9)
ROWS = 9
SA, CA, GA, SB, CB, GB = range(6)

NORM_FLOOR = 1e-24
SPLIT_SCALE = 64.0
COLLAPSE, SHARPNESS = 0.27, 15.0
RSQRT_MAGIC = float(0x5F3759DF)
RSQRT_STEPS = 11


def wait(eng, sem, n):
    if isinstance(n, int) and n <= 0:
        return
    eng.wait_ge(sem, n)


def stepped(eng, first, last, pair_first, pair_count, step):
    for b in range(first, pair_first):
        step(b, b % 2)
    with eng.Fori(0, pair_count) as i:
        step(i * 2 + pair_first, pair_first % 2)
        step(i * 2 + (pair_first + 1), (pair_first + 1) % 2)
    for b in range(pair_first + 2 * pair_count, last + 1):
        step(b, b % 2)


def setup_phase(nc, ctx, dram, sbuf, psum):
    def sem(name):
        return dram["semaphores"].enter_context(nc.semaphore(name))

    cond_loaded, wmod_loaded = sem("cond_loaded"), sem("wmod_loaded")
    weights_loaded, tanh_ready, silu_step = sem("weights_loaded"), sem("tanh_ready"), sem("silu_step")
    mod_psum, rows_step, rows_ready, table_stored = sem("mod_psum"), sem("rows_step"), sem("rows_ready"), sem("table_stored")
    cond = ctx.enter_context(nc.sbuf_tensor("cond", [P, 2, B], F32))
    cond_tanh = ctx.enter_context(nc.sbuf_tensor("cond_tanh", [P, 2, B], F32))
    cond_twice = ctx.enter_context(nc.sbuf_tensor("cond_twice", [P, 2, B], F32))
    cond_silu = ctx.enter_context(nc.sbuf_tensor("cond_silu", [P, 2, B], F32))
    wmod = ctx.enter_context(nc.sbuf_tensor("wmod", [P, 2, MOD], F32))
    bo_rows = ctx.enter_context(nc.sbuf_tensor("bo_rows", [B, 2, D], F32))
    rows = ctx.enter_context(nc.sbuf_tensor("rows", [B, ROWS, D], F32))
    sign = ctx.enter_context(nc.sbuf_tensor("sign", [B, 3, D], F32))
    size = ctx.enter_context(nc.sbuf_tensor("size", [B, 3, D], F32))
    minus = ctx.enter_context(nc.sbuf_tensor("minus", [B, 3, D], F32))
    col_minus = ctx.enter_context(nc.sbuf_tensor("col_minus", [P, B], F32))
    col_sign = ctx.enter_context(nc.sbuf_tensor("col_sign", [P, B], F32))
    col_size = ctx.enter_context(nc.sbuf_tensor("col_size", [P, B], F32))
    modcol = sbuf["modcol"]
    mod_ps = psum[0:B, 0:4 * 512].rearrange("b (l n) -> b l n", l=2)
    col_ps = psum[:, 4 * 512:4 * 512 + 5 * B].rearrange("p (j b) -> p j b", j=5)
    cols = [CA, SA, CB, SB, GB]

    with nc.Block() as block:
        @block.sync
        def _(sp):
            for layer in range(2):
                sp.dma_start(cond[:, layer, :], dram["condT"][layer]).then_inc(cond_loaded, 16)
            for layer in range(2):
                sp.dma_start(wmod[:, layer, :], dram["wmod"][layer]).then_inc(wmod_loaded, 16)
                sp.dma_start(bo_rows[:, layer, :], dram["bo"][layer].partition_broadcast(B)).then_inc(wmod_loaded, 16)
            for dst, src in dram["loads"]:
                sp.dma_start(dst, src).then_inc(weights_loaded, 16)
            sp.wait_ge(rows_ready, 1)
            sp.dma_start(dram["table"], rows[:, :, :]).then_inc(table_stored, 16)
            sp.wait_ge(table_stored, 16)
            sp.wait_ge(weights_loaded, 16 * len(dram["loads"]))

        @block.scalar
        def _(act):
            act.wait_ge(cond_loaded, 32)
            nc.scalar.activation(cond_tanh[:, :, :], cond[:, :, :], ACT.Tanh, scale=0.5).then_inc(tanh_ready, 1)

        @block.tensor
        def _(pe):
            pe.wait_ge(silu_step, 2)
            pe.wait_ge(wmod_loaded, 64)
            for layer in range(2):
                for n0, n in ((0, 512), (512, MOD - 512)):
                    nc.tensor.matmul(mod_ps[:, layer, n0:n0 + n], cond_silu[:, layer, :],
                                     wmod[:, layer, n0:n0 + n], start=True, stop=True)
            for j, part in enumerate(cols):
                last = nc.tensor.matmul(col_ps[:, j, :], wmod[:, 1, part * D:(part + 1) * D],
                                        cond_silu[:, 1, :], start=True, stop=True)
            last.then_inc(mod_psum, 1)

        @block.gpsimd
        def _(pool):
            for what, value in dram["fills"]:
                last = nc.gpsimd.memset(what, value)

        @block.vector
        def _(dve):
            dve.wait_ge(tanh_ready, 1)
            nc.vector.scalar_tensor_tensor(out=cond_twice[:, :, :], in0=cond_tanh[:, :, :], scalar=1.0,
                                           in1=cond[:, :, :], op0=ALU.add, op1=ALU.mult).then_inc(silu_step, 1)
            dve.wait_ge(silu_step, 1)
            nc.vector.tensor_scalar(cond_silu[:, :, :], cond_twice[:, :, :], 0.5, None, ALU.mult).then_inc(silu_step, 1)
            dve.wait_ge(mod_psum, 1)
            dve.wait_ge(wmod_loaded, 64)

            def part(layer, which):
                return mod_ps[:, layer, which * D:(which + 1) * D]

            gates = ((0, GA), (0, GB), (1, GA))
            for row, layer, which, plus in ((ROW_CA0, 0, CA, 1.0), (ROW_SA0, 0, SA, 0.0),
                                            (ROW_CB0, 0, CB, 1.0), (ROW_SB0, 0, SB, 0.0)):
                nc.vector.tensor_scalar(rows[:, row, :], part(layer, which), plus, None, ALU.add)
            for j, plus in ((0, 1.0), (1, 0.0), (2, 1.0), (3, 0.0)):
                nc.vector.tensor_scalar(modcol[:, j, :], col_ps[:, j, :], plus, None, ALU.add)
            for n, (layer, which) in enumerate(gates):
                nc.vector.tensor_scalar(sign[:, n, :], part(layer, which), 0.0, 2.0, ALU.is_ge, ALU.mult)
                nc.vector.tensor_scalar(minus[:, n, :], part(layer, which), -1.0, None, ALU.mult)
            nc.vector.tensor_scalar(col_sign[:, :], col_ps[:, 4, :], 0.0, 2.0, ALU.is_ge, ALU.mult)
            nc.vector.tensor_scalar(col_minus[:, :], col_ps[:, 4, :], -1.0, None, ALU.mult).then_inc(rows_step, 1)
            dve.wait_ge(rows_step, 1)
            for n, (layer, which) in enumerate(gates):
                nc.vector.scalar_tensor_tensor(out=size[:, n, :], in0=part(layer, which), scalar=0.25, in1=minus[:, n, :],
                                               op0=ALU.max, op1=ALU.max)
            nc.vector.scalar_tensor_tensor(out=col_size[:, :], in0=col_ps[:, 4, :], scalar=0.25, in1=col_minus[:, :],
                                           op0=ALU.max, op1=ALU.max).then_inc(rows_step, 1)
            dve.wait_ge(rows_step, 2)
            for n, row in enumerate((ROW_GA0, ROW_GB0, ROW_GA1)):
                nc.vector.scalar_tensor_tensor(out=rows[:, row, :], in0=sign[:, n, :], scalar=-1.0,
                                               in1=size[:, n, :], op0=ALU.add, op1=ALU.mult)
            nc.vector.scalar_tensor_tensor(out=modcol[:, 4, :], in0=col_sign[:, :], scalar=-1.0, in1=col_size[:, :],
                                           op0=ALU.add, op1=ALU.mult).then_inc(rows_step, 1)
            dve.wait_ge(rows_step, 3)
            nc.vector.tensor_tensor(rows[:, ROW_GABO0, :], rows[:, ROW_GA0, :], bo_rows[:, 0, :], ALU.mult)
            nc.vector.tensor_tensor(rows[:, ROW_GABO1, :], rows[:, ROW_GA1, :], bo_rows[:, 1, :],
                                    ALU.mult).then_inc(rows_ready, 1)


def attention_0(nc, ctx, dram, sbuf, psum):
    numbers = []

    def sem(name):
        s = ctx.enter_context(nc.semaphore("a0_" + name))
        numbers.append(s.num)
        return s

    def sb(name, shape, dt=F32):
        return ctx.enter_context(nc.sbuf_tensor("a0_" + name, shape, dt))

    X, ident, ident16 = sbuf["X"], sbuf["ident"], sbuf["ident16"]
    kmask, vpad, probs = sbuf["kmask"], sbuf["vpad"], sbuf["probs"]
    wqk, wv, wo, gammacol, betacol, gqk = (sbuf[k] for k in ("wqk0", "wv0", "wo0", "gamma", "beta", "gqk"))
    minus_half, eps, biases = sbuf["minus_half"], sbuf["eps"], sbuf["biases"]
    tanh_bias, gate_k_bias, gate_q_bias = (biases[:, i:i + 1] for i in range(3))

    mod_norm = [sb(f"mod_norm{i}", [P, 2, D]) for i in range(2)]
    mod_gate = [sb(f"mod_gate{i}", [P, 2, D]) for i in range(2)]
    stats1, stats2 = sb("stats1", [P, TT, 6]), sb("stats2", [P, TT, 6])
    moments1, moments2 = sb("moments1", [P, TT, 2]), sb("moments2", [P, TT, 2])
    vareps1, vareps2 = sb("vareps1", [P, TT]), sb("vareps2", [P, TT])
    rstd1, rstd2 = sb("rstd1", [P, TT]), sb("rstd2", [P, TT])
    xhat, scaled, h, xn = (sb(n, [P, TT, D]) for n in ("xhat", "scaled", "h", "xn"))
    hT, xnT = [sb(f"hT{i}", [P, T]) for i in range(2)], sb("xnT", [P, T])
    squares, qkn, qkg = sb("squares", [P, 64, HD]), sb("qkn", [P, 2, TT, D]), sb("qkg", [P, 2, TT, D])
    norm2, norm2c, seed_half, seed = (sb(n, [P, 64]) for n in ("norm2", "norm2c", "seed_half", "seed"))
    nw = [sb(f"newton{i}", [P, 64]) for i in range(7)]
    rnorm = sb("rnorm", [P, 64])
    gate_in, gate_tanh = sb("gate_in", [P, 64]), sb("gate_tanh", [P, 64])
    gate_k, gate_q = sb("gate_k", [P, TT * H]), sb("gate_q", [P, TT, D])
    qstack, kstack = sb("qstack", [P, TT * H, 4, HD], F16), sb("kstack", [P, TT * H, 4, HD], F16)
    qT = [sb(f"qT{i}", [P, G, T], F16) for i in range(2)]
    kT = sb("kT", [P, G, T], F16)
    gT = [sb(f"gT{i}", [P, T]) for i in range(2)]
    oT = sb("oT", [P, T])
    delta = sb("delta", [P, TT, D])

    SC = [psum[:, 1024 * i:1024 * (i + 1)] for i in range(2)]
    PO = psum[:, 2048:2048 + UNIT]
    PT, PQ = psum[:, 2560:3072], psum[:, 3072:3584]
    PV, PP = psum[:, 3584:3840], psum[:, 3840:4096]
    PT16, PQ16 = PT.bitcast(F16), PQ.bitcast(F16)

    x_loaded, mod_norm_loaded, k_spread = map(sem, ("x_loaded", "mod_norm_loaded", "k_spread"))
    mod_gate_loaded = [sem(f"mod_gate_loaded{i}") for i in range(2)]
    stats1_done, moments1_done, vareps1_done, rstd1_done, xhat_done = map(sem, ("stats1", "moments1", "vareps1", "rstd1", "xhat"))
    scaled_done, h_done = sem("scaled"), sem("h")
    stats2_done, moments2_done, vareps2_done, rstd2_done, xn_done = map(sem, ("stats2", "moments2", "vareps2", "rstd2", "xn"))
    turned, hT_done, xnT_done, qk_psum, v_psum = map(sem, ("turned", "hT", "xnT", "qk_psum", "v_psum"))
    squares_done, norm2_done, newton, qkn_done, qkg_done = map(sem, ("squares", "norm2", "newton", "qkn", "qkg"))
    gate_in_done, gate_tanh_done, gates_done, values_done = map(sem, ("gate_in", "gate_tanh", "gates", "values"))
    hi_done, stacks_done, qT_done, kT_done, gT_done = map(sem, ("hi", "stacks", "qT", "kT", "gT"))
    kstack_psum, qstack_psum, gates_psum = map(sem, ("kstack_psum", "qstack_psum", "gates_psum"))
    scores_ready, probs_ready, heads_done = map(sem, ("scores_ready", "probs_ready", "heads_done"))
    oT_done, projected, delta_done, x_biased, x_done = map(sem, ("oT", "projected", "delta", "x_biased", "x_done"))

    vdiag = [bass.AP(tensor=v[:, :, :, :].tensor, offset=v[:, :, :, :].offset,
                     ap=[[TT * H * 32, P], [P, TT * G], [32 + HD, G], [1, HD]]) for v in vpad]

    def tiles(b):
        return X[:, bass.ds(b * TT, TT), :] if not isinstance(b, int) else X[:, b * TT:(b + 1) * TT, :]

    def tile(b, t):
        return X[:, bass.ds(b * TT + t, 1), :] if not isinstance(b, int) else X[:, b * TT + t:b * TT + t + 1, :]

    def rows_of(b, row, n):
        src = dram["table"]
        src = src[bass.ds(b, 1), row:row + n, :] if not isinstance(b, int) else src[b:b + 1, row:row + n, :]
        return src.rearrange("o r d -> (o r d)").partition_broadcast(P)

    def x_rows(b):
        src = dram["x"]
        return src[:, bass.ds(b * TT, TT), :] if not isinstance(b, int) else src[:, b * TT:(b + 1) * TT, :]

    def is_last(b, back=0):
        return isinstance(b, int) and b >= B - back

    with nc.Block() as block:
        @block.sync
        def _(sp):
            def load(n, p):
                wait(sp, h_done, n - 1)
                wait(sp, mod_norm_loaded, n * 16)
                sp.dma_start(mod_norm[p][:, :, :], rows_of(n, ROW_CA0, 2)).then_inc(mod_norm_loaded, 16)
                wait(sp, x_loaded, n * 16)
                sp.dma_start(tiles(n), x_rows(n)).then_inc(x_loaded, 16)

            def load_gate(n, p):
                wait(sp, x_done, n - 1)
                sp.dma_start(mod_gate[p][:, :, :], rows_of(n, ROW_GA0, 2)).then_inc(mod_gate_loaded[p], 16)

            def spread(n, p):
                sp.wait_ge(kT_done, n + 1)
                wait(sp, scores_ready, n * CHUNKS - CHUNKS)
                for r in range(G):
                    sp.dma_start(kmask[p][32 * r:32 * r + 32, r:H:G, :], kT[32 * r:32 * r + 32, :, :]).then_inc(k_spread, 16)

            def step(b, p):
                if not is_last(b, 4):
                    load(b + 4, p)
                if not is_last(b, 1):
                    spread(b + 1, 1 - p)
                    load_gate(b + 1, 1 - p)

            load(0, 0)
            load(1, 1)
            load_gate(0, 0)
            load(2, 0)
            spread(0, 0)
            load(3, 1)
            stepped(sp, 0, B - 1, 1, 13, step)

        @block.tensor
        def _(pe):
            def turn(n):
                pe.wait_ge(h_done, n + 1)
                pe.wait_ge(xn_done, n + 1)
                wait(pe, qT_done, n - 1)
                for i, src in enumerate((h, xn)):
                    for t in range(TT):
                        last = nc.tensor.transpose(PT[:, (i * TT + t) * P:(i * TT + t + 1) * P], src[:, t, :], ident[:, :])
                last.then_inc(turned, 1)

            def project_qk(n):
                pe.wait_ge(xnT_done, n + 1)
                wait(pe, kT_done, n)
                for t in range(TT):
                    last = nc.tensor.matmul(PQ[:, t * 2 * D:(t + 1) * 2 * D], xnT[:, t * P:(t + 1) * P], wqk[:, :], start=True, stop=True)
                last.then_inc(qk_psum, 1)

            def project_v(n, p):
                pe.wait_ge(hT_done, n + 1)
                wait(pe, gT_done, n)
                wait(pe, delta_done, n - 2)
                for t in range(TT):
                    last = nc.tensor.matmul(PV[:, t * D:(t + 1) * D], hT[p][:, t * P:(t + 1) * P], wv[:, :], start=True, stop=True)
                last.then_inc(v_psum, 1)

            def turn_stack(n, dst, src, done):
                pe.wait_ge(stacks_done, n + 1)
                if done is qstack_psum:
                    pe.wait_ge(xnT_done, n + 2 if not is_last(n, 1) else B)
                for t in range(TT):
                    for g in range(G):
                        last = nc.tensor.transpose(dst[:, g * T + t * P:g * T + (t + 1) * P],
                                                   src[:, t * H + G * g:t * H + G * (g + 1), :, :].rearrange("p h s d -> p (h s d)"),
                                                   ident16[:, :])
                last.then_inc(done, 1)

            def turn_gates(n):
                pe.wait_ge(values_done, n + 1)
                pe.wait_ge(gates_done, n + 1)
                for t in range(TT):
                    last = nc.tensor.transpose(PV[:, t * P:(t + 1) * P], gate_q[:, t, :], ident[:, :])
                last.then_inc(gates_psum, 1)

            def scores(b, p, c):
                r, kb = c // TT, c % TT
                if c == 0:
                    pe.wait_ge(k_spread, b * (16 * G) + 16 * G)
                    pe.wait_ge(qT_done, b + 1)
                wait(pe, probs_ready, b * CHUNKS + (c - 1))
                for g in range(G):
                    last = nc.tensor.matmul(SC[c % 2][:, g * T:(g + 1) * T], kmask[p][:, G * g + r, kb * P:(kb + 1) * P],
                                            qT[p][:, g, :], start=True, stop=True)
                last.then_inc(scores_ready, 1)

            def heads(b, p, c):
                r, kb = c // TT, c % TT
                if c == 0:
                    wait(pe, oT_done, b)
                    pe.wait_ge(values_done, b + 1)
                pe.wait_ge(probs_ready, b * CHUNKS + (c + 1))
                for g in range(G):
                    last = nc.tensor.matmul(PO[32 * g:32 * g + 32, :], vpad[p][:, kb, G * g + r, :],
                                            probs[:, c % 4, g, 0:UNIT], start=(c == 0), stop=(c == CHUNKS - 1))
                last.then_inc(heads_done, 1)

            def project_out(n):
                pe.wait_ge(oT_done, n + 1)
                pe.wait_ge(gT_done, n + 3 if not is_last(n, 2) else B)
                wait(pe, delta_done, n)
                for t in range(TT):
                    last = nc.tensor.matmul(PP[:, t * D:(t + 1) * D], oT[:, t * P:(t + 1) * P], wo[:, :], start=True, stop=True)
                last.then_inc(projected, 1)

            def step(b, p):
                first, more, projects = isinstance(b, int) and b == 0, not is_last(b, 1), not is_last(b, 2)
                for c in range(CHUNKS):
                    scores(b, p, c)
                    if c < 2 and not first:
                        heads(b - 1, 1 - p, c + CHUNKS - 2)
                    if c >= 2:
                        heads(b, p, c - 2)
                    if c == 0 and projects:
                        turn(b + 2)
                    if c == 0 and more:
                        turn_stack(b + 1, PQ16, kstack, kstack_psum)
                    if c == 1 and more:
                        turn_stack(b + 1, PT16, qstack, qstack_psum)
                    if c == 1 and projects:
                        project_qk(b + 2)
                    if c == 2 and more:
                        project_v(b + 1, 1 - p)
                    if c == 5 and more:
                        turn_gates(b + 1)
                    if c == 6 and not first:
                        project_out(b - 1)

            turn(0)
            project_qk(0)
            turn(1)
            turn_stack(0, PQ16, kstack, kstack_psum)
            turn_stack(0, PT16, qstack, qstack_psum)
            project_v(0, 0)
            project_qk(1)
            turn_gates(0)
            stepped(pe, 0, B - 1, 1, 13, step)
            for c in (CHUNKS - 2, CHUNKS - 1):
                heads(B - 1, 1, c)
            project_out(B - 1)

        @block.scalar
        def _(act):
            def square(n):
                act.wait_ge(qk_psum, n + 1)
                wait(act, norm2_done, n)
                nc.scalar.activation(squares[:, :, :].rearrange("p a d -> p (a d)"), PQ, ACT.Square).then_inc(squares_done, 1)

            def gate(n):
                act.wait_ge(gate_in_done, n + 1)
                wait(act, gates_done, n)
                nc.scalar.activation(gate_tanh[:, :], gate_in[:, :], ACT.Tanh, scale=0.5 / SPLIT_SCALE).then_inc(gate_tanh_done, 1)
                wait(act, gates_psum, n)
                wait(act, values_done, n)
                act.wait_ge(gate_tanh_done, n + 1)
                nc.scalar.activation(gate_q[:, :, :].rearrange("p t (h d) -> p (t h) d", d=HD),
                                     gate_tanh[:, 0:32].unsqueeze(2).broadcast_to([P, TT * H, HD]),
                                     ACT.Identity, bias=gate_q_bias, scale=0.1875)
                nc.scalar.activation(gate_k[:, :], gate_tanh[:, 32:64], ACT.Identity,
                                     bias=gate_k_bias, scale=0.375).then_inc(gates_done, 1)

            def gT_out(n, p):
                act.wait_ge(gates_psum, n + 1)
                wait(act, oT_done, n - 1)
                nc.scalar.copy(gT[p][:, :], PV).then_inc(gT_done, 1)

            def prob(b, c):
                act.wait_ge(scores_ready, b * CHUNKS + (c + 1))
                wait(act, heads_done, b * CHUNKS + (c - 3))
                nc.scalar.activation(probs[:, c % 4, :, 0:T], SC[c % 2].rearrange("p (g q) -> p g q", g=G), ACT.Tanh,
                                     bias=tanh_bias, scale=SHARPNESS / SPLIT_SCALE ** 2).then_inc(probs_ready, 1)

            def step(b, p):
                more, projects = not is_last(b, 1), not is_last(b, 2)
                for c in range(CHUNKS):
                    prob(b, c)
                    if c == 1 and projects:
                        square(b + 2)
                    if c == 1 and more:
                        gate(b + 1)
                    if c == 5 and more:
                        gT_out(b + 1, 1 - p)

            square(0)
            gate(0)
            gT_out(0, 0)
            square(1)
            stepped(act, 0, B - 1, 1, 13, step)

        @block.gpsimd
        def _(pool):
            def rstd(n, moments, vareps, out, moments_done, vareps_done, out_done, used):
                wait(pool, out_done, n)
                pool.wait_ge(moments_done, n + 1)
                nc.gpsimd.tensor_tensor(vareps[:, :], moments[:, :, 1], eps[:, 0:TT], ALU.add).then_inc(vareps_done, 1)
                pool.wait_ge(vareps_done, n + 1)
                wait(pool, used, n)
                nc.gpsimd.tensor_tensor(out[:, :], vareps[:, :], minus_half[:, 0:TT], ALU.pow).then_inc(out_done, 1)

            def modulate(n, p):
                pool.wait_ge(xhat_done, n + 1)
                pool.wait_ge(mod_norm_loaded, n * 16 + 16)
                wait(pool, h_done, n)
                nc.gpsimd.tensor_tensor(scaled[:, :, :], xhat[:, :, :],
                                        mod_norm[p][:, 0:1, :].broadcast_to([P, TT, D]), ALU.mult).then_inc(scaled_done, 1)
                pool.wait_ge(scaled_done, n + 1)
                wait(pool, turned, n)
                nc.gpsimd.tensor_tensor(h[:, :, :], scaled[:, :, :],
                                        mod_norm[p][:, 1:2, :].broadcast_to([P, TT, D]), ALU.add).then_inc(h_done, 1)

            def norm_1(n):
                rstd(n, moments1, vareps1, rstd1, moments1_done, vareps1_done, rstd1_done, xhat_done)

            def norm_2(n):
                rstd(n, moments2, vareps2, rstd2, moments2_done, vareps2_done, rstd2_done, xn_done)

            def gate_products(n):
                pool.wait_ge(qkn_done, n + 1)
                wait(pool, gate_in_done, n)
                nc.gpsimd.tensor_tensor(qkg[:, :, :, :], qkn[:, :, :, :],
                                        gqk[:, :, :].unsqueeze(2).broadcast_to([P, 2, TT, D]), ALU.mult).then_inc(qkg_done, 1)

            def bias_x(n, p):
                pool.wait_ge(mod_gate_loaded[p], n * 8 + (16 - 8 * p))
                pool.wait_ge(xhat_done, n + 1)
                nc.gpsimd.tensor_tensor(tiles(n), tiles(n), mod_gate[p][:, 1:2, :].broadcast_to([P, TT, D]),
                                        ALU.add).then_inc(x_biased, 1)

            def step(b, p):
                norms = not is_last(b, 3)
                if norms:
                    norm_1(b + 3)
                    modulate(b + 3, 1 - p)
                bias_x(b, p)
                if norms:
                    norm_2(b + 3)
                if not is_last(b, 2):
                    gate_products(b + 2)

            norm_1(0)
            modulate(0, 0)
            norm_2(0)
            norm_1(1)
            gate_products(0)
            modulate(1, 1)
            norm_2(1)
            norm_1(2)
            modulate(2, 0)
            norm_2(2)
            gate_products(1)
            stepped(pool, 0, B - 1, 1, 13, step)

        @block.vector
        def _(dve):
            def moments(n, src, stats, out, stats_done, out_done, read_done):
                wait(dve, out_done, n)
                for t in range(TT):
                    last = nc.vector.bn_stats(stats[:, t, :], src(t))
                last.then_inc(stats_done, 1)
                wait(dve, read_done, n)
                dve.wait_ge(stats_done, n + 1)
                nc.vector.memset(unread[:, :], 0.0)
                for t in range(TT):
                    last = nc.vector.bn_aggr(out[:, t, :], stats[:, t, :])
                last.then_inc(out_done, 1)

            def standardise(n, src, dst, mom, rstd, rstd_done, done):
                dve.wait_ge(rstd_done, n + 1)
                for t in range(TT):
                    last = nc.vector.tensor_scalar(dst[:, t, :], src(t), mom[:, t, 0:1], rstd[:, t:t + 1], ALU.subtract, ALU.mult)
                last.then_inc(done, 1)

            def norm_1a(n):
                dve.wait_ge(x_loaded, n * 16 + 16)
                moments(n, lambda t: tile(n, t)[:, 0, :], stats1, moments1, stats1_done, moments1_done, xhat_done)

            def norm_1b(n):
                wait(dve, scaled_done, n)
                standardise(n, lambda t: tile(n, t)[:, 0, :], xhat, moments1, rstd1, rstd1_done, xhat_done)

            def norm_2a(n):
                dve.wait_ge(h_done, n + 1)
                moments(n, lambda t: h[:, t, :], stats2, moments2, stats2_done, moments2_done, xn_done)

            def norm_2b(n):
                wait(dve, turned, n)
                standardise(n, lambda t: h[:, t, :], xn, moments2, rstd2, rstd2_done, xn_done)

            def turned_out(n, p):
                dve.wait_ge(turned, n + 1)
                wait(dve, qk_psum, n)
                wait(dve, v_psum, n - 1)
                nc.vector.tensor_copy(hT[p][:, :], PT[:, 0:T]).then_inc(hT_done, 1)
                nc.vector.tensor_scalar(xnT[:, :], PT[:, T:2 * T], gammacol[:, :], betacol[:, :], ALU.mult, ALU.add).then_inc(xnT_done, 1)

            def unit_vectors(n):
                def then(ins, k):
                    ins.then_inc(newton, 1)
                    dve.wait_ge(newton, n * RSQRT_STEPS + k)

                dve.wait_ge(squares_done, n + 1)
                nc.vector.tensor_reduce(norm2[:, :], squares[:, :, :], AX.X, ALU.add).then_inc(norm2_done, 1)
                dve.wait_ge(norm2_done, n + 1)
                then(nc.vector.tensor_scalar(norm2c[:, :], norm2[:, :], NORM_FLOOR, SPLIT_SCALE ** -2, ALU.max, ALU.mult), 1)
                then(nc.vector.tensor_scalar(seed_half[:, :].bitcast(I32), norm2c[:, :].bitcast(I32), 1, None,
                                             ALU.logical_shift_right), 2)
                then(nc.vector.tensor_scalar(seed[:, :].bitcast(I32), seed_half[:, :].bitcast(I32), -1.0, RSQRT_MAGIC,
                                             ALU.mult, ALU.add), 3)
                then(nc.vector.tensor_tensor(nw[0][:, :], seed[:, :], seed[:, :], ALU.mult), 4)
                then(nc.vector.tensor_tensor(nw[1][:, :], nw[0][:, :], norm2c[:, :], ALU.mult), 5)
                then(nc.vector.tensor_scalar(nw[2][:, :], nw[1][:, :], 0.375, -1.25, ALU.mult, ALU.add), 6)
                then(nc.vector.tensor_tensor(nw[3][:, :], nw[2][:, :], nw[1][:, :], ALU.mult), 7)
                then(nc.vector.scalar_tensor_tensor(out=nw[4][:, :], in0=nw[3][:, :], scalar=1.875, in1=seed[:, :],
                                                    op0=ALU.add, op1=ALU.mult), 8)
                then(nc.vector.tensor_tensor(nw[5][:, :], nw[4][:, :], nw[4][:, :], ALU.mult), 9)
                then(nc.vector.scalar_tensor_tensor(out=nw[6][:, :], in0=nw[5][:, :], scalar=-0.5, in1=norm2c[:, :],
                                                    op0=ALU.mult, op1=ALU.mult), 10)
                nc.vector.scalar_tensor_tensor(out=rnorm[:, :], in0=nw[6][:, :], scalar=1.5, in1=nw[4][:, :],
                                               op0=ALU.add, op1=ALU.mult).then_inc(newton, 1)

            def scale(n):
                dve.wait_ge(newton, n * RSQRT_STEPS + RSQRT_STEPS)
                wait(dve, qkg_done, n)
                nc.vector.tensor_tensor(qkn[:, :, :, :].rearrange("p k t (h d) -> p t k h d", d=HD),
                                        PQ.rearrange("p (t k h d) -> p t k h d", t=TT, k=2, d=HD),
                                        rnorm[:, :].rearrange("p (t k h) -> p t k h", t=TT, k=2).unsqueeze(4).broadcast_to([P, TT, 2, H, HD]),
                                        ALU.mult).then_inc(qkn_done, 1)

            def twice(i):
                return qkn[:, i, :, :].rearrange("p t (h d) -> p (t h) d", d=HD).unsqueeze(2).broadcast_to([P, TT * H, 2, HD])

            def split_high(n):
                dve.wait_ge(qkn_done, n + 1)
                wait(dve, qstack_psum, n)

                nc.vector.tensor_copy(qstack[:, :, 0:4:2, :], twice(0))
                nc.vector.tensor_copy(kstack[:, :, 0:2, :], twice(1)).then_inc(hi_done, 1)

            def split_low(n):
                dve.wait_ge(hi_done, n + 1)
                nc.vector.tensor_tensor(qstack[:, :, 1:4:2, :], twice(0), qstack[:, :, 0:4:2, :], ALU.subtract)
                nc.vector.tensor_tensor(kstack[:, :, 2:4, :], twice(1), kstack[:, :, 0:2, :], ALU.subtract).then_inc(stacks_done, 1)

            def gate_sums(n):
                dve.wait_ge(qkg_done, n + 1)
                wait(dve, gate_tanh_done, n)
                nc.vector.tensor_reduce(gate_in[:, :], qkg[:, :, :, :].rearrange("p k t (h d) -> p (k t h) d", d=HD),
                                        AX.X, ALU.add).then_inc(gate_in_done, 1)

            def values(n, p):
                dve.wait_ge(v_psum, n + 1)
                dve.wait_ge(gates_done, n + 1)
                wait(dve, heads_done, n * CHUNKS - CHUNKS)
                nc.vector.tensor_tensor(vdiag[p], PV.rearrange("p (a r d) -> p a r d", r=G, d=HD),
                                        gate_k[:, :].rearrange("p (a r) -> p a r", r=G).unsqueeze(3).broadcast_to([P, TT * G, G, HD]),
                                        ALU.mult).then_inc(values_done, 1)

            def keys_out(n):
                dve.wait_ge(kstack_psum, n + 1)
                wait(dve, k_spread, n * (16 * G))
                nc.vector.tensor_copy(kT[:, :, :].rearrange("p g k -> p (g k)"), PQ16).then_inc(kT_done, 1)

            def queries_out(n, p):
                dve.wait_ge(qstack_psum, n + 1)
                wait(dve, scores_ready, n * CHUNKS - CHUNKS)
                nc.vector.tensor_copy(qT[p][:, :, :].rearrange("p g k -> p (g k)"), PT16).then_inc(qT_done, 1)

            def heads_out(n, p):
                dve.wait_ge(heads_done, n * CHUNKS + CHUNKS)
                dve.wait_ge(gT_done, n + 1)
                wait(dve, projected, n)
                nc.vector.tensor_copy(vsum[:, :], PO[:, T:UNIT]).then_inc(vsum_done, 1)
                dve.wait_ge(vsum_done, n + 1)
                nc.vector.scalar_tensor_tensor(out=oT[:, :], in0=PO[:, 0:T], scalar=vsum[:, :], in1=gT[p][:, :],
                                               op0=ALU.add, op1=ALU.mult).then_inc(oT_done, 1)

            def residual(n, p):
                dve.wait_ge(projected, n + 1)
                wait(dve, x_done, n)
                dve.wait_ge(mod_gate_loaded[p], n * 8 + (16 - 8 * p))
                nc.vector.tensor_tensor(delta[:, :, :], PP.rearrange("p (t d) -> p t d", t=TT),
                                        mod_gate[p][:, 0:1, :].broadcast_to([P, TT, D]), ALU.mult).then_inc(delta_done, 1)
                dve.wait_ge(delta_done, n + 1)
                dve.wait_ge(x_biased, n + 1)
                nc.vector.tensor_tensor(tiles(n), tiles(n), delta[:, :, :], ALU.add).then_inc(x_done, 1)

            def step(b, p):
                first, more, projects = isinstance(b, int) and b == 0, not is_last(b, 1), not is_last(b, 2)
                norms = not is_last(b, 3)
                if projects:
                    turned_out(b + 2, p)
                if more:
                    keys_out(b + 1)
                if norms:
                    norm_1a(b + 3)
                if more:
                    queries_out(b + 1, 1 - p)
                if not first:
                    heads_out(b - 1, 1 - p)
                if norms:
                    norm_1b(b + 3)
                if projects:
                    unit_vectors(b + 2)
                if more:
                    values(b + 1, 1 - p)
                if norms:
                    norm_2a(b + 3)
                if projects:
                    scale(b + 2)
                    split_high(b + 2)
                if norms:
                    norm_2b(b + 3)
                if projects:
                    split_low(b + 2)
                    gate_sums(b + 2)
                if not first:
                    residual(b - 1, 1 - p)

            unread = sb("unread", [P, 1])
            vsum, vsum_done = sb("vsum", [P, 1]), sem("vsum")
            norm_1a(0)
            norm_1b(0)
            norm_2a(0)
            norm_2b(0)
            turned_out(0, 0)
            norm_1a(1)
            norm_1b(1)
            unit_vectors(0)
            scale(0)
            norm_2a(1)
            split_high(0)
            split_low(0)
            norm_2b(1)
            gate_sums(0)
            turned_out(1, 1)
            keys_out(0)
            norm_1a(2)
            queries_out(0, 0)
            values(0, 0)
            norm_1b(2)
            unit_vectors(1)
            scale(1)
            norm_2a(2)
            split_high(1)
            split_low(1)
            norm_2b(2)
            gate_sums(1)
            stepped(dve, 0, B - 1, 1, 13, step)
            heads_out(B - 1, 1)
            residual(B - 1, 1)

    assert sorted(numbers) == list(range(min(numbers), max(numbers) + 1))
    with nc.Block() as block:
        @block.gpsimd
        def _(pool):
            pool.sem_clear(range(min(numbers), max(numbers) + 1))


GT = 32
NE, NS_, NF = 32, 4, 32
SLOTS = NE * NS_
CB_ = 8
NCHUNK = B // CB_
CG = CB_ * T // GT
TG = P // GT
EB = 512 // CG
ROUNDS = NE // EB


def experts_0(nc, ctx, dram, sbuf, psum):
    def sem(name):
        return dram["semaphores"].enter_context(nc.semaphore("e_" + name))

    def sb(name, shape, dt=F32):
        return ctx.enter_context(nc.sbuf_tensor("e_" + name, shape, dt))

    X, ident, minus_half, eps = (sbuf[k] for k in ("X", "ident", "minus_half", "eps"))
    ctrl, f1, f2, bias = sb("ctrl", [P, SLOTS]), sb("f1", [P, SLOTS, NF]), sb("f2", [P, NE, D]), sb("bias", [P, NE])
    tie, own = sb("tie", [P, GT]), sb("own", [P, TG])
    mod_norm = [sb(f"mod_norm{i}", [P, 2, D]) for i in range(2)]
    gates = sb("gates", [P, CB_, D])
    stats, moments = sb("stats", [P, TT, 6]), sb("moments", [P, TT, 2])
    vareps, rstd = sb("vareps", [P, TT]), sb("rstd", [P, TT])
    xhat, scaled = sb("xhat", [P, TT, D]), sb("scaled", [P, TT, D])
    h = [sb(f"h{i}", [P, TT, D]) for i in range(3)]
    hT = sb("hT", [P, T])
    logits, best = sb("logits", [P, T]), sb("best", [P, T // GT])
    takenT = sb("takenT", [P, CB_, T])
    taken = sb("taken", [P, TT, TG, SLOTS])
    sent = sb("sent", [P, SLOTS, CG])
    inner = sb("inner", [P, EB, CG])
    relued = [sb(f"relued{i}", [P, EB, NS_, CG]) for i in range(2)]
    given = sb("given", [P, CG, SLOTS])
    givenT = [sb(f"givenT{i}", [P, TG, D]) for i in range(2)]
    delta = sb("delta", [P, TT, D])
    unread = sb("unread", [P, 1])

    bank = [psum[:, 512 * i:512 * (i + 1)] for i in range(8)]

    w_loaded, mod_loaded, gates_loaded = sem("w_loaded"), sem("mod_loaded"), sem("gates_loaded")
    stats_done, moments_done, vareps_done, rstd_done, xhat_done, scaled_done, h_done = map(
        sem, ("stats", "moments", "vareps", "rstd", "xhat", "scaled", "h"))
    turned, hT_done, logits_psum, logits_done, best_done, takenT_done = map(
        sem, ("turned", "hT", "logits_psum", "logits", "best", "takenT"))
    taken_psum, taken_done, sent_psum, sent_done = map(sem, ("taken_psum", "taken", "sent_psum", "sent"))
    inner_psum, inner_done, relued_dve, relued_act = map(sem, ("inner_psum", "inner", "relued_dve", "relued_act"))
    given_psum, given_dve, given_act = map(sem, ("given_psum", "given_dve", "given_act"))
    turned_back, givenT_dve, givenT_act, out_psum, delta_done, x_done = map(
        sem, ("turned_back", "givenT_dve", "givenT_act", "out_psum", "delta", "x_done"))

    loads = [(ctrl[:, :], dram["ctrl"]), (f1[:, :, :].rearrange("p s f -> p (s f)"), dram["f1"]),
             (f2[:, :, :], dram["f2"]), (bias[:, :], dram["ebias"]),
             (tie[:, :], dram["tie"].partition_broadcast(P)), (own[:, :], dram["own"])]
    GB_, TB_ = NE // 2, CB_ * TT

    def tiles(c, j):
        return X[:, bass.ds(c * (CB_ * TT) + j * TT, TT), :]

    def tile(c, j, t):
        return X[:, bass.ds(c * (CB_ * TT) + (j * TT + t), 1), :][:, 0, :]

    def rows_of(c, j, row, n):
        return dram["table"][bass.ds(c * CB_ + j, 1), row:row + n, :].rearrange("o r d -> (o r d)").partition_broadcast(P)

    with nc.Block() as block:
        @block.sync
        def _(sp):
            for dst, src in loads:
                sp.dma_start(dst, src).then_inc(w_loaded, 16)
            def chunk(c):
                wait(sp, delta_done, c * CB_)
                for j in range(CB_):
                    sp.dma_start(gates[:, j, :], rows_of(c, j, ROW_GB0, 1)).then_inc(gates_loaded, 16)
                for j in range(CB_):
                    wait(sp, mod_loaded, c * (16 * CB_) + 16 * j)
                    wait(sp, h_done, c * CB_ + max(j - 1, 0))
                    sp.dma_start(mod_norm[j % 2][:, :, :], rows_of(c, j, ROW_CB0, 2)).then_inc(mod_loaded, 16)

            chunk(0)
            with sp.Fori(1, NCHUNK) as c:
                chunk(c)

        @block.tensor
        def _(pe):
            def turn(c, j):
                wait(pe, h_done, c * CB_ + (j + 1))
                wait(pe, hT_done, c * CB_ + j)
                for t in range(TT):
                    last = nc.tensor.transpose(bank[0][:, t * P:(t + 1) * P], h[j % 3][:, t, :], ident[:, :])
                last.then_inc(turned, 1)

            def score(c, j):
                wait(pe, hT_done, c * CB_ + (j + 1))
                wait(pe, logits_done, c * CB_ + j)
                nc.tensor.matmul(bank[1][:, 0:T], ctrl[:, :], hT[:, :], start=True, stop=True).then_inc(logits_psum, 1)

            def turn_taken(c, j):
                wait(pe, takenT_done, c * CB_ + (j + 1))
                wait(pe, taken_done, c * CB_ + j)
                for t in range(TT):
                    last = nc.tensor.transpose(bank[2][:, t * P:(t + 1) * P], takenT[:, j, t * P:(t + 1) * P], ident[:, :])
                last.then_inc(taken_psum, 1)

            def send(c, j):
                wait(pe, taken_done, c * CB_ + (j + 1))
                wait(pe, sent_done, c * CB_ + j)
                for t in range(TT):
                    last = nc.tensor.matmul(bank[3 + t], h[j % 3][:, t, :], taken[:, t, :, :].rearrange("p g s -> p (g s)"),
                                            start=True, stop=True)
                last.then_inc(sent_psum, 1)

            def first_matrices(c, r):
                wait(pe, sent_done, c * CB_ + CB_)
                for e in range(EB):
                    for s in range(NS_):
                        slot = (r * EB + e) * NS_ + s
                        last = nc.tensor.matmul(bank[r][NF * s:NF * (s + 1), e * CG:(e + 1) * CG], f1[:, slot, :],
                                                sent[:, slot, :], start=True, stop=True)
                last.then_inc(inner_psum, 1)

            def second_matrices(c, r):
                wait(pe, relued_dve, c * ROUNDS + (r + 1))
                wait(pe, relued_act, c * ROUNDS + (r + 1))
                for pair in range(EB // 2):
                    n = r * (EB // 2) + pair
                    if n >= 4:
                        wait(pe, (given_dve, given_act)[n % 2], c * (GB_ // 2) + (n // 2 - 1))
                    for i in range(2):
                        e = 2 * pair + i
                        last = nc.tensor.matmul(bank[4 + n % 4][:, i * NS_ * CG:(i + 1) * NS_ * CG], f2[:, r * EB + e, :],
                                                relued[r % 2][:, e, :, :].rearrange("p s g -> p (s g)"), start=True, stop=True)
                    last.then_inc(given_psum, 1)

            def turn_back(c, q):
                wait(pe, given_dve, c * (GB_ // 2) + GB_ // 2)
                wait(pe, given_act, c * (GB_ // 2) + GB_ // 2)
                if q >= 2:
                    wait(pe, (givenT_dve, givenT_act)[q % 2], c * (TB_ // 2) + q // 2)
                for g in range(TG):
                    last = nc.tensor.transpose(bank[q % 2][:, g * P:(g + 1) * P], given[:, q * TG + g, :], ident[:, :])
                last.then_inc(turned_back, 1)

            def hand_back(c, q):
                j, t = q // TT, q % TT
                wait(pe, (givenT_dve, givenT_act)[q % 2], c * (TB_ // 2) + (q // 2 + 1))
                if t == 0 and j >= 2:
                    wait(pe, delta_done, c * CB_ + (j - 1))
                for g in range(TG):
                    last = nc.tensor.matmul(bank[4 + j % 2][GT * g:GT * (g + 1), t * D:(t + 1) * D],
                                            takenT[:, j, t * P + GT * g:t * P + GT * (g + 1)], givenT[q % 2][:, g, :],
                                            start=True, stop=True)
                last.then_inc(out_psum, 1)

            wait(pe, w_loaded, 16 * len(loads))
            def chunk(c):
                wait(pe, delta_done, c * CB_)
                for k in range(CB_ + 2):
                    if k < CB_:
                        turn(c, k)
                    if 0 <= k - 1 < CB_:
                        turn_taken(c, k - 1)
                    if k < CB_:
                        score(c, k)
                    if k >= 2:
                        send(c, k - 2)
                first_matrices(c, 0)
                first_matrices(c, 1)
                for r in range(ROUNDS):
                    if r + 2 < ROUNDS:
                        first_matrices(c, r + 2)
                    second_matrices(c, r)
                turn_back(c, 0)
                for q in range(TB_):
                    if q + 1 < TB_:
                        turn_back(c, q + 1)
                    hand_back(c, q)

            chunk(0)
            with pe.Fori(1, NCHUNK) as c:
                chunk(c)

        def results_out(eng, copy, done, c, n):
            wait(eng, given_psum, c * GB_ + (n + 1))
            copy(given[:, :, 2 * NS_ * n:2 * NS_ * (n + 1)], bank[4 + n % 4].rearrange("p (s g) -> p g s", g=CG)).then_inc(done, 1)

        def turned_out(eng, copy, done, c, q):
            wait(eng, turned_back, c * TB_ + (q + 1))
            if q >= 2:
                wait(eng, out_psum, c * TB_ + (q - 1))
            copy(givenT[q % 2][:, :, :].rearrange("p g d -> p (g d)"), bank[q % 2]).then_inc(done, 1)

        @block.scalar
        def _(act):
            def chunk(c):
                def hT_out(j):
                    wait(act, turned, c * CB_ + (j + 1))
                    wait(act, logits_psum, c * CB_ + j)
                    nc.scalar.copy(hT[:, :], bank[0][:, 0:T]).then_inc(hT_done, 1)

                def sent_out(j):
                    wait(act, sent_psum, c * CB_ + (j + 1))
                    for t in range(TT):
                        g0 = (j * TT + t) * TG
                        last = nc.scalar.copy(sent[:, :, g0:g0 + TG], bank[3 + t].rearrange("p (g s) -> p s g", g=TG))
                    last.then_inc(sent_done, 1)

                def relu(r):
                    wait(act, inner_done, c * ROUNDS + (r + 1))
                    if r >= 2:
                        wait(act, given_psum, c * GB_ + (r - 1) * (EB // 2))
                    for s in (2, 3):
                        last = nc.scalar.activation(relued[r % 2][:, :, s, :], inner[:, :, :], ACT.Relu, scale=own[:, s:s + 1])
                    last.then_inc(relued_act, 1)

                for k in range(CB_ + 2):
                    if k < CB_:
                        hT_out(k)
                    if k >= 2:
                        sent_out(k - 2)
                relu(0)
                for r in range(ROUNDS):
                    if r + 1 < ROUNDS:
                        relu(r + 1)
                    for n in range(r * (EB // 2), (r + 1) * (EB // 2)):
                        if n % 2:
                            results_out(act, nc.scalar.copy, given_act, c, n)
                for q in range(1, TB_, 2):
                    turned_out(act, nc.scalar.copy, givenT_act, c, q)

            chunk(0)
            with act.Fori(1, NCHUNK) as c:
                chunk(c)

        @block.gpsimd
        def _(pool):
            def chunk(c):
                for j in range(CB_):
                    n = c * CB_ + j
                    wait(pool, moments_done, n + 1)
                    nc.gpsimd.tensor_tensor(vareps[:, :], moments[:, :, 1], eps[:, 0:TT], ALU.add).then_inc(vareps_done, 1)
                    wait(pool, vareps_done, n + 1)
                    wait(pool, xhat_done, n)
                    nc.gpsimd.tensor_tensor(rstd[:, :], vareps[:, :], minus_half[:, 0:TT], ALU.pow).then_inc(rstd_done, 1)
                    wait(pool, xhat_done, n + 1)
                    wait(pool, mod_loaded, n * 16 + 16)
                    nc.gpsimd.tensor_tensor(scaled[:, :, :], xhat[:, :, :],
                                            mod_norm[j % 2][:, 0:1, :].broadcast_to([P, TT, D]), ALU.mult).then_inc(scaled_done, 1)
                    wait(pool, scaled_done, n + 1)
                    wait(pool, sent_psum, c * CB_ + (j - 2))
                    nc.gpsimd.tensor_tensor(h[j % 3][:, :, :], scaled[:, :, :],
                                            mod_norm[j % 2][:, 1:2, :].broadcast_to([P, TT, D]), ALU.add).then_inc(h_done, 1)

            chunk(0)
            with pool.Fori(1, NCHUNK) as c:
                chunk(c)

        @block.vector
        def _(dve):
            wait(dve, w_loaded, 16 * len(loads))
            def chunk(c):
                def count(j):
                    return c * CB_ + j

                def moments_of(j):
                    wait(dve, moments_done, count(j))
                    for t in range(TT):
                        last = nc.vector.bn_stats(stats[:, t, :], tile(c, j, t))
                    last.then_inc(stats_done, 1)
                    wait(dve, rstd_done, count(j))
                    wait(dve, xhat_done, count(j))
                    wait(dve, stats_done, count(j + 1))
                    nc.vector.memset(unread[:, :], 0.0)
                    for t in range(TT):
                        last = nc.vector.bn_aggr(moments[:, t, :], stats[:, t, :])
                    last.then_inc(moments_done, 1)

                def standardise(j):
                    wait(dve, scaled_done, count(j))
                    wait(dve, rstd_done, count(j + 1))
                    for t in range(TT):
                        last = nc.vector.tensor_scalar(xhat[:, t, :], tile(c, j, t), moments[:, t, 0:1], rstd[:, t:t + 1],
                                                       ALU.subtract, ALU.mult)
                    last.then_inc(xhat_done, 1)

                def choose(j):
                    wait(dve, takenT_done, count(j))
                    wait(dve, logits_psum, count(j + 1))
                    nc.vector.tensor_tensor(logits[:, :].rearrange("p (g t) -> p g t", t=GT),
                                            bank[1][:, 0:T].rearrange("p (g t) -> p g t", t=GT),
                                            tie[:, :].unsqueeze(1).broadcast_to([P, T // GT, GT]), ALU.add).then_inc(logits_done, 1)
                    wait(dve, logits_done, count(j + 1))
                    nc.vector.tensor_reduce(best[:, :], logits[:, :].rearrange("p (g t) -> p g t", t=GT), AX.X,
                                            ALU.max).then_inc(best_done, 1)
                    wait(dve, best_done, count(j + 1))
                    nc.vector.tensor_tensor(takenT[:, j, :].rearrange("p (g t) -> p g t", t=GT),
                                            logits[:, :].rearrange("p (g t) -> p g t", t=GT),
                                            best[:, :].unsqueeze(2).broadcast_to([P, T // GT, GT]), ALU.is_equal).then_inc(takenT_done, 1)

                def own_groups(j):
                    wait(dve, taken_psum, count(j + 1))
                    wait(dve, sent_psum, count(j))
                    for t in range(TT):
                        last = nc.vector.tensor_tensor(taken[:, t, :, :], bank[2][:, t * P:(t + 1) * P].unsqueeze(1).broadcast_to([P, TG, SLOTS]),
                                                       own[:, :].unsqueeze(2).broadcast_to([P, TG, SLOTS]), ALU.mult)
                    last.then_inc(taken_done, 1)

                def relu(r):
                    wait(dve, inner_psum, c * ROUNDS + (r + 1))
                    wait(dve, relued_dve, c * ROUNDS + r)
                    wait(dve, relued_act, c * ROUNDS + r)
                    nc.vector.tensor_tensor(inner[:, :, :], bank[r].rearrange("p (e g) -> p e g", g=CG),
                                            bias[:, r * EB:(r + 1) * EB].unsqueeze(2).broadcast_to([P, EB, CG]), ALU.add).then_inc(inner_done, 1)
                    wait(dve, inner_done, c * ROUNDS + (r + 1))
                    if r >= 2:
                        wait(dve, given_psum, c * GB_ + (r - 1) * (EB // 2))
                    for s in (0, 1):
                        last = nc.vector.tensor_scalar(relued[r % 2][:, :, s, :], inner[:, :, :], 0.0, own[:, s:s + 1], ALU.max, ALU.mult)
                    last.then_inc(relued_dve, 1)

                def residual(j):
                    wait(dve, x_done, count(j))
                    wait(dve, out_psum, c * TB_ + (j + 1) * TT)
                    nc.vector.tensor_tensor(delta[:, :, :], bank[4 + j % 2][:, 0:T].rearrange("p (t d) -> p t d", t=TT),
                                            gates[:, j:j + 1, :].broadcast_to([P, TT, D]), ALU.mult).then_inc(delta_done, 1)
                    wait(dve, delta_done, count(j + 1))
                    nc.vector.tensor_tensor(tiles(c, j), tiles(c, j), delta[:, :, :], ALU.add).then_inc(x_done, 1)

                moments_of(0)
                standardise(0)
                for k in range(CB_ + 1):
                    if k + 1 < CB_:
                        moments_of(k + 1)
                    if k < CB_:
                        choose(k)
                    if k + 1 < CB_:
                        standardise(k + 1)
                    if k >= 1:
                        own_groups(k - 1)
                wait(dve, gates_loaded, c * (16 * CB_) + 16 * CB_)
                relu(0)
                for r in range(ROUNDS):
                    if r + 1 < ROUNDS:
                        relu(r + 1)
                    for n in range(r * (EB // 2), (r + 1) * (EB // 2)):
                        if n % 2 == 0:
                            results_out(dve, nc.vector.tensor_copy, given_dve, c, n)
                for q in range(0, TB_, 2):
                    turned_out(dve, nc.vector.tensor_copy, givenT_dve, c, q)
                    if q >= 2:
                        residual(q // 2 - 1)
                residual(CB_ - 1)

            chunk(0)
            with dve.Fori(1, NCHUNK) as c:
                chunk(c)


SMALL_SCORE = 40.0


def attention_1(nc, ctx, dram, sbuf, psum, with_max):
    def sem(name):
        key = "sem_" + name
        if key not in sbuf["a1"]:
            sbuf["a1"][key] = dram["semaphores"].enter_context(nc.semaphore("a1_" + name))
        return sbuf["a1"][key]

    def sb(name, shape, dt=F32):
        if name not in sbuf["a1"]:
            sbuf["a1"][name] = ctx.enter_context(nc.sbuf_tensor("a1_" + name, shape, dt))
        return sbuf["a1"][name]

    X, ident, minus_half, eps, modcol = (sbuf[k] for k in ("X", "ident", "minus_half", "eps", "modcol"))
    kmask, vpad, wqk, wv, wo, bqk, bv, rope = (sbuf[k] for k in ("kmask1", "vpad1", "wqk1", "wv1", "wo1", "bqk1", "bv1", "rope"))
    mod_gate = [sb(f"mod_gate{i}", [P, 2, D]) for i in range(2)]
    stats, moments, vareps, rstd = sb("stats", [P, TT, 6]), sb("moments", [P, TT, 2]), sb("vareps", [P, TT]), sb("rstd", [P, TT])
    xhat, hT = sb("xhat", [P, TT, D]), sb("hT", [P, T])
    qk = sb("qk", [P, TT, 2 * H, HD])
    by_cos, by_sin = sb("by_cos", [P, TT, 2 * H, HD]), sb("by_sin", [P, TT, 2 * H, HD])
    turned_qk = sb("turned_qk", [P, 2, TT * H, HD])
    qstack, kstack = sb("qstack", [P, TT * H, 4, HD], F32R), sb("kstack", [P, TT * H, 4, HD], F32R)
    qT = [sb(f"qT{i}", [P, G, T], F32R) for i in range(2)]
    kT = sb("kT", [P, G, T], F32R)
    probs = sb("probs", [P, 4, G, T])
    sums, recip, heads_out_tok, oT = sb("sums", [P, 2 * T]), sb("recip", [P, TT * H]), sb("heads_tok", [P, TT * H, HD]), sb("oT", [P, T])
    delta, unread = sb("delta", [P, TT, D]), sb("unread", [P, 1])

    SC = [psum[:, 1024 * i:1024 * (i + 1)] for i in range(2)]
    PO = psum[:, 2048:2560]
    PT, PQ = psum[:, 2560:3072], psum[:, 3072:3584]
    PV = PT[:, T:2 * T]
    PP = psum[:, 3584:4096]

    mod_gate_loaded = [sem(f"mod_gate_loaded{i}") for i in range(2)]
    stats_done, moments_done, vareps_done, rstd_done, xhat_done = map(sem, ("stats", "moments", "vareps", "rstd", "xhat"))
    turned, hT_done, qk_psum, qk_done, v_psum, values_done = map(sem, ("turned", "hT", "qk_psum", "qk", "v_psum", "values"))
    by_cos_done, rope_products, rope_done, hi_done, stacks_done = map(sem, ("by_cos", "rope_products", "rope", "hi", "stacks"))
    stacks_psum, even_out, odd_out, k_spread = map(sem, ("stacks_psum", "even_out", "odd_out", "k_spread"))
    scores_ready, probs_ready, heads_done = map(sem, ("scores_ready", "probs_ready", "heads_done"))
    sums_done, sums_turned, recip_done, heads_tok_done = map(sem, ("sums", "sums_turned", "recip", "heads_tok"))
    heads_turned, oT_done, projected, delta_done, x_biased, x_done = map(
        sem, ("heads_turned", "oT", "projected", "delta", "x_biased", "x_done"))

    vdiag = [[bass.AP(tensor=v[:, :, :, :].tensor, offset=v[:, :, :, :].offset + 64 * s,
                      ap=[[TT * H * 32, P], [G * 32, TT * G], [32 + 16, 2], [1, HD]]) for s in range(2)] for v in vpad]

    def tiles(b):
        return X[:, bass.ds(b * TT, TT), :] if not isinstance(b, int) else X[:, b * TT:(b + 1) * TT, :]

    def tile(b, t):
        return X[:, bass.ds(b * TT + t, 1), :] if not isinstance(b, int) else X[:, b * TT + t:b * TT + t + 1, :]

    def gate_rows(b):
        src = dram["table"]
        src = (src[bass.ds(b, 1), ROW_GA1:ROW_GA1 + 2, :] if not isinstance(b, int)
               else src[b:b + 1, ROW_GA1:ROW_GA1 + 2, :])
        return src.rearrange("o r d -> (o r d)").partition_broadcast(P)

    def mod(j, b):
        return modcol[:, j, bass.ds(b, 1)] if not isinstance(b, int) else modcol[:, j, b:b + 1]

    def is_last(b, back=0):
        return isinstance(b, int) and b >= B - back

    if with_max:
        sel = sbuf["sel"]
        rowmax = sb("rowmax", [P, TT, H])
        maxstack = sb("maxstack", [P, TT, P], F32R)
        maxT = sb("maxT", [P, T], F32R)
        max_psum, rowmax_done, max_hi, max_lo, max_turned, maxT_done = map(
            sem, ("max_psum", "rowmax", "max_hi", "max_lo", "max_turned", "maxT"))

    def table(i, lo, hi):
        return rope[:, i, :, lo:hi].unsqueeze(2).broadcast_to([P, TT, 2 * H, hi - lo])

    def sync(sp):
        def load_gate(n, p):
            wait(sp, x_done, n - 1)
            sp.dma_start(mod_gate[p][:, :, :], gate_rows(n)).then_inc(mod_gate_loaded[p], 16)

        def spread(n, p):
            sp.wait_ge(even_out, n * 2 + 1)
            sp.wait_ge(odd_out, n * 2 + 1)
            wait(sp, scores_ready, n * CHUNKS - CHUNKS)
            for r in range(G):
                sp.dma_start(kmask[p][32 * r:32 * r + 32, r:H:G, :].bitcast(F32), kT[32 * r:32 * r + 32, :, :].bitcast(F32)).then_inc(k_spread, 16)

        def step(b, p):
            if not is_last(b, 1):
                spread(b + 1, 1 - p)
                load_gate(b + 1, 1 - p)

        load_gate(0, 0)
        spread(0, 0)
        stepped(sp, 0, B - 1, 1, 14, step)

    def tensor(pe):
        def turn(n):
            pe.wait_ge(xhat_done, n + 1)
            wait(pe, values_done, n)
            for t in range(TT):
                last = nc.tensor.transpose(PT[:, t * P:(t + 1) * P], xhat[:, t, :], ident[:, :])
            last.then_inc(turned, 1)

        def project_qk(n):
            pe.wait_ge(hT_done, n + 1)
            wait(pe, odd_out, n * 2)
            for t in range(TT):
                last = nc.tensor.matmul(PQ[:, t * 2 * D:(t + 1) * 2 * D], hT[:, t * P:(t + 1) * P], wqk[:, :], start=True, stop=True)
            last.then_inc(qk_psum, 1)

        def project_v(n):
            pe.wait_ge(even_out, n * 2 + 2)
            for t in range(TT):
                last = nc.tensor.matmul(PV[:, t * D:(t + 1) * D], hT[:, t * P:(t + 1) * P], wv[:, :], start=True, stop=True)
            last.then_inc(v_psum, 1)

        def turn_stack(n, k):
            if k == 0:
                pe.wait_ge(stacks_done, n + 1)
            if k >= 2:
                pe.wait_ge((even_out, odd_out)[k % 2], n * 2 + 1)
            src, dst = (kstack, kstack, qstack, qstack)[k], (PT, PQ)[k % 2]
            for i in range(2):
                g = 2 * (k % 2) + i
                for t in range(TT):
                    last = nc.tensor.transpose(dst[:, i * T + t * P:i * T + (t + 1) * P],
                                               src[:, t * H + G * g:t * H + G * (g + 1), :, :].rearrange("p h s d -> p (h s d)").bitcast(F32),
                                               ident[:, :])
            last.then_inc(stacks_psum, 1)

        def maxima(b, p):
            pe.wait_ge(k_spread, b * (16 * G) + 16 * G)
            pe.wait_ge(even_out, b * 2 + 2)
            pe.wait_ge(odd_out, b * 2 + 2)
            wait(pe, probs_ready, b * CHUNKS)
            for c in range(CHUNKS):
                t, g = c // G, c % G
                wait(pe, rowmax_done, b * CHUNKS + (c - 1))
                for r in range(G):
                    last = nc.tensor.matmul(SC[c % 2][:, r * T:(r + 1) * T], qT[p][:, g, t * P:(t + 1) * P],
                                            kmask[p][:, G * g + r, :], start=True, stop=True)
                last.then_inc(max_psum, 1)
            pe.wait_ge(max_lo, b + 1)
            for t in range(TT):
                last = nc.tensor.transpose(SC[0][:, t * P:(t + 1) * P], maxstack[:, t, :].bitcast(F32), ident[:, :])
            last.then_inc(max_turned, 1)
            pe.wait_ge(maxT_done, b + 1)

        def scores(b, p, c):
            r, kb = c // TT, c % TT
            if c == 0:
                if with_max:
                    maxima(b, p)
                else:
                    pe.wait_ge(k_spread, b * (16 * G) + 16 * G)
                    pe.wait_ge(even_out, b * 2 + 2)
                    pe.wait_ge(odd_out, b * 2 + 2)
            wait(pe, probs_ready, b * CHUNKS + (c - 1))
            for g in range(G):
                last = nc.tensor.matmul(SC[c % 2][:, g * T:(g + 1) * T], kmask[p][:, G * g + r, kb * P:(kb + 1) * P],
                                        qT[p][:, g, :], start=True, stop=not with_max)
                if with_max:
                    last = nc.tensor.matmul(SC[c % 2][:, g * T:(g + 1) * T], sel[:, G * g + r, :], maxT[:, :],
                                            start=False, stop=True)
            last.then_inc(scores_ready, 1)

        def heads(b, p, c):
            r, kb = c // TT, c % TT
            s = r // 2
            if c == 0:
                wait(pe, sums_done, b)
                pe.wait_ge(values_done, b + 1)
            pe.wait_ge(probs_ready, b * CHUNKS + (c + 1))
            for g in range(G):
                last = nc.tensor.matmul(PO[32 * g:32 * g + 32, s * T:(s + 1) * T], vpad[p][:, kb, G * g + r, :],
                                        probs[:, c % 4, g, :], start=(c % 4 == 0), stop=(c % 4 == 3))
            last.then_inc(heads_done, 1)

        def turn_sums(n):
            pe.wait_ge(sums_done, n + 1)
            wait(pe, delta_done, n)
            for t in range(TT):
                for s in range(2):
                    last = nc.tensor.transpose(PP[:, (t * 2 + s) * P:(t * 2 + s + 1) * P], sums[:, s * T + t * P:s * T + (t + 1) * P], ident[:, :])
            last.then_inc(sums_turned, 1)

        def turn_heads(n):
            pe.wait_ge(heads_tok_done, n + 1)
            for t in range(TT):
                last = nc.tensor.transpose(PP[:, t * P:(t + 1) * P],
                                           heads_out_tok[:, t * H:(t + 1) * H, :].rearrange("p h d -> p (h d)"), ident[:, :])
            last.then_inc(heads_turned, 1)

        def project_out(n):
            pe.wait_ge(oT_done, n + 1)
            for t in range(TT):
                last = nc.tensor.matmul(PP[:, T + t * D:T + (t + 1) * D], oT[:, t * P:(t + 1) * P], wo[:, :], start=True, stop=True)
            last.then_inc(projected, 1)

        def step(b, p):
            first, more, projects = isinstance(b, int) and b == 0, not is_last(b, 1), not is_last(b, 2)
            for c in range(CHUNKS):
                scores(b, p, c)
                if c < 2 and not first:
                    heads(b - 1, 1 - p, c + CHUNKS - 2)
                if c >= 2:
                    heads(b, p, c - 2)
                if c < 2 and more:
                    turn_stack(b + 1, 2 * c)
                    turn_stack(b + 1, 2 * c + 1)
                if c == 2 and more:
                    project_v(b + 1)
                if c == 2 and not first:
                    turn_sums(b - 1)
                if c == 3 and projects:
                    turn(b + 2)
                if c == 4 and not first:
                    turn_heads(b - 1)
                if c == 4 and projects:
                    project_qk(b + 2)
                if c == 6 and not first:
                    project_out(b - 1)

        turn(0)
        project_qk(0)
        for k in range(4):
            turn_stack(0, k)
        project_v(0)
        turn(1)
        project_qk(1)
        stepped(pe, 0, B - 1, 1, 14, step)
        for c in (CHUNKS - 2, CHUNKS - 1):
            heads(B - 1, 1, c)
        turn_sums(B - 1)
        turn_heads(B - 1)
        project_out(B - 1)

    def scalar(act):
        def stacks_out(n, p, k):
            act.wait_ge(stacks_psum, n * 4 + (k + 1))
            if k == 1:
                wait(act, k_spread, n * (16 * G))
                dst = kT
            else:
                wait(act, scores_ready, n * CHUNKS - CHUNKS)
                dst = qT[p]
            nc.scalar.copy(dst[:, 2:4, :].rearrange("p g k -> p (g k)"), PQ).then_inc(odd_out, 1)

        def oT_out(n):
            act.wait_ge(heads_turned, n + 1)
            wait(act, projected, n)
            nc.scalar.copy(oT[:, :], PP[:, 0:T]).then_inc(oT_done, 1)

        def prob(b, c):
            act.wait_ge(scores_ready, b * CHUNKS + (c + 1))
            wait(act, heads_done, b * CHUNKS + (c - 3))
            nc.scalar.activation(probs[:, c % 4, :, :], SC[c % 2].rearrange("p (g q) -> p g q", g=G), ACT.Exp,
                                 scale=float(np.float32(1.0) / np.sqrt(np.float32(HD)))).then_inc(probs_ready, 1)

        def step(b, p):
            first, more = isinstance(b, int) and b == 0, not is_last(b, 1)
            for c in range(CHUNKS):
                prob(b, c)
                if c < 2 and more:
                    stacks_out(b + 1, 1 - p, 2 * c + 1)
                if c == 5 and not first:
                    oT_out(b - 1)

        stacks_out(0, 0, 1)
        stacks_out(0, 0, 3)
        stepped(act, 0, B - 1, 1, 14, step)
        oT_out(B - 1)

    def gpsimd(pool):
        def norm(n):
            wait(pool, rstd_done, n)
            pool.wait_ge(moments_done, n + 1)
            nc.gpsimd.tensor_tensor(vareps[:, :], moments[:, :, 1], eps[:, 0:TT], ALU.add).then_inc(vareps_done, 1)
            pool.wait_ge(vareps_done, n + 1)
            wait(pool, xhat_done, n)
            nc.gpsimd.tensor_tensor(rstd[:, :], vareps[:, :], minus_half[:, 0:TT], ALU.pow).then_inc(rstd_done, 1)

        def rotate(n):
            pool.wait_ge(qk_done, n + 1)
            wait(pool, rope_done, n)

            half = HD // 2
            nc.gpsimd.tensor_tensor(by_sin[:, :, :, 0:half], qk[:, :, :, half:HD], table(1, 0, half), ALU.mult)
            nc.gpsimd.tensor_tensor(by_sin[:, :, :, half:HD], qk[:, :, :, 0:half], table(1, half, HD), ALU.mult).then_inc(rope_products, 1)

        def bias_x(n, p):
            pool.wait_ge(mod_gate_loaded[p], n * 8 + (16 - 8 * p))
            pool.wait_ge(xhat_done, n + 1)
            nc.gpsimd.tensor_tensor(tiles(n), tiles(n), mod_gate[p][:, 1:2, :].broadcast_to([P, TT, D]),
                                    ALU.add).then_inc(x_biased, 1)

        def step(b, p):
            bias_x(b, p)
            if not is_last(b, 3):
                norm(b + 3)
            if not is_last(b, 2):
                rotate(b + 2)

        norm(0)
        norm(1)
        rotate(0)
        norm(2)
        rotate(1)
        stepped(pool, 0, B - 1, 1, 14, step)

    def vector(dve):
        def norm_a(n):
            wait(dve, moments_done, n)
            for t in range(TT):
                last = nc.vector.bn_stats(stats[:, t, :], tile(n, t)[:, 0, :])
            last.then_inc(stats_done, 1)
            wait(dve, xhat_done, n)
            dve.wait_ge(stats_done, n + 1)
            nc.vector.memset(unread[:, :], 0.0)
            for t in range(TT):
                last = nc.vector.bn_aggr(moments[:, t, :], stats[:, t, :])
            last.then_inc(moments_done, 1)

        def norm_b(n):
            dve.wait_ge(rstd_done, n + 1)
            wait(dve, turned, n)
            for t in range(TT):
                last = nc.vector.tensor_scalar(xhat[:, t, :], tile(n, t)[:, 0, :], moments[:, t, 0:1], rstd[:, t:t + 1], ALU.subtract, ALU.mult)
            last.then_inc(xhat_done, 1)

        def turned_out(n):
            dve.wait_ge(turned, n + 1)
            wait(dve, v_psum, n)
            nc.vector.tensor_scalar(hT[:, :], PT[:, 0:T], mod(0, n), mod(1, n), ALU.mult, ALU.add).then_inc(hT_done, 1)

        def add_biases(n):
            dve.wait_ge(qk_psum, n + 1)
            wait(dve, rope_products, n)
            wait(dve, by_cos_done, n)
            nc.vector.tensor_tensor(qk[:, :, :, :].rearrange("p t h d -> p t (h d)"), PQ.rearrange("p (t c) -> p t c", t=TT),
                                    bqk[:, :].unsqueeze(1).broadcast_to([P, TT, 2 * D]), ALU.add).then_inc(qk_done, 1)

        def cosines(n):
            dve.wait_ge(qk_done, n + 1)
            wait(dve, rope_done, n)
            nc.vector.tensor_tensor(by_cos[:, :, :, :], qk[:, :, :, :], table(0, 0, HD), ALU.mult).then_inc(by_cos_done, 1)

        def values(n, p):
            dve.wait_ge(v_psum, n + 1)
            wait(dve, heads_done, n * CHUNKS - CHUNKS)
            for s in range(2):
                def heads_of(ap):
                    return ap.rearrange("p (j r d) -> p j r d", r=G, d=HD)[:, :, 2 * s:2 * s + 2, :]
                last = nc.vector.tensor_tensor(vdiag[p][s], heads_of(PV), heads_of(bv[:, :]), ALU.add)
            last.then_inc(values_done, 1)

        def split(n):
            dve.wait_ge(rope_products, n + 1)
            dve.wait_ge(by_cos_done, n + 1)
            wait(dve, stacks_done, n)
            nc.vector.tensor_tensor(turned_qk[:, :, :, :].rearrange("p k (t h) d -> p t k (h d)", t=TT),
                                    by_cos[:, :, :, :].rearrange("p t (k h) d -> p t k (h d)", k=2),
                                    by_sin[:, :, :, :].rearrange("p t (k h) d -> p t k (h d)", k=2), ALU.add).then_inc(rope_done, 1)
            dve.wait_ge(rope_done, n + 1)
            wait(dve, stacks_psum, n * 4)

            def twice(i):
                return turned_qk[:, i, :, :].unsqueeze(2).broadcast_to([P, TT * H, 2, HD])

            nc.vector.tensor_copy(kstack[:, :, 0:2, :], twice(1))
            nc.vector.tensor_copy(qstack[:, :, 0:4:2, :], twice(0)).then_inc(hi_done, 1)
            dve.wait_ge(hi_done, n + 1)
            nc.vector.tensor_tensor(kstack[:, :, 2:4, :], twice(1), kstack[:, :, 0:2, :].bitcast(F32), ALU.subtract)
            nc.vector.tensor_tensor(qstack[:, :, 1:4:2, :], twice(0), qstack[:, :, 0:4:2, :].bitcast(F32), ALU.subtract).then_inc(stacks_done, 1)

        def stacks_out(n, p, k):
            dve.wait_ge(stacks_psum, n * 4 + (k + 1))
            if k == 0:
                wait(dve, k_spread, n * (16 * G))
                dst = kT
            else:
                wait(dve, scores_ready, n * CHUNKS - CHUNKS)
                dst = qT[p]
            nc.vector.tensor_copy(dst[:, 0:2, :].rearrange("p g k -> p (g k)"), PT).then_inc(even_out, 1)

        def sums_out(n):
            dve.wait_ge(heads_done, n * CHUNKS + CHUNKS)
            wait(dve, sums_turned, n)
            nc.vector.tensor_copy(sums[:, :], PO).then_inc(sums_done, 1)

        def divide(n):
            dve.wait_ge(sums_turned, n + 1)
            wait(dve, heads_tok_done, n)
            by_head = PP.rearrange("p (h w) -> p h w", w=16)
            nc.vector.reciprocal(recip[:, :], by_head[:, :, HD]).then_inc(recip_done, 1)
            dve.wait_ge(recip_done, n + 1)
            wait(dve, heads_turned, n)
            nc.vector.tensor_tensor(heads_out_tok[:, :, :], by_head[:, :, 0:HD],
                                    recip[:, :].unsqueeze(2).broadcast_to([P, TT * H, HD]), ALU.mult).then_inc(heads_tok_done, 1)

        def residual(n, p):
            dve.wait_ge(projected, n + 1)
            wait(dve, x_done, n)
            dve.wait_ge(mod_gate_loaded[p], n * 8 + (16 - 8 * p))
            nc.vector.tensor_tensor(delta[:, :, :], PP[:, T:2 * T].rearrange("p (t d) -> p t d", t=TT),
                                    mod_gate[p][:, 0:1, :].broadcast_to([P, TT, D]), ALU.mult).then_inc(delta_done, 1)
            dve.wait_ge(delta_done, n + 1)
            dve.wait_ge(x_biased, n + 1)
            nc.vector.tensor_tensor(tiles(n), tiles(n), delta[:, :, :], ALU.add).then_inc(x_done, 1)

        def maxima(b):
            for c in range(CHUNKS):
                t, g = c // G, c % G
                dve.wait_ge(max_psum, b * CHUNKS + (c + 1))
                if c == 0:
                    wait(dve, max_lo, b)
                nc.vector.tensor_reduce(rowmax[:, t, G * g:G * (g + 1)], SC[c % 2].rearrange("p (r k) -> p r k", r=G),
                                        AX.X, ALU.max).then_inc(rowmax_done, 1)
            dve.wait_ge(rowmax_done, b * CHUNKS + CHUNKS)
            wait(dve, max_turned, b)
            nc.vector.tensor_scalar(maxstack[:, :, 0:H], rowmax[:, :, :], -1.0, None, ALU.mult).then_inc(max_hi, 1)
            dve.wait_ge(max_hi, b + 1)
            nc.vector.scalar_tensor_tensor(out=maxstack[:, :, H:2 * H], in0=rowmax[:, :, :], scalar=-1.0,
                                           in1=maxstack[:, :, 0:H].bitcast(F32), op0=ALU.mult, op1=ALU.subtract).then_inc(max_lo, 1)
            dve.wait_ge(max_turned, b + 1)
            wait(dve, scores_ready, b * CHUNKS)
            nc.vector.tensor_copy(maxT[:, :], SC[0][:, 0:T]).then_inc(maxT_done, 1)

        def step(b, p):
            first, more, projects = isinstance(b, int) and b == 0, not is_last(b, 1), not is_last(b, 2)
            norms = not is_last(b, 3)
            if with_max:
                maxima(b)
            if more:
                stacks_out(b + 1, 1 - p, 0)
            if not first:
                sums_out(b - 1)
            if more:
                stacks_out(b + 1, 1 - p, 2)
                values(b + 1, 1 - p)
            if not first:
                divide(b - 1)
            if projects:
                turned_out(b + 2)
            if norms:
                norm_a(b + 3)
            if projects:
                add_biases(b + 2)
                cosines(b + 2)
            if norms:
                norm_b(b + 3)
            if projects:
                split(b + 2)
            if not first:
                residual(b - 1, 1 - p)

        norm_a(0)
        norm_b(0)
        turned_out(0)
        norm_a(1)
        add_biases(0)
        cosines(0)
        norm_b(1)
        split(0)
        stacks_out(0, 0, 0)
        stacks_out(0, 0, 2)
        values(0, 0)
        turned_out(1)
        norm_a(2)
        add_biases(1)
        cosines(1)
        norm_b(2)
        split(1)
        stepped(dve, 0, B - 1, 1, 14, step)
        sums_out(B - 1)
        divide(B - 1)
        residual(B - 1, 1)

    return {"sync": sync, "tensor": tensor, "scalar": scalar, "gpsimd": gpsimd, "vector": vector}


def attention_1_setup(nc, ctx, dram, sbuf, psum, loads):
    def sem(name):
        return dram["semaphores"].enter_context(nc.semaphore("s1_" + name))

    def sb(name, shape, dt=F32):
        return ctx.enter_context(nc.sbuf_tensor("s1_" + name, shape, dt))

    modcol, ident, wqk, bqk, kmask, vpad = (sbuf[k] for k in ("modcol", "ident", "wqk1", "bqk1", "kmask1", "vpad1"))
    w_loaded, zeroed, squared, most, summed, moved, step, filled = map(
        sem, ("w_loaded", "zeroed", "squared", "most", "summed", "moved", "step", "filled"))
    mod2, mod2max = sb("mod2", [P, 2, B]), sb("mod2max", [P, 2])
    w2, ones, b2 = sb("w2", [P, 2 * D]), sb("ones", [P, 1]), sb("b2", [1, 2 * D])
    terms, whead, bhead, h2 = sb("terms", [1, 2]), sb("whead", [1, 2 * H]), sb("bhead", [1, 2 * H]), sb("h2", [1, 4])
    head2, top = sb("head2", [1, 2 * H]), sb("top", [1, 1])
    small = sbuf["small_scores"]
    wsum, modrow = psum[0:1, 0:2 * D], psum[0:1, 512:512 + 2 * P]
    near, far = 1.0 + 1.0 / 16, 17.0

    with nc.Block() as block:
        @block.sync
        def _(sp):
            for dst, src in loads:
                sp.dma_start(dst, src).then_inc(w_loaded, 16)
            sp.wait_ge(w_loaded, 16 * len(loads))

        @block.gpsimd
        def _(pool):
            for v in vpad:
                last = nc.gpsimd.memset(v[:, :, :, :], 0.0)
            last.then_inc(zeroed, 1)
            pool.wait_ge(zeroed, 1)
            for v in vpad:
                for a in range(2):
                    nc.gpsimd.memset(v[:, :, a:H:2, 16 * a + HD:16 * a + HD + 1], 1.0)
            for k in kmask:
                nc.gpsimd.memset(k[:, :, :].bitcast(F32), 0.0)
            nc.gpsimd.memset(sbuf["a1"]["maxstack"][:, :, :].bitcast(F32), 0.0)

        @block.tensor
        def _(pe):
            pe.wait_ge(squared, 1)
            nc.tensor.matmul(wsum, ones[:, :], w2[:, :], start=True, stop=True)
            pe.wait_ge(most, 1)
            for i in range(2):
                last = nc.tensor.matmul(modrow[:, i * P:(i + 1) * P], mod2max[:, i:i + 1], ident[:, :], start=True, stop=True)
            last.then_inc(moved, 1)

        @block.vector
        def _(dve):
            def then(ins, k):
                ins.then_inc(step, 1)
                dve.wait_ge(step, k)

            nc.vector.memset(ones[:, :], 1.0)
            dve.wait_ge(w_loaded, 16 * len(loads))
            nc.vector.tensor_copy(sbuf["sel"][:, :, :], sbuf["sel_loaded"][:, :, :])
            nc.vector.tensor_tensor(w2[:, :], wqk[:, :], wqk[:, :], ALU.mult)
            nc.vector.tensor_tensor(b2[:, :], bqk[0:1, :], bqk[0:1, :], ALU.mult)
            nc.vector.tensor_tensor(mod2[:, :, :], modcol[:, 0:2, :], modcol[:, 0:2, :], ALU.mult).then_inc(squared, 1)
            dve.wait_ge(squared, 1)
            nc.vector.tensor_reduce(mod2max[:, :], mod2[:, :, :], AX.X, ALU.max).then_inc(most, 1)
            dve.wait_ge(moved, 1)
            nc.vector.tensor_reduce(terms[:, :], modrow.rearrange("p (i d) -> p i d", i=2), AX.X, ALU.max)
            nc.vector.tensor_reduce(bhead[:, :], b2[:, :].rearrange("p (h d) -> p h d", d=HD), AX.X, ALU.add)
            then(nc.vector.tensor_reduce(whead[:, :], wsum.rearrange("p (h d) -> p h d", d=HD), AX.X, ALU.add), 1)
            then(nc.vector.tensor_scalar(h2[:, 0:1], terms[:, 0:1], near * near * D, None, ALU.mult), 2)
            then(nc.vector.tensor_scalar(h2[:, 1:2], terms[:, 1:2], far * near * D, None, ALU.mult), 3)
            then(nc.vector.tensor_tensor(h2[:, 2:3], h2[:, 0:1], h2[:, 1:2], ALU.add), 4)
            then(nc.vector.tensor_scalar(bhead[:, :], bhead[:, :], far, None, ALU.mult), 5)
            then(nc.vector.scalar_tensor_tensor(out=head2[:, :], in0=whead[:, :], scalar=h2[:, 2:3], in1=bhead[:, :],
                                                op0=ALU.mult, op1=ALU.add), 6)
            then(nc.vector.tensor_reduce(top[:, :], head2[:, :], AX.X, ALU.max), 7)
            nc.vector.tensor_scalar(small[:, :], top[:, :], SMALL_SCORE * float(np.sqrt(HD)), None, ALU.is_le)


FT = 512
FTT = FT // P
FB = FT // T
NT = B * T // FT
HID = 512
KH = HID // P
EXACT_ABOVE = 0.5
W1, W2, H1, H2, W3, WEIGHTS = 0, HID, 2 * HID, 2 * HID + KH * HID, 2 * HID + 2 * KH * HID, 2 * HID + 2 * KH * HID + KH * D


def ffn_1(nc, ctx, dram, sbuf, psum, split):
    def sem(name):
        key = "sem_" + name
        if key not in sbuf["ffn"]:
            sbuf["ffn"][key] = dram["semaphores"].enter_context(nc.semaphore("f_" + name))
        return sbuf["ffn"][key]

    def sb(name, shape, dt=F32):
        if name not in sbuf["ffn"]:
            sbuf["ffn"][name] = ctx.enter_context(nc.sbuf_tensor("ffn_" + name, shape, dt))
        return sbuf["ffn"][name]

    X, ident, minus_half, eps, modcol = (sbuf[k] for k in ("X", "ident", "minus_half", "eps", "modcol"))
    scales, out_scale = sbuf["scales"], sbuf["out_scale"]
    weights = sbuf["weights_r"] if split else sbuf["weights"]
    stats, moments, vareps, rstd = sb("stats", [P, FTT, 6]), sb("moments", [P, FTT, 2]), sb("vareps", [P, FTT]), sb("rstd", [P, FTT])
    xhat, unread = sb("xhat", [P, FTT, D]), sb("unread", [P, 1])
    tanh, gated = sb("tanh", [P, 2, FT]), sb("gated", [P, 2, FT])
    y = sb("y", [P, FT])
    full = [sb(f"full{i}", [P, KH if i else 1, FT]) for i in range(4)]
    hi = [sb(f"hi{i}", [P, KH if i else 1, FT], F32R) for i in range(4)]
    lo = [sb(f"lo{i}", [P, KH if i else 1, FT], F32R) for i in range(4)]
    bank = [psum[:, 512 * i:512 * (i + 1)] for i in range(8)]

    stats_done, moments_done, vareps_done, rstd_done, xhat_done, turned = map(
        sem, ("stats", "moments", "vareps", "rstd", "xhat", "turned"))
    full_done = [sem(f"full{i}") for i in range(4)]
    hi_done, lo_done = [sem(f"hi{i}") for i in range(4)], [sem(f"lo{i}") for i in range(4)]
    tanh_done, gated_done = sem("tanh"), sem("gated")
    psum_done = [sem(f"psum{i}") for i in range(4)]
    y_done, turned_back, x_done = sem("y"), sem("turned_back"), sem("x_done")
    blocks = [1, KH, KH, KH]
    sums = [KH, KH, KH, 1]

    def tile(n, t):
        return X[:, bass.ds(n * FTT + t, 1), :][:, 0, :] if not isinstance(n, int) else X[:, n * FTT + t, :]

    def tiles(n):
        return X[:, bass.ds(n * FTT, FTT), :] if not isinstance(n, int) else X[:, n * FTT:(n + 1) * FTT, :]

    def col(ap, n, i):
        return ap[:, bass.ds(n * FB + i, 1)] if not isinstance(n, int) else ap[:, n * FB + i:n * FB + i + 1]

    def tensor(pe):
        def value_ready(layer, n, k):
            for s in ((hi_done, lo_done) if split else (full_done,)):
                pe.wait_ge(s[layer], n * blocks[layer] + (k + 1))

        def product(dst, layer, w0, k, first, last):
            parts = (hi, lo) if split else (full,)
            for i, part in enumerate(parts):
                ins = nc.tensor.matmul(dst, weights[:, w0:w0 + P], part[layer][:, k, :],
                                       start=first and i == 0, stop=last and i == len(parts) - 1)
            return ins

        def turn(n):
            pe.wait_ge(xhat_done, n + 1)
            wait(pe, full_done[0], n)
            for t in range(FTT):
                last = nc.tensor.transpose(bank[4][:, t * P:(t + 1) * P], xhat[:, t, :], ident[:, :])
            last.then_inc(turned, 1)

        def gates(n):
            value_ready(0, n, 0)
            for m in range(KH):
                if m < 2:
                    wait(pe, full_done[3], n * KH)
                else:
                    pe.wait_ge(full_done[1], n * KH + (m - 1))
                pair = 2 * (m % 2)
                product(bank[pair], 0, W1 + m * P, 0, True, True)
                product(bank[pair + 1], 0, W2 + m * P, 0, True, True).then_inc(psum_done[0], 1)

        def last_layer(n):
            wait(pe, y_done, n)
            for k in range(KH):
                value_ready(3, n, k)
                last = product(bank[5], 3, W3 + k * D, k, k == 0, k == KH - 1)
            last.then_inc(psum_done[3], 1)

        def hidden(layer, n, w0):
            if layer == 1:
                order = [(k, m) for k in range(KH - 1) for m in (0, 1)] + [(k, m) for k in range(KH - 1) for m in (2, 3)]
                order += [(KH - 1, m) for m in range(KH)]
            else:
                order = [(k, m) for k in range(KH) for m in range(KH)]
            seen = set()
            for k, m in order:
                if k not in seen:
                    value_ready(layer, n, k)
                    seen.add(k)
                if k == 0:
                    pe.wait_ge(full_done[layer], n * KH + ((3 + m // 2) if layer == 1 else (m + 1)))
                ins = product(bank[m], layer, w0 + k * HID + m * P, k, k == 0, k == KH - 1)
                if k == KH - 1:
                    ins.then_inc(psum_done[layer], 1)

        def turn_back(n):
            pe.wait_ge(y_done, n + 1)
            wait(pe, x_done, n)
            for t in range(FTT):
                last = nc.tensor.transpose(bank[6][:, t * P:(t + 1) * P], y[:, t * P:(t + 1) * P], ident[:, :])
            last.then_inc(turned_back, 1)

        def step(n):
            first = isinstance(n, int) and n == 0
            gates(n)
            if not first:
                last_layer(n - 1)
            hidden(1, n, H1)
            if not (isinstance(n, int) and n == NT - 1):
                turn(n + 1)
            hidden(2, n, H2)
            if not first:
                turn_back(n - 1)

        turn(0)
        step(0)
        with pe.Fori(1, NT - 1) as n:
            step(n)
        step(NT - 1)
        last_layer(NT - 1)
        turn_back(NT - 1)

    def scalar(act):
        def high(layer, n, k):
            act.wait_ge(full_done[layer], n * blocks[layer] + (k + 1))
            wait(act, psum_done[layer], n * sums[layer])
            nc.scalar.copy(hi[layer][:, k, :], full[layer][:, k, :]).then_inc(hi_done[layer], 1)

        def gate(n, m):
            act.wait_ge(psum_done[0], n * KH + (m + 1))
            wait(act, gated_done, n * KH + (m - 1))
            nc.scalar.activation(tanh[:, m % 2, :], bank[2 * (m % 2)], ACT.Tanh, scale=scales[:, 0, m:m + 1]).then_inc(tanh_done, 1)

        def gelu(layer, n, m):
            act.wait_ge(psum_done[layer], n * KH + (m + 1))
            wait(act, psum_done[layer + 1], n * sums[layer + 1])
            nc.scalar.activation(full[layer + 1][:, m, :], bank[m], ACT.Gelu,
                                 scale=scales[:, 1 + layer, m:m + 1]).then_inc(full_done[layer + 1], 1)

        def step(n):
            for m in range(KH):
                gate(n, m)
                if split and m >= 1:
                    high(1, n, m - 1)
            if split:
                high(1, n, KH - 1)
            for layer in (1, 2):
                for m in range(KH):
                    gelu(layer, n, m)

        step(0)
        with act.Fori(1, NT - 1) as n:
            step(n)
        step(NT - 1)

    def gpsimd(pool):
        def norm(n):
            wait(pool, rstd_done, n)
            pool.wait_ge(moments_done, n + 1)
            nc.gpsimd.tensor_tensor(vareps[:, :], moments[:, :, 1], eps[:, 0:FTT], ALU.add).then_inc(vareps_done, 1)
            pool.wait_ge(vareps_done, n + 1)
            wait(pool, xhat_done, n)
            nc.gpsimd.tensor_tensor(rstd[:, :], vareps[:, :], minus_half[:, 0:FTT], ALU.pow).then_inc(rstd_done, 1)

        def low(layer, n, k):
            if not split:
                return
            pool.wait_ge(hi_done[layer], n * blocks[layer] + (k + 1))
            pool.wait_ge(full_done[layer], n * blocks[layer] + (k + 1))
            wait(pool, psum_done[layer], n * sums[layer])
            nc.gpsimd.tensor_tensor(lo[layer][:, k, :], full[layer][:, k, :], hi[layer][:, k, :].bitcast(F32),
                                    ALU.subtract).then_inc(lo_done[layer], 1)

        def step(n):
            more = not (isinstance(n, int) and n == NT - 1)
            for k in range(KH):
                low(1, n, k)
            if more:
                norm(n + 1)
            for k in range(KH):
                low(2, n, k)
            if more:
                low(0, n + 1, 0)
            for k in range(KH):
                low(3, n, k)

        norm(0)
        low(0, 0, 0)
        step(0)
        with pool.Fori(1, NT - 1) as n:
            step(n)
        step(NT - 1)

    def vector(dve):
        def norm_a(n):
            wait(dve, moments_done, n)
            for t in range(FTT):
                last = nc.vector.bn_stats(stats[:, t, :], tile(n, t))
            last.then_inc(stats_done, 1)
            wait(dve, xhat_done, n)
            dve.wait_ge(stats_done, n + 1)
            nc.vector.memset(unread[:, :], 0.0)
            for t in range(FTT):
                last = nc.vector.bn_aggr(moments[:, t, :], stats[:, t, :])
            last.then_inc(moments_done, 1)

        def norm_b(n):
            dve.wait_ge(rstd_done, n + 1)
            wait(dve, turned, n)
            for t in range(FTT):
                last = nc.vector.tensor_scalar(xhat[:, t, :], tile(n, t), moments[:, t, 0:1], rstd[:, t:t + 1], ALU.subtract, ALU.mult)
            last.then_inc(xhat_done, 1)

        def high(layer, n, k):
            if not split:
                return
            dve.wait_ge(full_done[layer], n * blocks[layer] + (k + 1))
            wait(dve, psum_done[layer], n * sums[layer])
            nc.vector.tensor_copy(hi[layer][:, k, :], full[layer][:, k, :]).then_inc(hi_done[layer], 1)

        def modulate(n):
            dve.wait_ge(turned, n + 1)
            wait(dve, psum_done[0], n * KH)
            for i in range(FB):
                last = nc.vector.tensor_scalar(full[0][:, 0, i * T:(i + 1) * T], bank[4][:, i * T:(i + 1) * T],
                                               col(modcol[:, 2, :], n, i), col(modcol[:, 3, :], n, i), ALU.mult, ALU.add)
            last.then_inc(full_done[0], 1)

        def gate(n, m):
            dve.wait_ge(tanh_done, n * KH + (m + 1))
            wait(dve, full_done[1], n * KH + (m - 1))
            nc.vector.scalar_tensor_tensor(out=gated[:, m % 2, :], in0=tanh[:, m % 2, :], scalar=1.0, in1=bank[2 * (m % 2)],
                                           op0=ALU.add, op1=ALU.mult).then_inc(gated_done, 1)
            dve.wait_ge(gated_done, n * KH + (m + 1))
            wait(dve, psum_done[1], n * KH)
            nc.vector.scalar_tensor_tensor(out=full[1][:, m, :], in0=bank[2 * (m % 2) + 1], scalar=scales[:, 1, m:m + 1],
                                           in1=gated[:, m % 2, :], op0=ALU.mult, op1=ALU.mult).then_inc(full_done[1], 1)

        def y_out(n):
            dve.wait_ge(psum_done[3], n + 1)
            wait(dve, turned_back, n)
            for i in range(FB):
                last = nc.vector.tensor_scalar(y[:, i * T:(i + 1) * T], bank[5][:, i * T:(i + 1) * T],
                                               col(out_scale, n, i), None, ALU.mult)
            last.then_inc(y_done, 1)

        def residual(n):
            dve.wait_ge(turned_back, n + 1)
            nc.vector.tensor_tensor(tiles(n), tiles(n), bank[6].rearrange("p (t d) -> p t d", t=FTT), ALU.add).then_inc(x_done, 1)

        def step(n):
            first, more = isinstance(n, int) and n == 0, not (isinstance(n, int) and n == NT - 1)
            for m in range(KH):
                gate(n, m)
            if not first:
                y_out(n - 1)
            if more:
                norm_a(n + 1)
                norm_b(n + 1)
            for k in range(KH):
                high(2, n, k)
            if more:
                modulate(n + 1)
                high(0, n + 1, 0)
            for k in range(KH):
                high(3, n, k)
            if not first:
                residual(n - 1)

        norm_a(0)
        norm_b(0)
        modulate(0)
        high(0, 0, 0)
        step(0)
        with dve.Fori(1, NT - 1) as n:
            step(n)
        step(NT - 1)
        y_out(NT - 1)
        residual(NT - 1)

    return {"tensor": tensor, "scalar": scalar, "gpsimd": gpsimd, "vector": vector}


def ffn_1_setup(nc, ctx, dram, sbuf, psum, loads):
    def sem(name):
        return dram["semaphores"].enter_context(nc.semaphore("s2_" + name))

    def sb(name, shape, dt=F32):
        return ctx.enter_context(nc.sbuf_tensor("s2_" + name, shape, dt))

    ident, weights, weights_r, scales = (sbuf[k] for k in ("ident", "weights", "weights_r", "scales"))
    w_loaded, rounded, compared, least, moved, scaled = map(sem, ("w_loaded", "rounded", "compared", "least", "moved", "scaled"))
    equal, worst, all_equal, raw = sb("equal", [P, WEIGHTS]), sb("worst", [P, 1]), sb("all_equal", [1, 1]), sb("raw", [P, 5, KH])

    with nc.Block() as block:
        @block.sync
        def _(sp):
            for dst, src in loads + [(raw[:, :, :].rearrange("p i k -> p (i k)"), sbuf["scales_in"])]:
                sp.dma_start(dst, src).then_inc(w_loaded, 16)
            sp.wait_ge(w_loaded, 16 * (len(loads) + 1))

        @block.scalar
        def _(act):
            act.wait_ge(w_loaded, 16 * (len(loads) + 1))
            nc.scalar.copy(weights_r[:, 0:H2], weights[:, 0:H2]).then_inc(rounded, 1)

        @block.tensor
        def _(pe):
            pe.wait_ge(least, 1)
            nc.tensor.matmul(psum[0:1, 0:P], worst[:, :], ident[:, :], start=True, stop=True).then_inc(moved, 1)

        @block.vector
        def _(dve):
            dve.wait_ge(w_loaded, 16 * (len(loads) + 1))
            nc.vector.tensor_scalar(scales[:, 0, :], raw[:, 0, :], 0.5, None, ALU.mult)
            nc.vector.scalar_tensor_tensor(out=scales[:, 1, :], in0=raw[:, 0, :], scalar=0.5, in1=raw[:, 1, :], op0=ALU.mult, op1=ALU.mult)
            nc.vector.tensor_copy(scales[:, 2:4, :], raw[:, 2:4, :])
            nc.vector.tensor_scalar(sbuf["out_scale"][:, :], sbuf["modcol"][:, 4, :], raw[:, 4, 0:1], None, ALU.mult)
            nc.vector.tensor_copy(weights_r[:, H2:], weights[:, H2:]).then_inc(scaled, 1)
            dve.wait_ge(scaled, 1)
            dve.wait_ge(rounded, 1)
            nc.vector.tensor_tensor(equal[:, :], weights[:, :], weights_r[:, :].bitcast(F32), ALU.is_equal).then_inc(compared, 1)
            dve.wait_ge(compared, 1)
            nc.vector.tensor_reduce(worst[:, :], equal[:, :], AX.X, ALU.min).then_inc(least, 1)
            dve.wait_ge(moved, 1)
            nc.vector.tensor_reduce(all_equal[:, :], psum[0:1, 0:P], AX.X, ALU.min).then_inc(scaled, 1)
            dve.wait_ge(scaled, 2)
            nc.vector.tensor_scalar(sbuf["exact_weights"][:, :], all_equal[:, :], EXACT_ABOVE, None, ALU.is_gt)


def adaln_program(nc, ins, out):
    with ExitStack() as ctx:
        def sb(name, shape, dt=F32):
            return ctx.enter_context(nc.sbuf_tensor(name, shape, dt))

        psum_all = ctx.enter_context(nc.psum_tensor("psum_all", [P, 8 * 512], F32))
        psum = psum_all[:, :]
        X = sb("X", [P, B * TT, D])
        sbuf = {
            "X": X, "ident": sb("ident", [P, P]), "ident16": sb("ident16", [P, P], F16),
            "modcol": sb("modcol", [P, 5, B]), "minus_half": sb("minus_half", [P, 8]),
            "eps": sb("eps", [P, 8]), "biases": sb("biases", [P, 3]),
        }
        x_view = ins["x"].rearrange("b (t p) d -> p (b t) d", p=P)
        out_view = out.rearrange("b (t p) d -> p (b t) d", p=P)
        table = nc.dram_tensor("modulation_table", [B, ROWS, D], F32, kind="Internal").ap()
        dram = {
            "x": x_view, "table": table,
            "condT": [ins["c0T"], ins["c1T"]], "wmod": [ins["wmod0"], ins["wmod1"]],
            "bo": [ins["bo0"], ins["bo1"]],
        }
        dram["semaphores"] = ctx
        dram["loads"] = [(sbuf["ident"][:, :], ins["ident"])]
        dram["fills"] = [(sbuf["minus_half"][:, :], -0.5), (sbuf["eps"][:, :], LN_EPS)]
        dram["fills"] += [(sbuf["biases"][:, i:i + 1], v) for i, v in enumerate((-COLLAPSE * SHARPNESS, 0.625, 0.3125))]
        with ExitStack() as part:
            def sb0(name, shape, dt=F32):
                return part.enter_context(nc.sbuf_tensor(name, shape, dt))
            sbuf["kmask"] = [sb0(f"kmask{i}", [P, H, T], F16) for i in range(2)]
            sbuf["vpad"] = [sb0(f"vpad{i}", [P, TT, H, 32]) for i in range(2)]
            sbuf["probs"] = sb0("probs", [P, 4, G, UNIT_PAD])
            sbuf["wqk0"], sbuf["wv0"], sbuf["wo0"] = sb0("wqk0", [P, 2 * D]), sb0("wv0", [P, D]), sb0("wo0", [P, D])
            sbuf["gamma"], sbuf["beta"], sbuf["gqk"] = sb0("gammacol", [P, 1]), sb0("betacol", [P, 1]), sb0("gqk", [P, 2, D])
            dram["loads"] += [
                (sbuf["wqk0"][:, :], ins["wqk0"]), (sbuf["wv0"][:, :], ins["wv0"]), (sbuf["wo0"][:, :], ins["wo0"]),
                (sbuf["gamma"][:, :], ins["gamma"]), (sbuf["beta"][:, :], ins["beta"]),
                (sbuf["gqk"][:, :, :].rearrange("p a d -> p (a d)"), ins["gqk"].partition_broadcast(P)),
                (sbuf["ident16"][:, :], ins["ident16"]),
            ]
            dram["fills"] += [(k[:, :, :], 0.0) for k in sbuf["kmask"]] + [(v[:, :, :, :], 0.0) for v in sbuf["vpad"]]
            dram["fills"] += [(sbuf["probs"][:, :, :, T:UNIT_PAD], 1.0)]
            with ExitStack() as first:
                setup_phase(nc, first, dram, sbuf, psum)
            with ExitStack() as first:
                attention_0(nc, first, dram, sbuf, psum)
        dram.update({k: ins[k] for k in ("ctrl", "f1", "f2", "ebias", "tie", "own")})
        with ExitStack() as first:
            experts_0(nc, first, dram, sbuf, psum)
        with ExitStack() as part:
            def sb1(name, shape, dt=F32):
                return part.enter_context(nc.sbuf_tensor(name, shape, dt))
            sbuf["kmask1"] = [sb1(f"kmask1_{i}", [P, H, T], F32R) for i in range(2)]
            sbuf["vpad1"] = [sb1(f"vpad1_{i}", [P, TT, H, 32]) for i in range(2)]
            sbuf["wqk1"], sbuf["wv1"], sbuf["wo1"] = sb1("wqk1", [P, 2 * D]), sb1("wv1", [P, D]), sb1("wo1", [P, D])
            sbuf["bqk1"], sbuf["bv1"] = sb1("bqk1", [P, 2 * D]), sb1("bv1", [P, TT * D])
            sbuf["rope"], sbuf["sel"] = sb1("rope", [P, 2, TT, HD]), sb1("sel", [P, H, P], F32R)
            sbuf["sel_loaded"] = sb1("sel_loaded", [P, H, P])
            sbuf["small_scores"] = sb1("small_scores", [1, 1], I32)
            sbuf["a1"] = {}
            loads = [(sbuf["wqk1"][:, :], ins["wqk1"]), (sbuf["wv1"][:, :], ins["wv1"]), (sbuf["wo1"][:, :], ins["wo1"]),
                     (sbuf["bqk1"][:, :], ins["bqk1"].partition_broadcast(P)),
                     (sbuf["bv1"][:, :], ins["bv1"].partition_broadcast(P)),
                     (sbuf["rope"][:, :, :, :].rearrange("p i t d -> p (i t d)"), ins["rope"]),
                     (sbuf["sel_loaded"][:, :, :].rearrange("p h c -> p (h c)"), ins["sel"])]
            general = attention_1(nc, part, dram, sbuf, psum, True)
            bounded = attention_1(nc, part, dram, sbuf, psum, False)
            with ExitStack() as first:
                attention_1_setup(nc, first, dram, sbuf, psum, loads)
            with nc.Block() as block:
                def either(eng, name):
                    small = eng.value_load(sbuf["small_scores"][0:1, 0:1], min_val=0, max_val=1)
                    with eng.If(small == 1):
                        bounded[name](eng)
                    with eng.Else():
                        general[name](eng)

                @block.sync
                def _(sp):
                    either(sp, "sync")

                @block.tensor
                def _(pe):
                    either(pe, "tensor")

                @block.scalar
                def _(act):
                    either(act, "scalar")

                @block.gpsimd
                def _(pool):
                    either(pool, "gpsimd")

                @block.vector
                def _(dve):
                    either(dve, "vector")
        with ExitStack() as part:
            def sb2(name, shape, dt=F32):
                return part.enter_context(nc.sbuf_tensor(name, shape, dt))
            sbuf["weights"], sbuf["weights_r"] = sb2("weights", [P, WEIGHTS]), sb2("weights_r", [P, WEIGHTS], F32R)
            sbuf["scales"], sbuf["out_scale"] = sb2("scales", [P, 4, KH]), sb2("out_scale", [P, B])
            sbuf["exact_weights"], sbuf["scales_in"], sbuf["ffn"] = sb2("exact_weights", [1, 1], I32), ins["scales"], {}
            loads = [(sbuf["weights"][:, lo:hi], ins[k]) for k, lo, hi in (
                ("w1", W1, W2), ("w2", W2, H1), ("h1", H1, H2), ("h2", H2, W3), ("w3", W3, WEIGHTS))]
            with ExitStack() as first:
                ffn_1_setup(nc, first, dram, sbuf, psum, loads)
            general = ffn_1(nc, part, dram, sbuf, psum, False)
            exact = ffn_1(nc, part, dram, sbuf, psum, True)
            with nc.Block() as block:
                def either(eng, name):
                    flag = eng.value_load(sbuf["exact_weights"][0:1, 0:1], min_val=0, max_val=1)
                    with eng.If(flag == 1):
                        exact[name](eng)
                    with eng.Else():
                        general[name](eng)

                @block.tensor
                def _(pe):
                    either(pe, "tensor")

                @block.scalar
                def _(act):
                    either(act, "scalar")

                @block.gpsimd
                def _(pool):
                    either(pool, "gpsimd")

                @block.vector
                def _(dve):
                    either(dve, "vector")
        out_stored = ctx.enter_context(nc.semaphore("out_stored"))
        with nc.Block() as block:
            @block.sync
            def _(sp):
                sp.dma_start(out_view, X[:, :, :]).then_inc(out_stored, 16)
                sp.wait_ge(out_stored, 16)


def kernel(**inputs):
    import concourse.bacc as bacc
    from concourse.bass_utils import run_bass_kernel_spmd

    a = {k: np.asarray(v) for k, v in inputs.items()}
    c = np.ascontiguousarray
    f32 = np.float32
    inv_freq = f32(1.0) / np.power(f32(10000.0), np.arange(0, HD, 2, dtype=f32) / f32(HD))
    angle = (np.arange(T, dtype=f32)[:, None] * inv_freq[None, :].astype(f32)).astype(f32)
    cos, sin = np.cos(angle).astype(f32), np.sin(angle).astype(f32)
    rope = np.stack([np.concatenate([cos, cos], 1), np.concatenate([-sin, sin], 1)])
    sel = np.zeros((P, H, P), f32)
    for head in range(H):
        sel[head, head] = sel[H + head, head] = 1.0
    order = [G * j + 2 * s + i for s in range(2) for j in range(G) for i in range(2)]
    def inputs_first(w):
        return c(w.T.reshape(-1, P, w.shape[0]).transpose(1, 0, 2).reshape(P, -1))

    def by_block(s):
        return s.reshape(KH, P).T

    w3_s = np.repeat(a["L1_ffn_w3_s"][:, None], KH, axis=1)
    arrays = {
        "w1": inputs_first(a["L1_ffn_w1_w"]), "w2": inputs_first(a["L1_ffn_w2_w"]), "h1": inputs_first(a["L1_ffn_h1_w"]),
        "h2": inputs_first(a["L1_ffn_h2_w"]), "w3": inputs_first(a["L1_ffn_w3_w"]),
        "scales": c(np.concatenate([by_block(a["L1_ffn_w1_s"]), by_block(a["L1_ffn_w2_s"]), by_block(a["L1_ffn_h1_s"]),
                                    by_block(a["L1_ffn_h2_s"]), w3_s], axis=1)),
        "wqk1": c(np.concatenate([a["L1_attn_Wq"], a["L1_attn_Wk"]], axis=1)), "wv1": c(a["L1_attn_Wv"]),
        "wo1": c(a["L1_attn_Wo"].reshape(H, HD, D)[order].reshape(D, D)),
        "bqk1": c(np.concatenate([a["L1_attn_bq"], a["L1_attn_bk"]])), "bv1": c(np.tile(a["L1_attn_bv"], TT)),
        "rope": c(rope.reshape(2, TT, P, HD).transpose(2, 0, 1, 3).reshape(P, 2 * TT * HD)),
        "sel": c(sel.reshape(P, H * P)),
        "x": c(a["L0_attn_x"]),
        "c0T": c(a["L0_c"].T), "c1T": c(a["L1_c"].T), "wmod0": c(a["L0_wmod"]), "wmod1": c(a["L1_wmod"]),
        "bo0": c(a["L0_attn_b_o"]), "bo1": c(a["L1_attn_bo"]),
        "wqk0": c(np.concatenate([a["L0_attn_w_q"], a["L0_attn_w_k"]], axis=1)),
        "wv0": c(a["L0_attn_w_v"]), "wo0": c(a["L0_attn_w_o"]),
        "gamma": c(a["L0_attn_gamma"][:, None]), "beta": c(a["L0_attn_beta"][:, None]),
        "gqk": c(np.concatenate([np.tile(a["L0_attn_g_q"], H), np.tile(a["L0_attn_g_k"], H)])),
        "ctrl": c(a["L0_ffn_controller"].reshape(D, SLOTS)), "f1": c(a["L0_ffn_f1"].reshape(D, SLOTS * NF)),
        "f2": c(a["L0_ffn_f2"].transpose(1, 2, 0, 3).reshape(NS_ * NF, NE, D)),
        "ebias": c(a["L0_ffn_bias"].transpose(1, 2, 0).reshape(NS_ * NF, NE)),
        "tie": (np.arange(GT, dtype=f32) * f32(1e-6 / (GT - 1))).astype(f32),
        "own": np.kron(np.eye(TG, dtype=f32), np.ones((GT, 1), f32)),
        "ident": np.eye(P, dtype=f32), "ident16": np.eye(P, dtype=np.float16),
    }
    nc = bacc.Bacc("TRN2", target_bir_lowering=False, num_devices=1)
    ins = {k: nc.dram_tensor(f"in_{k}", v.shape, mybir.dt.from_np(v.dtype), kind="ExternalInput").ap() for k, v in arrays.items()}
    out = nc.dram_tensor("out", a["L0_attn_x"].shape, F32, kind="ExternalOutput").ap()
    adaln_program(nc, ins, out)
    return run_bass_kernel_spmd(nc, [{f"in_{k}": v for k, v in arrays.items()}], core_ids=[0]).results[0]["out"]
```

```python
from contextlib import ExitStack

import numpy as np

import concourse.bass as bass
from concourse import mybir

F32 = mybir.dt.float32
F32R = mybir.dt.float32r
F16 = mybir.dt.float16
I32 = mybir.dt.int32
ALU = mybir.AluOpType
ACT = mybir.ActivationFunctionType
AX = mybir.AxisListType

P = 128
B = 32
T = 256
D = 128
TT = T // P
H = 16
HD = D // H
G = 4
MOD = 6 * D
LN_EPS = 1e-5
CHUNKS = 8
UNIT = 257
UNIT_PAD = 260

ROW_CA0, ROW_SA0, ROW_GA0, ROW_GABO0, ROW_CB0, ROW_SB0, ROW_GB0, ROW_GA1, ROW_GABO1 = range(9)
ROWS = 9
SA, CA, GA, SB, CB, GB = range(6)

NORM_FLOOR = 1e-24
SPLIT_SCALE = 64.0
COLLAPSE, SHARPNESS = 0.27, 15.0
RSQRT_MAGIC = float(0x5F3759DF)
RSQRT_STEPS = 11


def wait(eng, sem, n):
    if isinstance(n, int) and n <= 0:
        return
    eng.wait_ge(sem, n)


def stepped(eng, first, last, pair_first, pair_count, step):
    for b in range(first, pair_first):
        step(b, b % 2)
    with eng.Fori(0, pair_count) as i:
        step(i * 2 + pair_first, pair_first % 2)
        step(i * 2 + (pair_first + 1), (pair_first + 1) % 2)
    for b in range(pair_first + 2 * pair_count, last + 1):
        step(b, b % 2)


def setup_phase(nc, ctx, dram, sbuf, psum):
    def sem(name):
        return dram["semaphores"].enter_context(nc.semaphore(name))

    cond_loaded, wmod_loaded = sem("cond_loaded"), sem("wmod_loaded")
    weights_loaded, tanh_ready, silu_step = sem("weights_loaded"), sem("tanh_ready"), sem("silu_step")
    mod_psum, rows_step, rows_ready, table_stored = sem("mod_psum"), sem("rows_step"), sem("rows_ready"), sem("table_stored")
    cond = ctx.enter_context(nc.sbuf_tensor("cond", [P, 2, B], F32))
    cond_tanh = ctx.enter_context(nc.sbuf_tensor("cond_tanh", [P, 2, B], F32))
    cond_twice = ctx.enter_context(nc.sbuf_tensor("cond_twice", [P, 2, B], F32))
    cond_silu = ctx.enter_context(nc.sbuf_tensor("cond_silu", [P, 2, B], F32))
    wmod = ctx.enter_context(nc.sbuf_tensor("wmod", [P, 2, MOD], F32))
    bo_rows = ctx.enter_context(nc.sbuf_tensor("bo_rows", [B, 2, D], F32))
    rows = ctx.enter_context(nc.sbuf_tensor("rows", [B, ROWS, D], F32))
    sign = ctx.enter_context(nc.sbuf_tensor("sign", [B, 3, D], F32))
    size = ctx.enter_context(nc.sbuf_tensor("size", [B, 3, D], F32))
    minus = ctx.enter_context(nc.sbuf_tensor("minus", [B, 3, D], F32))
    col_minus = ctx.enter_context(nc.sbuf_tensor("col_minus", [P, B], F32))
    col_sign = ctx.enter_context(nc.sbuf_tensor("col_sign", [P, B], F32))
    col_size = ctx.enter_context(nc.sbuf_tensor("col_size", [P, B], F32))
    modcol = sbuf["modcol"]
    mod_ps = psum[0:B, 0:4 * 512].rearrange("b (l n) -> b l n", l=2)
    col_ps = psum[:, 4 * 512:4 * 512 + 5 * B].rearrange("p (j b) -> p j b", j=5)
    cols = [CA, SA, CB, SB, GB]

    with nc.Block() as block:
        @block.sync
        def _(sp):
            for layer in range(2):
                sp.dma_start(cond[:, layer, :], dram["condT"][layer]).then_inc(cond_loaded, 16)
            for layer in range(2):
                sp.dma_start(wmod[:, layer, :], dram["wmod"][layer]).then_inc(wmod_loaded, 16)
                sp.dma_start(bo_rows[:, layer, :], dram["bo"][layer].partition_broadcast(B)).then_inc(wmod_loaded, 16)
            for dst, src in dram["loads"]:
                sp.dma_start(dst, src).then_inc(weights_loaded, 16)
            sp.wait_ge(rows_ready, 1)
            sp.dma_start(dram["table"], rows[:, :, :]).then_inc(table_stored, 16)
            sp.wait_ge(table_stored, 16)
            sp.wait_ge(weights_loaded, 16 * len(dram["loads"]))

        @block.scalar
        def _(act):
            act.wait_ge(cond_loaded, 32)
            nc.scalar.activation(cond_tanh[:, :, :], cond[:, :, :], ACT.Tanh, scale=0.5).then_inc(tanh_ready, 1)

        @block.tensor
        def _(pe):
            pe.wait_ge(silu_step, 2)
            pe.wait_ge(wmod_loaded, 64)
            for layer in range(2):
                for n0, n in ((0, 512), (512, MOD - 512)):
                    nc.tensor.matmul(mod_ps[:, layer, n0:n0 + n], cond_silu[:, layer, :],
                                     wmod[:, layer, n0:n0 + n], start=True, stop=True)
            for j, part in enumerate(cols):
                last = nc.tensor.matmul(col_ps[:, j, :], wmod[:, 1, part * D:(part + 1) * D],
                                        cond_silu[:, 1, :], start=True, stop=True)
            last.then_inc(mod_psum, 1)

        @block.gpsimd
        def _(pool):
            for what, value in dram["fills"]:
                last = nc.gpsimd.memset(what, value)

        @block.vector
        def _(dve):
            dve.wait_ge(tanh_ready, 1)
            nc.vector.scalar_tensor_tensor(out=cond_twice[:, :, :], in0=cond_tanh[:, :, :], scalar=1.0,
                                           in1=cond[:, :, :], op0=ALU.add, op1=ALU.mult).then_inc(silu_step, 1)
            dve.wait_ge(silu_step, 1)
            nc.vector.tensor_scalar(cond_silu[:, :, :], cond_twice[:, :, :], 0.5, None, ALU.mult).then_inc(silu_step, 1)
            dve.wait_ge(mod_psum, 1)
            dve.wait_ge(wmod_loaded, 64)

            def part(layer, which):
                return mod_ps[:, layer, which * D:(which + 1) * D]

            gates = ((0, GA), (0, GB), (1, GA))
            for row, layer, which, plus in ((ROW_CA0, 0, CA, 1.0), (ROW_SA0, 0, SA, 0.0),
                                            (ROW_CB0, 0, CB, 1.0), (ROW_SB0, 0, SB, 0.0)):
                nc.vector.tensor_scalar(rows[:, row, :], part(layer, which), plus, None, ALU.add)
            for j, plus in ((0, 1.0), (1, 0.0), (2, 1.0), (3, 0.0)):
                nc.vector.tensor_scalar(modcol[:, j, :], col_ps[:, j, :], plus, None, ALU.add)
            for n, (layer, which) in enumerate(gates):
                nc.vector.tensor_scalar(sign[:, n, :], part(layer, which), 0.0, 2.0, ALU.is_ge, ALU.mult)
                nc.vector.tensor_scalar(minus[:, n, :], part(layer, which), -1.0, None, ALU.mult)
            nc.vector.tensor_scalar(col_sign[:, :], col_ps[:, 4, :], 0.0, 2.0, ALU.is_ge, ALU.mult)
            nc.vector.tensor_scalar(col_minus[:, :], col_ps[:, 4, :], -1.0, None, ALU.mult).then_inc(rows_step, 1)
            dve.wait_ge(rows_step, 1)
            for n, (layer, which) in enumerate(gates):
                nc.vector.scalar_tensor_tensor(out=size[:, n, :], in0=part(layer, which), scalar=0.25, in1=minus[:, n, :],
                                               op0=ALU.max, op1=ALU.max)
            nc.vector.scalar_tensor_tensor(out=col_size[:, :], in0=col_ps[:, 4, :], scalar=0.25, in1=col_minus[:, :],
                                           op0=ALU.max, op1=ALU.max).then_inc(rows_step, 1)
            dve.wait_ge(rows_step, 2)
            for n, row in enumerate((ROW_GA0, ROW_GB0, ROW_GA1)):
                nc.vector.scalar_tensor_tensor(out=rows[:, row, :], in0=sign[:, n, :], scalar=-1.0,
                                               in1=size[:, n, :], op0=ALU.add, op1=ALU.mult)
            nc.vector.scalar_tensor_tensor(out=modcol[:, 4, :], in0=col_sign[:, :], scalar=-1.0, in1=col_size[:, :],
                                           op0=ALU.add, op1=ALU.mult).then_inc(rows_step, 1)
            dve.wait_ge(rows_step, 3)
            nc.vector.tensor_tensor(rows[:, ROW_GABO0, :], rows[:, ROW_GA0, :], bo_rows[:, 0, :], ALU.mult)
            nc.vector.tensor_tensor(rows[:, ROW_GABO1, :], rows[:, ROW_GA1, :], bo_rows[:, 1, :],
                                    ALU.mult).then_inc(rows_ready, 1)


def attention_0(nc, ctx, dram, sbuf, psum):
    numbers = []

    def sem(name):
        s = ctx.enter_context(nc.semaphore("a0_" + name))
        numbers.append(s.num)
        return s

    def sb(name, shape, dt=F32):
        return ctx.enter_context(nc.sbuf_tensor("a0_" + name, shape, dt))

    X, ident, ident16 = sbuf["X"], sbuf["ident"], sbuf["ident16"]
    kmask, vpad, probs = sbuf["kmask"], sbuf["vpad"], sbuf["probs"]
    wqk, wv, wo, gammacol, betacol, gqk = (sbuf[k] for k in ("wqk0", "wv0", "wo0", "gamma", "beta", "gqk"))
    minus_half, eps, biases = sbuf["minus_half"], sbuf["eps"], sbuf["biases"]
    tanh_bias, gate_k_bias, gate_q_bias = (biases[:, i:i + 1] for i in range(3))

    mod_norm = [sb(f"mod_norm{i}", [P, 2, D]) for i in range(2)]
    mod_gate = [sb(f"mod_gate{i}", [P, 2, D]) for i in range(2)]
    stats1, stats2 = sb("stats1", [P, TT, 6]), sb("stats2", [P, TT, 6])
    moments1, moments2 = sb("moments1", [P, TT, 2]), sb("moments2", [P, TT, 2])
    vareps1, vareps2 = sb("vareps1", [P, TT]), sb("vareps2", [P, TT])
    rstd1, rstd2 = sb("rstd1", [P, TT]), sb("rstd2", [P, TT])
    xhat, scaled, h, xn = (sb(n, [P, TT, D]) for n in ("xhat", "scaled", "h", "xn"))
    hT, xnT = [sb(f"hT{i}", [P, T]) for i in range(2)], sb("xnT", [P, T])
    squares, qkn, qkg = sb("squares", [P, 64, HD]), sb("qkn", [P, 2, TT, D]), sb("qkg", [P, 2, TT, D])
    norm2, norm2c, seed_half, seed = (sb(n, [P, 64]) for n in ("norm2", "norm2c", "seed_half", "seed"))
    nw = [sb(f"newton{i}", [P, 64]) for i in range(7)]
    rnorm = sb("rnorm", [P, 64])
    gate_in, gate_tanh = sb("gate_in", [P, 64]), sb("gate_tanh", [P, 64])
    gate_k, gate_q = sb("gate_k", [P, TT * H]), sb("gate_q", [P, TT, D])
    qstack, kstack = sb("qstack", [P, TT * H, 4, HD], F16), sb("kstack", [P, TT * H, 4, HD], F16)
    qT = [sb(f"qT{i}", [P, G, T], F16) for i in range(2)]
    kT = sb("kT", [P, G, T], F16)
    gT = [sb(f"gT{i}", [P, T]) for i in range(2)]
    oT = sb("oT", [P, T])
    delta = sb("delta", [P, TT, D])

    SC = [psum[:, 1024 * i:1024 * (i + 1)] for i in range(2)]
    PO = psum[:, 2048:2048 + UNIT]
    PT, PQ = psum[:, 2560:3072], psum[:, 3072:3584]
    PV, PP = psum[:, 3584:3840], psum[:, 3840:4096]
    PT16, PQ16 = PT.bitcast(F16), PQ.bitcast(F16)

    x_loaded, mod_norm_loaded, k_spread = map(sem, ("x_loaded", "mod_norm_loaded", "k_spread"))
    mod_gate_loaded = [sem(f"mod_gate_loaded{i}") for i in range(2)]
    stats1_done, moments1_done, vareps1_done, rstd1_done, xhat_done = map(sem, ("stats1", "moments1", "vareps1", "rstd1", "xhat"))
    scaled_done, h_done = sem("scaled"), sem("h")
    stats2_done, moments2_done, vareps2_done, rstd2_done, xn_done = map(sem, ("stats2", "moments2", "vareps2", "rstd2", "xn"))
    turned, hT_done, xnT_done, qk_psum, v_psum = map(sem, ("turned", "hT", "xnT", "qk_psum", "v_psum"))
    squares_done, norm2_done, newton, qkn_done, qkg_done = map(sem, ("squares", "norm2", "newton", "qkn", "qkg"))
    gate_in_done, gate_tanh_done, gates_done, values_done = map(sem, ("gate_in", "gate_tanh", "gates", "values"))
    hi_done, stacks_done, qT_done, kT_done, gT_done = map(sem, ("hi", "stacks", "qT", "kT", "gT"))
    kstack_psum, qstack_psum, gates_psum = map(sem, ("kstack_psum", "qstack_psum", "gates_psum"))
    scores_ready, probs_ready, heads_done = map(sem, ("scores_ready", "probs_ready", "heads_done"))
    oT_done, projected, delta_done, x_biased, x_done = map(sem, ("oT", "projected", "delta", "x_biased", "x_done"))

    vdiag = [bass.AP(tensor=v[:, :, :, :].tensor, offset=v[:, :, :, :].offset,
                     ap=[[TT * H * 32, P], [P, TT * G], [32 + HD, G], [1, HD]]) for v in vpad]

    def tiles(b):
        return X[:, bass.ds(b * TT, TT), :] if not isinstance(b, int) else X[:, b * TT:(b + 1) * TT, :]

    def tile(b, t):
        return X[:, bass.ds(b * TT + t, 1), :] if not isinstance(b, int) else X[:, b * TT + t:b * TT + t + 1, :]

    def rows_of(b, row, n):
        src = dram["table"]
        src = src[bass.ds(b, 1), row:row + n, :] if not isinstance(b, int) else src[b:b + 1, row:row + n, :]
        return src.rearrange("o r d -> (o r d)").partition_broadcast(P)

    def x_rows(b):
        src = dram["x"]
        return src[:, bass.ds(b * TT, TT), :] if not isinstance(b, int) else src[:, b * TT:(b + 1) * TT, :]

    def is_last(b, back=0):
        return isinstance(b, int) and b >= B - back

    with nc.Block() as block:
        @block.sync
        def _(sp):
            def load(n, p):
                wait(sp, h_done, n - 1)
                wait(sp, mod_norm_loaded, n * 16)
                sp.dma_start(mod_norm[p][:, :, :], rows_of(n, ROW_CA0, 2)).then_inc(mod_norm_loaded, 16)
                wait(sp, x_loaded, n * 16)
                sp.dma_start(tiles(n), x_rows(n)).then_inc(x_loaded, 16)

            def load_gate(n, p):
                wait(sp, x_done, n - 1)
                sp.dma_start(mod_gate[p][:, :, :], rows_of(n, ROW_GA0, 2)).then_inc(mod_gate_loaded[p], 16)

            def spread(n, p):
                sp.wait_ge(kT_done, n + 1)
                wait(sp, scores_ready, n * CHUNKS - CHUNKS)
                for r in range(G):
                    sp.dma_start(kmask[p][32 * r:32 * r + 32, r:H:G, :], kT[32 * r:32 * r + 32, :, :]).then_inc(k_spread, 16)

            def step(b, p):
                if not is_last(b, 4):
                    load(b + 4, p)
                if not is_last(b, 1):
                    spread(b + 1, 1 - p)
                    load_gate(b + 1, 1 - p)

            load(0, 0)
            load(1, 1)
            load_gate(0, 0)
            load(2, 0)
            spread(0, 0)
            load(3, 1)
            for dst, src in dram["experts_loads"]:
                sp.dma_start(dst, src).then_inc(dram["experts_loaded"], 16)
            stepped(sp, 0, B - 1, 1, 13, step)

        @block.tensor
        def _(pe):
            def turn(n):
                pe.wait_ge(h_done, n + 1)
                pe.wait_ge(xn_done, n + 1)
                wait(pe, qT_done, n - 1)
                for i, src in enumerate((h, xn)):
                    for t in range(TT):
                        last = nc.tensor.transpose(PT[:, (i * TT + t) * P:(i * TT + t + 1) * P], src[:, t, :], ident[:, :])
                last.then_inc(turned, 1)

            def project_qk(n):
                pe.wait_ge(xnT_done, n + 1)
                wait(pe, kT_done, n)
                for t in range(TT):
                    last = nc.tensor.matmul(PQ[:, t * 2 * D:(t + 1) * 2 * D], xnT[:, t * P:(t + 1) * P], wqk[:, :], start=True, stop=True)
                last.then_inc(qk_psum, 1)

            def project_v(n, p):
                pe.wait_ge(hT_done, n + 1)
                wait(pe, gT_done, n)
                wait(pe, delta_done, n - 2)
                for t in range(TT):
                    last = nc.tensor.matmul(PV[:, t * D:(t + 1) * D], hT[p][:, t * P:(t + 1) * P], wv[:, :], start=True, stop=True)
                last.then_inc(v_psum, 1)

            def turn_stack(n, dst, src, done):
                pe.wait_ge(stacks_done, n + 1)
                if done is qstack_psum:
                    pe.wait_ge(xnT_done, n + 2 if not is_last(n, 1) else B)
                for t in range(TT):
                    for g in range(G):
                        last = nc.tensor.transpose(dst[:, g * T + t * P:g * T + (t + 1) * P],
                                                   src[:, t * H + G * g:t * H + G * (g + 1), :, :].rearrange("p h s d -> p (h s d)"),
                                                   ident16[:, :])
                last.then_inc(done, 1)

            def turn_gates(n):
                pe.wait_ge(values_done, n + 1)
                pe.wait_ge(gates_done, n + 1)
                for t in range(TT):
                    last = nc.tensor.transpose(PV[:, t * P:(t + 1) * P], gate_q[:, t, :], ident[:, :])
                last.then_inc(gates_psum, 1)

            def scores(b, p, c):
                r, kb = c // TT, c % TT
                if c == 0:
                    pe.wait_ge(k_spread, b * (16 * G) + 16 * G)
                    pe.wait_ge(qT_done, b + 1)
                wait(pe, probs_ready, b * CHUNKS + (c - 1))
                for g in range(G):
                    last = nc.tensor.matmul(SC[c % 2][:, g * T:(g + 1) * T], kmask[p][:, G * g + r, kb * P:(kb + 1) * P],
                                            qT[p][:, g, :], start=True, stop=True)
                last.then_inc(scores_ready, 1)

            def heads(b, p, c):
                r, kb = c // TT, c % TT
                if c == 0:
                    wait(pe, oT_done, b)
                    pe.wait_ge(values_done, b + 1)
                pe.wait_ge(probs_ready, b * CHUNKS + (c + 1))
                for g in range(G):
                    last = nc.tensor.matmul(PO[32 * g:32 * g + 32, :], vpad[p][:, kb, G * g + r, :],
                                            probs[:, c % 4, g, 0:UNIT], start=(c == 0), stop=(c == CHUNKS - 1))
                last.then_inc(heads_done, 1)

            def project_out(n):
                pe.wait_ge(oT_done, n + 1)
                pe.wait_ge(gT_done, n + 3 if not is_last(n, 2) else B)
                wait(pe, delta_done, n)
                for t in range(TT):
                    last = nc.tensor.matmul(PP[:, t * D:(t + 1) * D], oT[:, t * P:(t + 1) * P], wo[:, :], start=True, stop=True)
                last.then_inc(projected, 1)

            def step(b, p):
                first, more, projects = isinstance(b, int) and b == 0, not is_last(b, 1), not is_last(b, 2)
                for c in range(CHUNKS):
                    scores(b, p, c)
                    if c < 2 and not first:
                        heads(b - 1, 1 - p, c + CHUNKS - 2)
                    if c >= 2:
                        heads(b, p, c - 2)
                    if c == 0 and projects:
                        turn(b + 2)
                    if c == 0 and more:
                        turn_stack(b + 1, PQ16, kstack, kstack_psum)
                    if c == 1 and more:
                        turn_stack(b + 1, PT16, qstack, qstack_psum)
                    if c == 1 and projects:
                        project_qk(b + 2)
                    if c == 2 and more:
                        project_v(b + 1, 1 - p)
                    if c == 5 and more:
                        turn_gates(b + 1)
                    if c == 6 and not first:
                        project_out(b - 1)

            turn(0)
            project_qk(0)
            turn(1)
            turn_stack(0, PQ16, kstack, kstack_psum)
            turn_stack(0, PT16, qstack, qstack_psum)
            project_v(0, 0)
            project_qk(1)
            turn_gates(0)
            stepped(pe, 0, B - 1, 1, 13, step)
            for c in (CHUNKS - 2, CHUNKS - 1):
                heads(B - 1, 1, c)
            project_out(B - 1)

        @block.scalar
        def _(act):
            def square(n):
                act.wait_ge(qk_psum, n + 1)
                wait(act, norm2_done, n)
                nc.scalar.activation(squares[:, :, :].rearrange("p a d -> p (a d)"), PQ, ACT.Square).then_inc(squares_done, 1)

            def gate(n):
                act.wait_ge(gate_in_done, n + 1)
                wait(act, gates_done, n)
                nc.scalar.activation(gate_tanh[:, :], gate_in[:, :], ACT.Tanh, scale=0.5 / SPLIT_SCALE).then_inc(gate_tanh_done, 1)
                wait(act, gates_psum, n)
                wait(act, values_done, n)
                act.wait_ge(gate_tanh_done, n + 1)
                nc.scalar.activation(gate_q[:, :, :].rearrange("p t (h d) -> p (t h) d", d=HD),
                                     gate_tanh[:, 0:32].unsqueeze(2).broadcast_to([P, TT * H, HD]),
                                     ACT.Identity, bias=gate_q_bias, scale=0.1875)
                nc.scalar.activation(gate_k[:, :], gate_tanh[:, 32:64], ACT.Identity,
                                     bias=gate_k_bias, scale=0.375).then_inc(gates_done, 1)

            def gT_out(n, p):
                act.wait_ge(gates_psum, n + 1)
                wait(act, oT_done, n - 1)
                nc.scalar.copy(gT[p][:, :], PV).then_inc(gT_done, 1)

            def prob(b, c):
                act.wait_ge(scores_ready, b * CHUNKS + (c + 1))
                wait(act, heads_done, b * CHUNKS + (c - 3))
                nc.scalar.activation(probs[:, c % 4, :, 0:T], SC[c % 2].rearrange("p (g q) -> p g q", g=G), ACT.Tanh,
                                     bias=tanh_bias, scale=SHARPNESS / SPLIT_SCALE ** 2).then_inc(probs_ready, 1)

            def step(b, p):
                more, projects = not is_last(b, 1), not is_last(b, 2)
                for c in range(CHUNKS):
                    prob(b, c)
                    if c == 1 and projects:
                        square(b + 2)
                    if c == 1 and more:
                        gate(b + 1)
                    if c == 5 and more:
                        gT_out(b + 1, 1 - p)

            square(0)
            gate(0)
            gT_out(0, 0)
            square(1)
            stepped(act, 0, B - 1, 1, 13, step)

        @block.gpsimd
        def _(pool):
            def rstd(n, moments, vareps, out, moments_done, vareps_done, out_done, used):
                wait(pool, out_done, n)
                pool.wait_ge(moments_done, n + 1)
                nc.gpsimd.tensor_tensor(vareps[:, :], moments[:, :, 1], eps[:, 0:TT], ALU.add).then_inc(vareps_done, 1)
                pool.wait_ge(vareps_done, n + 1)
                wait(pool, used, n)
                nc.gpsimd.tensor_tensor(out[:, :], vareps[:, :], minus_half[:, 0:TT], ALU.pow).then_inc(out_done, 1)

            def modulate(n, p):
                pool.wait_ge(xhat_done, n + 1)
                pool.wait_ge(mod_norm_loaded, n * 16 + 16)
                wait(pool, h_done, n)
                nc.gpsimd.tensor_tensor(scaled[:, :, :], xhat[:, :, :],
                                        mod_norm[p][:, 0:1, :].broadcast_to([P, TT, D]), ALU.mult).then_inc(scaled_done, 1)
                pool.wait_ge(scaled_done, n + 1)
                wait(pool, turned, n)
                nc.gpsimd.tensor_tensor(h[:, :, :], scaled[:, :, :],
                                        mod_norm[p][:, 1:2, :].broadcast_to([P, TT, D]), ALU.add).then_inc(h_done, 1)

            def norm_1(n):
                rstd(n, moments1, vareps1, rstd1, moments1_done, vareps1_done, rstd1_done, xhat_done)

            def norm_2(n):
                rstd(n, moments2, vareps2, rstd2, moments2_done, vareps2_done, rstd2_done, xn_done)

            def gate_products(n):
                pool.wait_ge(qkn_done, n + 1)
                wait(pool, gate_in_done, n)
                nc.gpsimd.tensor_tensor(qkg[:, :, :, :], qkn[:, :, :, :],
                                        gqk[:, :, :].unsqueeze(2).broadcast_to([P, 2, TT, D]), ALU.mult).then_inc(qkg_done, 1)

            def bias_x(n, p):
                pool.wait_ge(mod_gate_loaded[p], n * 8 + (16 - 8 * p))
                pool.wait_ge(xhat_done, n + 1)
                nc.gpsimd.tensor_tensor(tiles(n), tiles(n), mod_gate[p][:, 1:2, :].broadcast_to([P, TT, D]),
                                        ALU.add).then_inc(x_biased, 1)

            def step(b, p):
                norms = not is_last(b, 3)
                if norms:
                    norm_1(b + 3)
                    modulate(b + 3, 1 - p)
                bias_x(b, p)
                if norms:
                    norm_2(b + 3)
                if not is_last(b, 2):
                    gate_products(b + 2)

            norm_1(0)
            modulate(0, 0)
            norm_2(0)
            norm_1(1)
            modulate(1, 1)
            gate_products(0)
            norm_2(1)
            norm_1(2)
            modulate(2, 0)
            norm_2(2)
            gate_products(1)
            stepped(pool, 0, B - 1, 1, 13, step)

        @block.vector
        def _(dve):
            def moments(n, src, stats, out, stats_done, out_done, read_done):
                wait(dve, out_done, n)
                for t in range(TT):
                    last = nc.vector.bn_stats(stats[:, t, :], src(t))
                last.then_inc(stats_done, 1)
                wait(dve, read_done, n)
                dve.wait_ge(stats_done, n + 1)
                nc.vector.memset(unread[:, :], 0.0)
                for t in range(TT):
                    last = nc.vector.bn_aggr(out[:, t, :], stats[:, t, :])
                last.then_inc(out_done, 1)

            def standardise(n, src, dst, mom, rstd, rstd_done, done):
                dve.wait_ge(rstd_done, n + 1)
                for t in range(TT):
                    last = nc.vector.tensor_scalar(dst[:, t, :], src(t), mom[:, t, 0:1], rstd[:, t:t + 1], ALU.subtract, ALU.mult)
                last.then_inc(done, 1)

            def norm_1a(n):
                dve.wait_ge(x_loaded, n * 16 + 16)
                moments(n, lambda t: tile(n, t)[:, 0, :], stats1, moments1, stats1_done, moments1_done, xhat_done)

            def norm_1b(n):
                wait(dve, scaled_done, n)
                standardise(n, lambda t: tile(n, t)[:, 0, :], xhat, moments1, rstd1, rstd1_done, xhat_done)

            def norm_2a(n):
                dve.wait_ge(h_done, n + 1)
                moments(n, lambda t: h[:, t, :], stats2, moments2, stats2_done, moments2_done, xn_done)

            def norm_2b(n):
                wait(dve, turned, n)
                standardise(n, lambda t: h[:, t, :], xn, moments2, rstd2, rstd2_done, xn_done)

            def turned_out(n, p):
                dve.wait_ge(turned, n + 1)
                wait(dve, qk_psum, n)
                wait(dve, v_psum, n - 1)
                nc.vector.tensor_copy(hT[p][:, :], PT[:, 0:T]).then_inc(hT_done, 1)
                nc.vector.tensor_scalar(xnT[:, :], PT[:, T:2 * T], gammacol[:, :], betacol[:, :], ALU.mult, ALU.add).then_inc(xnT_done, 1)

            def unit_vectors(n):
                def then(ins, k):
                    ins.then_inc(newton, 1)
                    dve.wait_ge(newton, n * RSQRT_STEPS + k)

                dve.wait_ge(squares_done, n + 1)
                nc.vector.tensor_reduce(norm2[:, :], squares[:, :, :], AX.X, ALU.add).then_inc(norm2_done, 1)
                dve.wait_ge(norm2_done, n + 1)
                then(nc.vector.tensor_scalar(norm2c[:, :], norm2[:, :], NORM_FLOOR, SPLIT_SCALE ** -2, ALU.max, ALU.mult), 1)
                then(nc.vector.tensor_scalar(seed_half[:, :].bitcast(I32), norm2c[:, :].bitcast(I32), 1, None,
                                             ALU.logical_shift_right), 2)
                then(nc.vector.tensor_scalar(seed[:, :].bitcast(I32), seed_half[:, :].bitcast(I32), -1.0, RSQRT_MAGIC,
                                             ALU.mult, ALU.add), 3)
                then(nc.vector.tensor_tensor(nw[0][:, :], seed[:, :], seed[:, :], ALU.mult), 4)
                then(nc.vector.tensor_tensor(nw[1][:, :], nw[0][:, :], norm2c[:, :], ALU.mult), 5)
                then(nc.vector.tensor_scalar(nw[2][:, :], nw[1][:, :], 0.375, -1.25, ALU.mult, ALU.add), 6)
                then(nc.vector.tensor_tensor(nw[3][:, :], nw[2][:, :], nw[1][:, :], ALU.mult), 7)
                then(nc.vector.scalar_tensor_tensor(out=nw[4][:, :], in0=nw[3][:, :], scalar=1.875, in1=seed[:, :],
                                                    op0=ALU.add, op1=ALU.mult), 8)
                then(nc.vector.tensor_tensor(nw[5][:, :], nw[4][:, :], nw[4][:, :], ALU.mult), 9)
                then(nc.vector.scalar_tensor_tensor(out=nw[6][:, :], in0=nw[5][:, :], scalar=-0.5, in1=norm2c[:, :],
                                                    op0=ALU.mult, op1=ALU.mult), 10)
                nc.vector.scalar_tensor_tensor(out=rnorm[:, :], in0=nw[6][:, :], scalar=1.5, in1=nw[4][:, :],
                                               op0=ALU.add, op1=ALU.mult).then_inc(newton, 1)

            def scale(n):
                dve.wait_ge(newton, n * RSQRT_STEPS + RSQRT_STEPS)
                wait(dve, qkg_done, n)
                nc.vector.tensor_tensor(qkn[:, :, :, :].rearrange("p k t (h d) -> p t k h d", d=HD),
                                        PQ.rearrange("p (t k h d) -> p t k h d", t=TT, k=2, d=HD),
                                        rnorm[:, :].rearrange("p (t k h) -> p t k h", t=TT, k=2).unsqueeze(4).broadcast_to([P, TT, 2, H, HD]),
                                        ALU.mult).then_inc(qkn_done, 1)

            def twice(i):
                return qkn[:, i, :, :].rearrange("p t (h d) -> p (t h) d", d=HD).unsqueeze(2).broadcast_to([P, TT * H, 2, HD])

            def split_high(n):
                dve.wait_ge(qkn_done, n + 1)
                wait(dve, qstack_psum, n)

                nc.vector.tensor_copy(qstack[:, :, 0:4:2, :], twice(0))
                nc.vector.tensor_copy(kstack[:, :, 0:2, :], twice(1)).then_inc(hi_done, 1)

            def split_low(n):
                dve.wait_ge(hi_done, n + 1)
                nc.vector.tensor_tensor(qstack[:, :, 1:4:2, :], twice(0), qstack[:, :, 0:4:2, :], ALU.subtract)
                nc.vector.tensor_tensor(kstack[:, :, 2:4, :], twice(1), kstack[:, :, 0:2, :], ALU.subtract).then_inc(stacks_done, 1)

            def gate_sums(n):
                dve.wait_ge(qkg_done, n + 1)
                wait(dve, gate_tanh_done, n)
                nc.vector.tensor_reduce(gate_in[:, :], qkg[:, :, :, :].rearrange("p k t (h d) -> p (k t h) d", d=HD),
                                        AX.X, ALU.add).then_inc(gate_in_done, 1)

            def values(n, p):
                dve.wait_ge(v_psum, n + 1)
                dve.wait_ge(gates_done, n + 1)
                wait(dve, heads_done, n * CHUNKS - CHUNKS)
                nc.vector.tensor_tensor(vdiag[p], PV.rearrange("p (a r d) -> p a r d", r=G, d=HD),
                                        gate_k[:, :].rearrange("p (a r) -> p a r", r=G).unsqueeze(3).broadcast_to([P, TT * G, G, HD]),
                                        ALU.mult).then_inc(values_done, 1)

            def keys_out(n):
                dve.wait_ge(kstack_psum, n + 1)
                wait(dve, k_spread, n * (16 * G))
                nc.vector.tensor_copy(kT[:, :, :].rearrange("p g k -> p (g k)"), PQ16).then_inc(kT_done, 1)

            def queries_out(n, p):
                dve.wait_ge(qstack_psum, n + 1)
                wait(dve, scores_ready, n * CHUNKS - CHUNKS)
                nc.vector.tensor_copy(qT[p][:, :, :].rearrange("p g k -> p (g k)"), PT16).then_inc(qT_done, 1)

            def heads_out(n, p):
                dve.wait_ge(heads_done, n * CHUNKS + CHUNKS)
                dve.wait_ge(gT_done, n + 1)
                wait(dve, projected, n)
                nc.vector.tensor_copy(vsum[:, :], PO[:, T:UNIT]).then_inc(vsum_done, 1)
                dve.wait_ge(vsum_done, n + 1)
                nc.vector.scalar_tensor_tensor(out=oT[:, :], in0=PO[:, 0:T], scalar=vsum[:, :], in1=gT[p][:, :],
                                               op0=ALU.add, op1=ALU.mult).then_inc(oT_done, 1)

            def residual(n, p):
                dve.wait_ge(projected, n + 1)
                wait(dve, x_done, n)
                dve.wait_ge(mod_gate_loaded[p], n * 8 + (16 - 8 * p))
                nc.vector.tensor_tensor(delta[:, :, :], PP.rearrange("p (t d) -> p t d", t=TT),
                                        mod_gate[p][:, 0:1, :].broadcast_to([P, TT, D]), ALU.mult).then_inc(delta_done, 1)
                dve.wait_ge(delta_done, n + 1)
                dve.wait_ge(x_biased, n + 1)
                nc.vector.tensor_tensor(tiles(n), tiles(n), delta[:, :, :], ALU.add).then_inc(x_done, 1)

            def step(b, p):
                first, more, projects = isinstance(b, int) and b == 0, not is_last(b, 1), not is_last(b, 2)
                norms = not is_last(b, 3)
                if projects:
                    turned_out(b + 2, p)
                if more:
                    keys_out(b + 1)
                if norms:
                    norm_1a(b + 3)
                if more:
                    queries_out(b + 1, 1 - p)
                if not first:
                    heads_out(b - 1, 1 - p)
                if norms:
                    norm_1b(b + 3)
                if projects:
                    unit_vectors(b + 2)
                if norms:
                    norm_2a(b + 3)
                if more:
                    values(b + 1, 1 - p)
                if projects:
                    scale(b + 2)
                if projects:
                    split_high(b + 2)
                if norms:
                    norm_2b(b + 3)
                if projects:
                    split_low(b + 2)
                if not first:
                    residual(b - 1, 1 - p)
                if projects:
                    gate_sums(b + 2)

            unread = sb("unread", [P, 1])
            vsum, vsum_done = sb("vsum", [P, 1]), sem("vsum")
            norm_1a(0)
            norm_1b(0)
            norm_2a(0)
            norm_2b(0)
            turned_out(0, 0)
            norm_1a(1)
            norm_1b(1)
            unit_vectors(0)
            scale(0)
            norm_2a(1)
            split_high(0)
            split_low(0)
            norm_2b(1)
            gate_sums(0)
            turned_out(1, 1)
            keys_out(0)
            norm_1a(2)
            queries_out(0, 0)
            values(0, 0)
            norm_1b(2)
            unit_vectors(1)
            scale(1)
            norm_2a(2)
            split_high(1)
            split_low(1)
            norm_2b(2)
            gate_sums(1)
            stepped(dve, 0, B - 1, 1, 13, step)
            heads_out(B - 1, 1)
            residual(B - 1, 1)

    assert sorted(numbers) == list(range(min(numbers), max(numbers) + 1))
    with nc.Block() as block:
        @block.gpsimd
        def _(pool):
            pool.sem_clear(range(min(numbers), max(numbers) + 1))


GT = 32
NE, NS_, NF = 32, 4, 32
SLOTS = NE * NS_
CB_ = 8
NCHUNK = B // CB_
CG = CB_ * T // GT
TG = P // GT
EB = 512 // CG
ROUNDS = NE // EB
HB = 4


def experts_0(nc, ctx, dram, sbuf, psum):
    def sem(name):
        return dram["semaphores"].enter_context(nc.semaphore("e_" + name))

    def sb(name, shape, dt=F32):
        return ctx.enter_context(nc.sbuf_tensor("e_" + name, shape, dt))

    X, ident, minus_half, eps = (sbuf[k] for k in ("X", "ident", "minus_half", "eps"))
    ctrl, f1, f2, bias, tie, own = sbuf["experts"]
    mod_norm = [sb(f"mod_norm{i}", [P, 2, D]) for i in range(2)]
    gates = sb("gates", [P, CB_, D])
    stats, moments = sb("stats", [P, TT, 6]), sb("moments", [P, TT, 2])
    vareps, rstd = sb("vareps", [P, TT]), sb("rstd", [P, TT])
    xhat, scaled = sb("xhat", [P, TT, D]), sb("scaled", [P, TT, D])
    h = [sb(f"h{i}", [P, TT, D]) for i in range(HB)]
    hT = sb("hT", [P, T])
    logits, best = sb("logits", [P, T]), sb("best", [P, T // GT])
    takenT = sb("takenT", [P, CB_, T])
    taken = sb("taken", [P, TT, TG, SLOTS])
    sent = sb("sent", [P, SLOTS, CG])
    inner = sb("inner", [P, EB, CG])
    relued = [sb(f"relued{i}", [P, EB, NS_, CG]) for i in range(2)]
    given = sb("given", [P, CG, SLOTS])
    givenT = [sb(f"givenT{i}", [P, TG, D]) for i in range(2)]
    delta = sb("delta", [P, TT, D])
    unread = sb("unread", [P, 1])

    bank = [psum[:, 512 * i:512 * (i + 1)] for i in range(8)]

    w_loaded, mod_loaded, gates_loaded = dram["experts_loaded"], sem("mod_loaded"), sem("gates_loaded")
    stats_done, moments_done, vareps_done, rstd_done, xhat_done, scaled_done, h_done = map(
        sem, ("stats", "moments", "vareps", "rstd", "xhat", "scaled", "h"))
    turned, hT_done, logits_psum, logits_done, best_done, takenT_done = map(
        sem, ("turned", "hT", "logits_psum", "logits", "best", "takenT"))
    taken_psum, taken_done, sent_psum, sent_done = map(sem, ("taken_psum", "taken", "sent_psum", "sent"))
    inner_psum, inner_done, relued_dve, relued_act = map(sem, ("inner_psum", "inner", "relued_dve", "relued_act"))
    given_psum, given_dve, given_act = map(sem, ("given_psum", "given_dve", "given_act"))
    turned_back, givenT_dve, givenT_act, out_psum, delta_done, x_done = map(
        sem, ("turned_back", "givenT_dve", "givenT_act", "out_psum", "delta", "x_done"))

    GB_, TB_ = NE // 2, CB_ * TT

    def is_last(c):
        return isinstance(c, int) and c == NCHUNK - 1

    def tiles(c, j):
        return X[:, bass.ds(c * (CB_ * TT) + j * TT, TT), :]

    def tile(c, j, t):
        return X[:, bass.ds(c * (CB_ * TT) + (j * TT + t), 1), :][:, 0, :]

    def rows_of(c, j, row, n):
        return dram["table"][bass.ds(c * CB_ + j, 1), row:row + n, :].rearrange("o r d -> (o r d)").partition_broadcast(P)

    with nc.Block() as block:
        @block.sync
        def _(sp):
            def load(c, j):
                wait(sp, mod_loaded, c * (16 * CB_) + 16 * j)
                wait(sp, h_done, c * CB_ + (j - 1))
                sp.dma_start(mod_norm[j % 2][:, :, :], rows_of(c, j, ROW_CB0, 2)).then_inc(mod_loaded, 16)

            def chunk(c):
                for j in range(2, CB_):
                    load(c, j)
                wait(sp, delta_done, c * CB_)
                for j in range(CB_):
                    sp.dma_start(gates[:, j, :], rows_of(c, j, ROW_GB0, 1)).then_inc(gates_loaded, 16)
                if not is_last(c):
                    load(c, CB_)
                    load(c, CB_ + 1)

            load(0, 0)
            load(0, 1)
            chunk(0)
            with sp.Fori(1, NCHUNK - 1) as c:
                chunk(c)
            chunk(NCHUNK - 1)

        @block.tensor
        def _(pe):
            def turn(c, j):
                wait(pe, h_done, c * CB_ + (j + 1))
                wait(pe, hT_done, c * CB_ + j)
                for t in range(TT):
                    last = nc.tensor.transpose(bank[0][:, t * P:(t + 1) * P], h[j % HB][:, t, :], ident[:, :])
                last.then_inc(turned, 1)

            def score(c, j):
                wait(pe, hT_done, c * CB_ + (j + 1))
                wait(pe, logits_done, c * CB_ + j)
                nc.tensor.matmul(bank[1][:, 0:T], ctrl[:, :], hT[:, :], start=True, stop=True).then_inc(logits_psum, 1)

            def turn_taken(c, j):
                wait(pe, takenT_done, c * CB_ + (j + 1))
                wait(pe, taken_done, c * CB_ + j)
                for t in range(TT):
                    last = nc.tensor.transpose(bank[2][:, t * P:(t + 1) * P], takenT[:, j, t * P:(t + 1) * P], ident[:, :])
                last.then_inc(taken_psum, 1)

            def send(c, j):
                wait(pe, taken_done, c * CB_ + (j + 1))
                wait(pe, sent_done, c * CB_ + j)
                for t in range(TT):
                    last = nc.tensor.matmul(bank[3 + t], h[j % HB][:, t, :], taken[:, t, :, :].rearrange("p g s -> p (g s)"),
                                            start=True, stop=True)
                last.then_inc(sent_psum, 1)

            def first_matrices(c, r):
                wait(pe, sent_done, c * CB_ + CB_)
                for e in range(EB):
                    for s in range(NS_):
                        slot = (r * EB + e) * NS_ + s
                        last = nc.tensor.matmul(bank[r][NF * s:NF * (s + 1), e * CG:(e + 1) * CG], f1[:, slot, :],
                                                sent[:, slot, :], start=True, stop=True)
                last.then_inc(inner_psum, 1)

            def second_matrices(c, r):
                wait(pe, relued_dve, c * ROUNDS + (r + 1))
                wait(pe, relued_act, c * ROUNDS + (r + 1))
                for pair in range(EB // 2):
                    n = r * (EB // 2) + pair
                    if n >= 4:
                        wait(pe, (given_dve, given_act)[n % 2], c * (GB_ // 2) + (n // 2 - 1))
                    for i in range(2):
                        e = 2 * pair + i
                        last = nc.tensor.matmul(bank[4 + n % 4][:, i * NS_ * CG:(i + 1) * NS_ * CG], f2[:, r * EB + e, :],
                                                relued[r % 2][:, e, :, :].rearrange("p s g -> p (s g)"), start=True, stop=True)
                    last.then_inc(given_psum, 1)

            def turn_back(c, q):
                wait(pe, given_dve, c * (GB_ // 2) + GB_ // 2)
                wait(pe, given_act, c * (GB_ // 2) + GB_ // 2)
                if q >= 2:
                    wait(pe, (givenT_dve, givenT_act)[q % 2], c * (TB_ // 2) + q // 2)
                for g in range(TG):
                    last = nc.tensor.transpose(bank[q % 2][:, g * P:(g + 1) * P], given[:, q * TG + g, :], ident[:, :])
                last.then_inc(turned_back, 1)

            def hand_back(c, q):
                j, t = q // TT, q % TT
                wait(pe, (givenT_dve, givenT_act)[q % 2], c * (TB_ // 2) + (q // 2 + 1))
                if t == 0 and j >= 2:
                    wait(pe, delta_done, c * CB_ + (j - 1))
                for g in range(TG):
                    last = nc.tensor.matmul(bank[4 + j % 2][GT * g:GT * (g + 1), t * D:(t + 1) * D],
                                            takenT[:, j, t * P + GT * g:t * P + GT * (g + 1)], givenT[q % 2][:, g, :],
                                            start=True, stop=True)
                last.then_inc(out_psum, 1)

            wait(pe, w_loaded, 16 * len(dram["experts_loads"]))
            def chunk(c):
                wait(pe, delta_done, c * CB_)
                for k in range(CB_ + 2):
                    if k < CB_:
                        turn(c, k)
                    if k < CB_:
                        score(c, k)
                    if 0 <= k - 1 < CB_:
                        turn_taken(c, k - 1)
                    if k >= 2:
                        send(c, k - 2)
                first_matrices(c, 0)
                first_matrices(c, 1)
                for r in range(ROUNDS):
                    if r + 2 < ROUNDS:
                        first_matrices(c, r + 2)
                    second_matrices(c, r)
                turn_back(c, 0)
                for q in range(TB_):
                    if q + 1 < TB_:
                        turn_back(c, q + 1)
                    hand_back(c, q)

            chunk(0)
            with pe.Fori(1, NCHUNK - 1) as c:
                chunk(c)
            chunk(NCHUNK - 1)

        def results_out(eng, copy, done, c, n):
            wait(eng, given_psum, c * GB_ + (n + 1))
            copy(given[:, :, 2 * NS_ * n:2 * NS_ * (n + 1)], bank[4 + n % 4].rearrange("p (s g) -> p g s", g=CG)).then_inc(done, 1)

        def turned_out(eng, copy, done, c, q):
            wait(eng, turned_back, c * TB_ + (q + 1))
            if q >= 2:
                wait(eng, out_psum, c * TB_ + (q - 1))
            copy(givenT[q % 2][:, :, :].rearrange("p g d -> p (g d)"), bank[q % 2]).then_inc(done, 1)

        @block.scalar
        def _(act):
            wait(act, w_loaded, 16 * len(dram["experts_loads"]))

            def chunk(c):
                def hT_out(j):
                    wait(act, turned, c * CB_ + (j + 1))
                    wait(act, logits_psum, c * CB_ + j)
                    nc.scalar.copy(hT[:, :], bank[0][:, 0:T]).then_inc(hT_done, 1)

                def sent_out(j):
                    wait(act, sent_psum, c * CB_ + (j + 1))
                    for t in range(TT):
                        g0 = (j * TT + t) * TG
                        last = nc.scalar.copy(sent[:, :, g0:g0 + TG], bank[3 + t].rearrange("p (g s) -> p s g", g=TG))
                    last.then_inc(sent_done, 1)

                def relu(r):
                    wait(act, inner_done, c * ROUNDS + (r + 1))
                    if r >= 2:
                        wait(act, given_psum, c * GB_ + (r - 1) * (EB // 2))
                    for s in (2, 3):
                        last = nc.scalar.activation(relued[r % 2][:, :, s, :], inner[:, :, :], ACT.Relu, scale=own[:, s:s + 1])
                    last.then_inc(relued_act, 1)

                for k in range(CB_ + 2):
                    if k < CB_:
                        hT_out(k)
                    if k >= 2:
                        sent_out(k - 2)
                relu(0)
                for r in range(ROUNDS):
                    if r + 1 < ROUNDS:
                        relu(r + 1)
                    for n in range(r * (EB // 2), (r + 1) * (EB // 2)):
                        if n % 2:
                            results_out(act, nc.scalar.copy, given_act, c, n)
                for q in range(1, TB_, 2):
                    turned_out(act, nc.scalar.copy, givenT_act, c, q)

            chunk(0)
            with act.Fori(1, NCHUNK - 1) as c:
                chunk(c)
            chunk(NCHUNK - 1)

        @block.gpsimd
        def _(pool):
            def norm(c, j):
                n = c * CB_ + j
                wait(pool, moments_done, n + 1)
                nc.gpsimd.tensor_tensor(vareps[:, :], moments[:, :, 1], eps[:, 0:TT], ALU.add).then_inc(vareps_done, 1)
                wait(pool, vareps_done, n + 1)
                wait(pool, xhat_done, n)
                nc.gpsimd.tensor_tensor(rstd[:, :], vareps[:, :], minus_half[:, 0:TT], ALU.pow).then_inc(rstd_done, 1)
                wait(pool, xhat_done, n + 1)
                wait(pool, mod_loaded, n * 16 + 16)
                nc.gpsimd.tensor_tensor(scaled[:, :, :], xhat[:, :, :],
                                        mod_norm[j % 2][:, 0:1, :].broadcast_to([P, TT, D]), ALU.mult).then_inc(scaled_done, 1)
                wait(pool, scaled_done, n + 1)
                wait(pool, sent_psum, c * CB_ + (j - HB + 1))
                nc.gpsimd.tensor_tensor(h[j % HB][:, :, :], scaled[:, :, :],
                                        mod_norm[j % 2][:, 1:2, :].broadcast_to([P, TT, D]), ALU.add).then_inc(h_done, 1)

            def chunk(c):
                for j in range(2, CB_ if is_last(c) else CB_ + 2):
                    norm(c, j)

            norm(0, 0)
            norm(0, 1)
            chunk(0)
            with pool.Fori(1, NCHUNK - 1) as c:
                chunk(c)
            chunk(NCHUNK - 1)

        @block.vector
        def _(dve):
            wait(dve, w_loaded, 16 * len(dram["experts_loads"]))

            def count(c, j):
                return c * CB_ + j

            def moments_of(c, j):
                wait(dve, moments_done, count(c, j))
                for t in range(TT):
                    last = nc.vector.bn_stats(stats[:, t, :], tile(c, j, t))
                last.then_inc(stats_done, 1)
                wait(dve, rstd_done, count(c, j))
                wait(dve, xhat_done, count(c, j))
                wait(dve, stats_done, count(c, j + 1))
                nc.vector.memset(unread[:, :], 0.0)
                for t in range(TT):
                    last = nc.vector.bn_aggr(moments[:, t, :], stats[:, t, :])
                last.then_inc(moments_done, 1)

            def standardise(c, j):
                wait(dve, scaled_done, count(c, j))
                wait(dve, rstd_done, count(c, j + 1))
                for t in range(TT):
                    last = nc.vector.tensor_scalar(xhat[:, t, :], tile(c, j, t), moments[:, t, 0:1], rstd[:, t:t + 1],
                                                   ALU.subtract, ALU.mult)
                last.then_inc(xhat_done, 1)

            def chunk(c):
                def choose(j):
                    wait(dve, takenT_done, count(c, j))
                    wait(dve, logits_psum, count(c, j + 1))
                    nc.vector.tensor_tensor(logits[:, :].rearrange("p (g t) -> p g t", t=GT),
                                            bank[1][:, 0:T].rearrange("p (g t) -> p g t", t=GT),
                                            tie[:, :].unsqueeze(1).broadcast_to([P, T // GT, GT]), ALU.add).then_inc(logits_done, 1)
                    wait(dve, logits_done, count(c, j + 1))
                    nc.vector.tensor_reduce(best[:, :], logits[:, :].rearrange("p (g t) -> p g t", t=GT), AX.X,
                                            ALU.max).then_inc(best_done, 1)
                    wait(dve, best_done, count(c, j + 1))
                    nc.vector.tensor_tensor(takenT[:, j, :].rearrange("p (g t) -> p g t", t=GT),
                                            logits[:, :].rearrange("p (g t) -> p g t", t=GT),
                                            best[:, :].unsqueeze(2).broadcast_to([P, T // GT, GT]), ALU.is_equal).then_inc(takenT_done, 1)

                def own_groups(j):
                    wait(dve, taken_psum, count(c, j + 1))
                    wait(dve, sent_psum, count(c, j))
                    for t in range(TT):
                        last = nc.vector.tensor_tensor(taken[:, t, :, :], bank[2][:, t * P:(t + 1) * P].unsqueeze(1).broadcast_to([P, TG, SLOTS]),
                                                       own[:, :].unsqueeze(2).broadcast_to([P, TG, SLOTS]), ALU.mult)
                    last.then_inc(taken_done, 1)

                def relu(r):
                    wait(dve, inner_psum, c * ROUNDS + (r + 1))
                    wait(dve, relued_dve, c * ROUNDS + r)
                    wait(dve, relued_act, c * ROUNDS + r)
                    nc.vector.tensor_tensor(inner[:, :, :], bank[r].rearrange("p (e g) -> p e g", g=CG),
                                            bias[:, r * EB:(r + 1) * EB].unsqueeze(2).broadcast_to([P, EB, CG]), ALU.add).then_inc(inner_done, 1)
                    wait(dve, inner_done, c * ROUNDS + (r + 1))
                    if r >= 2:
                        wait(dve, given_psum, c * GB_ + (r - 1) * (EB // 2))
                    for s in (0, 1):
                        last = nc.vector.tensor_scalar(relued[r % 2][:, :, s, :], inner[:, :, :], 0.0, own[:, s:s + 1], ALU.max, ALU.mult)
                    last.then_inc(relued_dve, 1)

                def residual(j):
                    wait(dve, x_done, count(c, j))
                    wait(dve, out_psum, c * TB_ + (j + 1) * TT)
                    nc.vector.tensor_tensor(delta[:, :, :], bank[4 + j % 2][:, 0:T].rearrange("p (t d) -> p t d", t=TT),
                                            gates[:, j:j + 1, :].broadcast_to([P, TT, D]), ALU.mult).then_inc(delta_done, 1)
                    wait(dve, delta_done, count(c, j + 1))
                    nc.vector.tensor_tensor(tiles(c, j), tiles(c, j), delta[:, :, :], ALU.add).then_inc(x_done, 1)

                for k in range(CB_ + 1):
                    if k + 2 < CB_:
                        moments_of(c, k + 2)
                    if k < CB_:
                        choose(k)
                    if k >= 1:
                        own_groups(k - 1)
                    if k + 2 < CB_:
                        standardise(c, k + 2)
                wait(dve, gates_loaded, c * (16 * CB_) + 16 * CB_)
                relu(0)
                for r in range(ROUNDS):
                    if r + 1 < ROUNDS:
                        relu(r + 1)
                    for n in range(r * (EB // 2), (r + 1) * (EB // 2)):
                        if n % 2 == 0:
                            results_out(dve, nc.vector.tensor_copy, given_dve, c, n)
                    if not is_last(c) and r < 2:
                        moments_of(c, CB_ + r)
                        standardise(c, CB_ + r)
                for q in range(0, TB_, 2):
                    turned_out(dve, nc.vector.tensor_copy, givenT_dve, c, q)
                    if q >= 2:
                        residual(q // 2 - 1)
                residual(CB_ - 1)

            for j in range(2):
                moments_of(0, j)
                standardise(0, j)
            chunk(0)
            with dve.Fori(1, NCHUNK - 1) as c:
                chunk(c)
            chunk(NCHUNK - 1)


SMALL_SCORE = 40.0
STACK_ORDER = (1, 0, 3, 2)


def attention_1(nc, ctx, dram, sbuf, psum, with_max):
    def sem(name):
        key = "sem_" + name
        if key not in sbuf["a1"]:
            sbuf["a1"][key] = dram["semaphores"].enter_context(nc.semaphore("a1_" + name))
        return sbuf["a1"][key]

    def sb(name, shape, dt=F32):
        if name not in sbuf["a1"]:
            sbuf["a1"][name] = ctx.enter_context(nc.sbuf_tensor("a1_" + name, shape, dt))
        return sbuf["a1"][name]

    X, ident, minus_half, eps, modcol = (sbuf[k] for k in ("X", "ident", "minus_half", "eps", "modcol"))
    kmask, vpad, wqk, wv, wo, bqk, bv, rope = (sbuf[k] for k in ("kmask1", "vpad1", "wqk1", "wv1", "wo1", "bqk1", "bv1", "rope"))
    mod_gate = [sb(f"mod_gate{i}", [P, 2, D]) for i in range(2)]
    stats, moments, vareps, rstd = sb("stats", [P, TT, 6]), sb("moments", [P, TT, 2]), sb("vareps", [P, TT]), sb("rstd", [P, TT])
    xhat, hT = sb("xhat", [P, TT, D]), [sb(f"hT{i}", [P, T]) for i in range(2)]
    qk = sb("qk", [P, TT, 2 * H, HD])
    by_cos, by_sin = sb("by_cos", [P, TT, 2 * H, HD]), sb("by_sin", [P, TT, 2 * H, HD])
    turned_qk = sb("turned_qk", [P, 2, TT * H, HD])
    qstack, kstack = sb("qstack", [P, TT * H, 4, HD], F32R), sb("kstack", [P, TT * H, 4, HD], F32R)
    qT = [sb(f"qT{i}", [P, G, T], F32R) for i in range(2)]
    kT = sb("kT", [P, G, T], F32R)
    probs = sb("probs", [P, 4, G, T])
    sums, recip, heads_out_tok, oT = sb("sums", [P, 2 * T]), sb("recip", [P, TT * H]), sb("heads_tok", [P, TT * H, HD]), sb("oT", [P, T])
    delta, unread = sb("delta", [P, TT, D]), sb("unread", [P, 1])

    SC = [psum[:, 1024 * i:1024 * (i + 1)] for i in range(2)]
    PO = psum[:, 2048:2560]
    PT, PQ = psum[:, 2560:3072], psum[:, 3072:3584]
    PV = PT[:, T:2 * T]
    PP = psum[:, 3584:4096]

    mod_gate_loaded = [sem(f"mod_gate_loaded{i}") for i in range(2)]
    stats_done, moments_done, vareps_done, rstd_done, xhat_done = map(sem, ("stats", "moments", "vareps", "rstd", "xhat"))
    turned, hT_done, qk_psum, qk_done, v_psum, values_done = map(sem, ("turned", "hT", "qk_psum", "qk", "v_psum", "values"))
    by_cos_done, rope_products, rope_done, hi_done, stacks_done = map(sem, ("by_cos", "rope_products", "rope", "hi", "stacks"))
    stacks_psum, even_out, odd_out, k_spread = map(sem, ("stacks_psum", "even_out", "odd_out", "k_spread"))
    scores_ready, probs_ready, heads_done = map(sem, ("scores_ready", "probs_ready", "heads_done"))
    sums_done, sums_turned, recip_done, heads_tok_done = map(sem, ("sums", "sums_turned", "recip", "heads_tok"))
    heads_turned, oT_done, projected, delta_done, x_biased, x_done = map(
        sem, ("heads_turned", "oT", "projected", "delta", "x_biased", "x_done"))

    vdiag = [[bass.AP(tensor=v[:, :, :, :].tensor, offset=v[:, :, :, :].offset + 64 * s,
                      ap=[[TT * H * 32, P], [G * 32, TT * G], [32 + 16, 2], [1, HD]]) for s in range(2)] for v in vpad]

    def tiles(b):
        return X[:, bass.ds(b * TT, TT), :] if not isinstance(b, int) else X[:, b * TT:(b + 1) * TT, :]

    def tile(b, t):
        return X[:, bass.ds(b * TT + t, 1), :] if not isinstance(b, int) else X[:, b * TT + t:b * TT + t + 1, :]

    def gate_rows(b):
        src = dram["table"]
        src = (src[bass.ds(b, 1), ROW_GA1:ROW_GA1 + 2, :] if not isinstance(b, int)
               else src[b:b + 1, ROW_GA1:ROW_GA1 + 2, :])
        return src.rearrange("o r d -> (o r d)").partition_broadcast(P)

    def mod(j, b):
        return modcol[:, j, bass.ds(b, 1)] if not isinstance(b, int) else modcol[:, j, b:b + 1]

    def is_last(b, back=0):
        return isinstance(b, int) and b >= B - back

    if with_max:
        sel = sbuf["sel"]
        rowmax = sb("rowmax", [P, TT, H])
        maxstack = sb("maxstack", [P, TT, P], F32R)
        maxT = sb("maxT", [P, T], F32R)
        max_psum, rowmax_done, max_hi, max_lo, max_turned, maxT_done, sel_loaded, sel_done = map(
            sem, ("max_psum", "rowmax", "max_hi", "max_lo", "max_turned", "maxT", "sel_loaded", "sel"))

    def table(i, lo, hi):
        return rope[:, i, :, lo:hi].unsqueeze(2).broadcast_to([P, TT, 2 * H, hi - lo])

    def sync(sp):
        def load_gate(n, p):
            wait(sp, x_done, n - 1)
            sp.dma_start(mod_gate[p][:, :, :], gate_rows(n)).then_inc(mod_gate_loaded[p], 16)

        def spread(n, p):
            sp.wait_ge(even_out, n * 2 + 1)
            sp.wait_ge(odd_out, n * 2 + 1)
            wait(sp, scores_ready, n * CHUNKS - CHUNKS)
            for r in range(G):
                sp.dma_start(kmask[p][32 * r:32 * r + 32, r:H:G, :].bitcast(F32), kT[32 * r:32 * r + 32, :, :].bitcast(F32)).then_inc(k_spread, 16)

        def step(b, p):
            if not is_last(b, 1):
                spread(b + 1, 1 - p)
                load_gate(b + 1, 1 - p)

        load_gate(0, 0)
        for dst, src in dram["ffn_loads"]:
            sp.dma_start(dst, src).then_inc(dram["ffn_loaded"], 16)
        if with_max:
            sp.dma_start(sbuf["sel_loaded"][:, :, :].rearrange("p h c -> p (h c)"), dram["sel"]).then_inc(sel_loaded, 16)
        spread(0, 0)
        stepped(sp, 0, B - 1, 1, 14, step)

    def tensor(pe):
        def turn(n):
            pe.wait_ge(xhat_done, n + 1)
            wait(pe, values_done, n - 1)
            for t in range(TT):
                last = nc.tensor.transpose(PT[:, t * P:(t + 1) * P], xhat[:, t, :], ident[:, :])
            last.then_inc(turned, 1)

        def project_qk(n, p):
            pe.wait_ge(hT_done, n + 1)
            wait(pe, odd_out, n * 2)
            for t in range(TT):
                last = nc.tensor.matmul(PQ[:, t * 2 * D:(t + 1) * 2 * D], hT[p][:, t * P:(t + 1) * P], wqk[:, :], start=True, stop=True)
            last.then_inc(qk_psum, 1)

        def project_v(n, p):
            pe.wait_ge(even_out, n * 2 + 2)
            for t in range(TT):
                last = nc.tensor.matmul(PV[:, t * D:(t + 1) * D], hT[p][:, t * P:(t + 1) * P], wv[:, :], start=True, stop=True)
            last.then_inc(v_psum, 1)

        def turn_stack(n, k):
            pe.wait_ge(stacks_done, n + 1)
            if k == 0:
                pe.wait_ge(hT_done, n + 2 if not is_last(n, 1) else B)
            if k >= 2:
                pe.wait_ge((even_out, odd_out)[k % 2], n * 2 + 1)
            src, dst = (kstack, kstack, qstack, qstack)[k], (PT, PQ)[k % 2]
            for i in range(2):
                g = 2 * (k % 2) + i
                for t in range(TT):
                    last = nc.tensor.transpose(dst[:, i * T + t * P:i * T + (t + 1) * P].bitcast(F32R),
                                               src[:, t * H + G * g:t * H + G * (g + 1), :, :].rearrange("p h s d -> p (h s d)"),
                                               sbuf["ident_r"][:, :])
            last.then_inc(stacks_psum, 1)

        def maxima(b, p):
            pe.wait_ge(k_spread, b * (16 * G) + 16 * G)
            pe.wait_ge(even_out, b * 2 + 2)
            pe.wait_ge(odd_out, b * 2 + 2)
            wait(pe, probs_ready, b * CHUNKS)
            for c in range(CHUNKS):
                t, g = c // G, c % G
                wait(pe, rowmax_done, b * CHUNKS + (c - 1))
                for r in range(G):
                    last = nc.tensor.matmul(SC[c % 2][:, r * T:(r + 1) * T], qT[p][:, g, t * P:(t + 1) * P],
                                            kmask[p][:, G * g + r, :], start=True, stop=True)
                last.then_inc(max_psum, 1)
            pe.wait_ge(max_lo, b + 1)
            for t in range(TT):
                last = nc.tensor.transpose(SC[0][:, t * P:(t + 1) * P], maxstack[:, t, :].bitcast(F32), ident[:, :])
            last.then_inc(max_turned, 1)
            pe.wait_ge(maxT_done, b + 1)

        def scores(b, p, c):
            r, kb = c // TT, c % TT
            if c == 0:
                if with_max:
                    maxima(b, p)
                else:
                    pe.wait_ge(k_spread, b * (16 * G) + 16 * G)
                    pe.wait_ge(even_out, b * 2 + 2)
                    pe.wait_ge(odd_out, b * 2 + 2)
            wait(pe, probs_ready, b * CHUNKS + (c - 1))
            for g in range(G):
                last = nc.tensor.matmul(SC[c % 2][:, g * T:(g + 1) * T], kmask[p][:, G * g + r, kb * P:(kb + 1) * P],
                                        qT[p][:, g, :], start=True, stop=not with_max)
                if with_max:
                    last = nc.tensor.matmul(SC[c % 2][:, g * T:(g + 1) * T], sel[:, G * g + r, :], maxT[:, :],
                                            start=False, stop=True)
            last.then_inc(scores_ready, 1)

        def heads(b, p, c):
            r, kb = c // TT, c % TT
            s = r // 2
            if c == 0:
                wait(pe, sums_done, b)
                pe.wait_ge(values_done, b + 1)
            pe.wait_ge(probs_ready, b * CHUNKS + (c + 1))
            for g in range(G):
                last = nc.tensor.matmul(PO[32 * g:32 * g + 32, s * T:(s + 1) * T], vpad[p][:, kb, G * g + r, :],
                                        probs[:, c % 4, g, :], start=(c % 4 == 0), stop=(c % 4 == 3))
            last.then_inc(heads_done, 1)

        def turn_sums(n):
            pe.wait_ge(sums_done, n + 1)
            wait(pe, delta_done, n)
            for t in range(TT):
                for s in range(2):
                    last = nc.tensor.transpose(PP[:, (t * 2 + s) * P:(t * 2 + s + 1) * P], sums[:, s * T + t * P:s * T + (t + 1) * P], ident[:, :])
            last.then_inc(sums_turned, 1)

        def turn_heads(n):
            pe.wait_ge(heads_tok_done, n + 1)
            for t in range(TT):
                last = nc.tensor.transpose(PP[:, t * P:(t + 1) * P],
                                           heads_out_tok[:, t * H:(t + 1) * H, :].rearrange("p h d -> p (h d)"), ident[:, :])
            last.then_inc(heads_turned, 1)

        def project_out(n):
            pe.wait_ge(oT_done, n + 1)
            for t in range(TT):
                last = nc.tensor.matmul(PP[:, T + t * D:T + (t + 1) * D], oT[:, t * P:(t + 1) * P], wo[:, :], start=True, stop=True)
            last.then_inc(projected, 1)

        def step(b, p):
            first, more, projects = isinstance(b, int) and b == 0, not is_last(b, 1), not is_last(b, 2)
            if projects:
                turn(b + 2)
            for c in range(CHUNKS):
                scores(b, p, c)
                if c < 2 and not first:
                    heads(b - 1, 1 - p, c + CHUNKS - 2)
                if c >= 2:
                    heads(b, p, c - 2)
                if c == 0 and more:
                    turn_stack(b + 1, 1)
                if c == 0 and more:
                    turn_stack(b + 1, 0)
                if c == 1 and more:
                    turn_stack(b + 1, 3)
                if c == 1 and more:
                    turn_stack(b + 1, 2)
                if c == 2 and not first:
                    turn_sums(b - 1)
                if c == 2 and projects:
                    project_qk(b + 2, p)
                if c == 3 and more:
                    project_v(b + 1, 1 - p)
                if c == 4 and not first:
                    turn_heads(b - 1)
                if c == 5 and not first:
                    project_out(b - 1)

        if with_max:
            pe.wait_ge(sel_done, 1)
        turn(0)
        project_qk(0, 0)
        turn(1)
        for k in STACK_ORDER:
            turn_stack(0, k)
        project_v(0, 0)
        project_qk(1, 1)
        stepped(pe, 0, B - 1, 1, 14, step)
        for c in (CHUNKS - 2, CHUNKS - 1):
            heads(B - 1, 1, c)
        turn_sums(B - 1)
        turn_heads(B - 1)
        project_out(B - 1)

    def scalar(act):
        def stacks_out(n, p, k):
            act.wait_ge(stacks_psum, n * 4 + (STACK_ORDER.index(k) + 1))
            if k == 1:
                wait(act, k_spread, n * (16 * G))
                dst = kT
            else:
                wait(act, scores_ready, n * CHUNKS - CHUNKS)
                dst = qT[p]
            nc.scalar.copy(dst[:, 2:4, :].rearrange("p g k -> p (g k)"), PQ).then_inc(odd_out, 1)

        def oT_out(n):
            act.wait_ge(heads_turned, n + 1)
            wait(act, projected, n)
            nc.scalar.copy(oT[:, :], PP[:, 0:T]).then_inc(oT_done, 1)

        def prob(b, c):
            act.wait_ge(scores_ready, b * CHUNKS + (c + 1))
            wait(act, heads_done, b * CHUNKS + (c - 3))
            nc.scalar.activation(probs[:, c % 4, :, :], SC[c % 2].rearrange("p (g q) -> p g q", g=G), ACT.Exp,
                                 scale=float(np.float32(1.0) / np.sqrt(np.float32(HD)))).then_inc(probs_ready, 1)

        def step(b, p):
            first, more = isinstance(b, int) and b == 0, not is_last(b, 1)
            for c in range(CHUNKS):
                prob(b, c)
                if c == 0 and more:
                    stacks_out(b + 1, 1 - p, 1)
                if c == 1 and more:
                    stacks_out(b + 1, 1 - p, 3)
                if c == 4 and not first:
                    oT_out(b - 1)

        stacks_out(0, 0, 1)
        stacks_out(0, 0, 3)
        stepped(act, 0, B - 1, 1, 14, step)
        oT_out(B - 1)

    def gpsimd(pool):
        def norm(n):
            wait(pool, rstd_done, n)
            pool.wait_ge(moments_done, n + 1)
            nc.gpsimd.tensor_tensor(vareps[:, :], moments[:, :, 1], eps[:, 0:TT], ALU.add).then_inc(vareps_done, 1)
            pool.wait_ge(vareps_done, n + 1)
            wait(pool, xhat_done, n)
            nc.gpsimd.tensor_tensor(rstd[:, :], vareps[:, :], minus_half[:, 0:TT], ALU.pow).then_inc(rstd_done, 1)

        def rotate(n):
            pool.wait_ge(qk_done, n + 1)
            wait(pool, rope_done, n)

            half = HD // 2
            nc.gpsimd.tensor_tensor(by_sin[:, :, :, 0:half], qk[:, :, :, half:HD], table(1, 0, half), ALU.mult)
            nc.gpsimd.tensor_tensor(by_sin[:, :, :, half:HD], qk[:, :, :, 0:half], table(1, half, HD), ALU.mult).then_inc(rope_products, 1)

        def bias_x(n, p):
            pool.wait_ge(mod_gate_loaded[p], n * 8 + (16 - 8 * p))
            pool.wait_ge(xhat_done, n + 1)
            nc.gpsimd.tensor_tensor(tiles(n), tiles(n), mod_gate[p][:, 1:2, :].broadcast_to([P, TT, D]),
                                    ALU.add).then_inc(x_biased, 1)

        def step(b, p):
            bias_x(b, p)
            if not is_last(b, 3):
                norm(b + 3)
            if not is_last(b, 2):
                rotate(b + 2)

        norm(0)
        norm(1)
        rotate(0)
        norm(2)
        rotate(1)
        stepped(pool, 0, B - 1, 1, 14, step)

    def vector(dve):
        def norm_a(n):
            wait(dve, moments_done, n)
            for t in range(TT):
                last = nc.vector.bn_stats(stats[:, t, :], tile(n, t)[:, 0, :])
            last.then_inc(stats_done, 1)
            wait(dve, xhat_done, n)
            dve.wait_ge(stats_done, n + 1)
            nc.vector.memset(unread[:, :], 0.0)
            for t in range(TT):
                last = nc.vector.bn_aggr(moments[:, t, :], stats[:, t, :])
            last.then_inc(moments_done, 1)

        def norm_b(n):
            dve.wait_ge(rstd_done, n + 1)
            wait(dve, turned, n)
            for t in range(TT):
                last = nc.vector.tensor_scalar(xhat[:, t, :], tile(n, t)[:, 0, :], moments[:, t, 0:1], rstd[:, t:t + 1], ALU.subtract, ALU.mult)
            last.then_inc(xhat_done, 1)

        def turned_out(n, p):
            dve.wait_ge(turned, n + 1)
            wait(dve, qk_psum, n - 1)
            wait(dve, v_psum, n - 1)
            nc.vector.tensor_scalar(hT[p][:, :], PT[:, 0:T], mod(0, n), mod(1, n), ALU.mult, ALU.add).then_inc(hT_done, 1)

        def add_biases(n):
            dve.wait_ge(qk_psum, n + 1)
            wait(dve, rope_products, n)
            wait(dve, by_cos_done, n)
            nc.vector.tensor_tensor(qk[:, :, :, :].rearrange("p t h d -> p t (h d)"), PQ.rearrange("p (t c) -> p t c", t=TT),
                                    bqk[:, :].unsqueeze(1).broadcast_to([P, TT, 2 * D]), ALU.add).then_inc(qk_done, 1)

        def cosines(n):
            dve.wait_ge(qk_done, n + 1)
            wait(dve, rope_done, n)
            nc.vector.tensor_tensor(by_cos[:, :, :, :], qk[:, :, :, :], table(0, 0, HD), ALU.mult).then_inc(by_cos_done, 1)

        def values(n, p):
            dve.wait_ge(v_psum, n + 1)
            wait(dve, heads_done, n * CHUNKS - CHUNKS)
            for s in range(2):
                def heads_of(ap):
                    return ap.rearrange("p (j r d) -> p j r d", r=G, d=HD)[:, :, 2 * s:2 * s + 2, :]
                last = nc.vector.tensor_tensor(vdiag[p][s], heads_of(PV), heads_of(bv[:, :]), ALU.add)
            last.then_inc(values_done, 1)

        def split(n):
            dve.wait_ge(rope_products, n + 1)
            dve.wait_ge(by_cos_done, n + 1)
            wait(dve, stacks_done, n)
            nc.vector.tensor_tensor(turned_qk[:, :, :, :].rearrange("p k (t h) d -> p t k (h d)", t=TT),
                                    by_cos[:, :, :, :].rearrange("p t (k h) d -> p t k (h d)", k=2),
                                    by_sin[:, :, :, :].rearrange("p t (k h) d -> p t k (h d)", k=2), ALU.add).then_inc(rope_done, 1)
            dve.wait_ge(rope_done, n + 1)
            wait(dve, stacks_psum, n * 4)

            def twice(i):
                return turned_qk[:, i, :, :].unsqueeze(2).broadcast_to([P, TT * H, 2, HD])

            nc.vector.tensor_copy(kstack[:, :, 0:2, :], twice(1))
            nc.vector.tensor_copy(qstack[:, :, 0:4:2, :], twice(0)).then_inc(hi_done, 1)
            dve.wait_ge(hi_done, n + 1)
            nc.vector.tensor_tensor(kstack[:, :, 2:4, :], twice(1), kstack[:, :, 0:2, :].bitcast(F32), ALU.subtract)
            nc.vector.tensor_tensor(qstack[:, :, 1:4:2, :], twice(0), qstack[:, :, 0:4:2, :].bitcast(F32), ALU.subtract).then_inc(stacks_done, 1)

        def stacks_out(n, p, k):
            dve.wait_ge(stacks_psum, n * 4 + (STACK_ORDER.index(k) + 1))
            if k == 0:
                wait(dve, k_spread, n * (16 * G))
                dst = kT
            else:
                wait(dve, scores_ready, n * CHUNKS - CHUNKS)
                dst = qT[p]
            nc.vector.tensor_copy(dst[:, 0:2, :].rearrange("p g k -> p (g k)"), PT).then_inc(even_out, 1)

        def sums_out(n):
            dve.wait_ge(heads_done, n * CHUNKS + CHUNKS)
            wait(dve, sums_turned, n)
            nc.vector.tensor_copy(sums[:, :], PO).then_inc(sums_done, 1)

        def divide(n):
            dve.wait_ge(sums_turned, n + 1)
            wait(dve, heads_tok_done, n)
            by_head = PP.rearrange("p (h w) -> p h w", w=16)
            nc.vector.reciprocal(recip[:, :], by_head[:, :, HD]).then_inc(recip_done, 1)
            dve.wait_ge(recip_done, n + 1)
            wait(dve, heads_turned, n)
            nc.vector.tensor_tensor(heads_out_tok[:, :, :], by_head[:, :, 0:HD],
                                    recip[:, :].unsqueeze(2).broadcast_to([P, TT * H, HD]), ALU.mult).then_inc(heads_tok_done, 1)

        def residual(n, p):
            dve.wait_ge(projected, n + 1)
            wait(dve, x_done, n)
            dve.wait_ge(mod_gate_loaded[p], n * 8 + (16 - 8 * p))
            nc.vector.tensor_tensor(delta[:, :, :], PP[:, T:2 * T].rearrange("p (t d) -> p t d", t=TT),
                                    mod_gate[p][:, 0:1, :].broadcast_to([P, TT, D]), ALU.mult).then_inc(delta_done, 1)
            dve.wait_ge(delta_done, n + 1)
            dve.wait_ge(x_biased, n + 1)
            nc.vector.tensor_tensor(tiles(n), tiles(n), delta[:, :, :], ALU.add).then_inc(x_done, 1)

        def maxima(b):
            for c in range(CHUNKS):
                t, g = c // G, c % G
                dve.wait_ge(max_psum, b * CHUNKS + (c + 1))
                if c == 0:
                    wait(dve, max_lo, b)
                nc.vector.tensor_reduce(rowmax[:, t, G * g:G * (g + 1)], SC[c % 2].rearrange("p (r k) -> p r k", r=G),
                                        AX.X, ALU.max).then_inc(rowmax_done, 1)
            dve.wait_ge(rowmax_done, b * CHUNKS + CHUNKS)
            wait(dve, max_turned, b)
            nc.vector.tensor_scalar(maxstack[:, :, 0:H], rowmax[:, :, :], -1.0, None, ALU.mult).then_inc(max_hi, 1)
            dve.wait_ge(max_hi, b + 1)
            nc.vector.scalar_tensor_tensor(out=maxstack[:, :, H:2 * H], in0=rowmax[:, :, :], scalar=-1.0,
                                           in1=maxstack[:, :, 0:H].bitcast(F32), op0=ALU.mult, op1=ALU.subtract).then_inc(max_lo, 1)
            dve.wait_ge(max_turned, b + 1)
            wait(dve, scores_ready, b * CHUNKS)
            nc.vector.tensor_copy(maxT[:, :], SC[0][:, 0:T]).then_inc(maxT_done, 1)

        def step(b, p):
            first, more, projects = isinstance(b, int) and b == 0, not is_last(b, 1), not is_last(b, 2)
            norms = not is_last(b, 3)
            if with_max:
                maxima(b)
            if projects:
                turned_out(b + 2, p)
            if more:
                stacks_out(b + 1, 1 - p, 0)
            if not first:
                sums_out(b - 1)
            if more:
                stacks_out(b + 1, 1 - p, 2)
            if norms:
                norm_a(b + 3)
            if not first:
                divide(b - 1)
            if projects:
                add_biases(b + 2)
                cosines(b + 2)
            if more:
                values(b + 1, 1 - p)
            if norms:
                norm_b(b + 3)
            if projects:
                split(b + 2)
            if not first:
                residual(b - 1, 1 - p)

        if with_max:
            dve.wait_ge(sel_loaded, 16)
            nc.vector.tensor_copy(sel[:, :, :], sbuf["sel_loaded"][:, :, :]).then_inc(sel_done, 1)
        norm_a(0)
        norm_b(0)
        turned_out(0, 0)
        norm_a(1)
        norm_b(1)
        add_biases(0)
        cosines(0)
        split(0)
        turned_out(1, 1)
        norm_a(2)
        stacks_out(0, 0, 0)
        stacks_out(0, 0, 2)
        values(0, 0)
        add_biases(1)
        cosines(1)
        norm_b(2)
        split(1)
        stepped(dve, 0, B - 1, 1, 14, step)
        sums_out(B - 1)
        divide(B - 1)
        residual(B - 1, 1)

    return {"sync": sync, "tensor": tensor, "scalar": scalar, "gpsimd": gpsimd, "vector": vector}


def attention_1_setup(nc, ctx, dram, sbuf, psum):
    def sem(name):
        return dram["semaphores"].enter_context(nc.semaphore("s1_" + name))

    def sb(name, shape, dt=F32):
        return ctx.enter_context(nc.sbuf_tensor("s1_" + name, shape, dt))

    modcol, ident, wqk, bqk, kmask, vpad = (sbuf[k] for k in ("modcol", "ident", "wqk1", "bqk1", "kmask1", "vpad1"))
    zeroed, squared, most, summed, moved, step, filled = map(
        sem, ("zeroed", "squared", "most", "summed", "moved", "step", "filled"))
    mod2, mod2max = sb("mod2", [P, 2, B]), sb("mod2max", [P, 2])
    w2, ones, b2 = sb("w2", [P, 2 * D]), sb("ones", [P, 1]), sb("b2", [1, 2 * D])
    terms, whead, bhead, h2 = sb("terms", [1, 2]), sb("whead", [1, 2 * H]), sb("bhead", [1, 2 * H]), sb("h2", [1, 4])
    head2, top = sb("head2", [1, 2 * H]), sb("top", [1, 1])
    small = sbuf["small_scores"]
    wsum, modrow = psum[0:1, 0:2 * D], psum[0:1, 512:512 + 2 * P]
    near, far = 1.0 + 1.0 / 16, 17.0

    with nc.Block() as block:
        @block.gpsimd
        def _(pool):
            for v in vpad:
                last = nc.gpsimd.memset(v[:, :, :, :], 0.0)
            last.then_inc(zeroed, 1)
            pool.wait_ge(zeroed, 1)
            for v in vpad:
                for a in range(2):
                    nc.gpsimd.memset(v[:, :, a:H:2, 16 * a + HD:16 * a + HD + 1], 1.0)
            nc.gpsimd.memset(kmask[0][:, :, :].bitcast(F32), 0.0)
            nc.gpsimd.memset(sbuf["a1"]["maxstack"][:, :, :].bitcast(F32), 0.0)

        @block.tensor
        def _(pe):
            pe.wait_ge(squared, 1)
            nc.tensor.matmul(wsum, ones[:, :], w2[:, :], start=True, stop=True)
            pe.wait_ge(most, 1)
            for i in range(2):
                last = nc.tensor.matmul(modrow[:, i * P:(i + 1) * P], mod2max[:, i:i + 1], ident[:, :], start=True, stop=True)
            last.then_inc(moved, 1)

        @block.vector
        def _(dve):
            def then(ins, k):
                ins.then_inc(step, 1)
                dve.wait_ge(step, k)

            nc.vector.memset(ones[:, :], 1.0)
            nc.vector.tensor_copy(sbuf["ident_r"][:, :], ident[:, :])
            nc.vector.tensor_tensor(w2[:, :], wqk[:, :], wqk[:, :], ALU.mult)
            nc.vector.tensor_tensor(b2[:, :], bqk[0:1, :], bqk[0:1, :], ALU.mult)
            nc.vector.tensor_tensor(mod2[:, :, :], modcol[:, 0:2, :], modcol[:, 0:2, :], ALU.mult).then_inc(squared, 1)
            dve.wait_ge(squared, 1)
            nc.vector.tensor_reduce(mod2max[:, :], mod2[:, :, :], AX.X, ALU.max).then_inc(most, 1)
            nc.vector.memset(kmask[1][:, :, :].bitcast(F32), 0.0)
            dve.wait_ge(moved, 1)
            nc.vector.tensor_reduce(terms[:, :], modrow.rearrange("p (i d) -> p i d", i=2), AX.X, ALU.max)
            nc.vector.tensor_reduce(bhead[:, :], b2[:, :].rearrange("p (h d) -> p h d", d=HD), AX.X, ALU.add)
            then(nc.vector.tensor_reduce(whead[:, :], wsum.rearrange("p (h d) -> p h d", d=HD), AX.X, ALU.add), 1)
            then(nc.vector.tensor_scalar(h2[:, 0:1], terms[:, 0:1], near * near * D, None, ALU.mult), 2)
            then(nc.vector.tensor_scalar(h2[:, 1:2], terms[:, 1:2], far * near * D, None, ALU.mult), 3)
            then(nc.vector.tensor_tensor(h2[:, 2:3], h2[:, 0:1], h2[:, 1:2], ALU.add), 4)
            then(nc.vector.tensor_scalar(bhead[:, :], bhead[:, :], far, None, ALU.mult), 5)
            then(nc.vector.scalar_tensor_tensor(out=head2[:, :], in0=whead[:, :], scalar=h2[:, 2:3], in1=bhead[:, :],
                                                op0=ALU.mult, op1=ALU.add), 6)
            then(nc.vector.tensor_reduce(top[:, :], head2[:, :], AX.X, ALU.max), 7)
            nc.vector.tensor_scalar(small[:, :], top[:, :], SMALL_SCORE * float(np.sqrt(HD)), None, ALU.is_le)


FT = 512
FTT = FT // P
FB = FT // T
NT = B * T // FT
HID = 512
KH = HID // P
EXACT_BELOW = 0.0
PIECES = 4
W1, W2, H1, H2, W3, WEIGHTS = 0, HID, 2 * HID, 2 * HID + KH * HID, 2 * HID + 2 * KH * HID, 2 * HID + 2 * KH * HID + KH * D


def ffn_1(nc, ctx, dram, sbuf, psum, split):
    def sem(name):
        key = "sem_" + name
        if key not in sbuf["ffn"]:
            sbuf["ffn"][key] = dram["semaphores"].enter_context(nc.semaphore("f_" + name))
        return sbuf["ffn"][key]

    def sb(name, shape, dt=F32):
        if name not in sbuf["ffn"]:
            sbuf["ffn"][name] = ctx.enter_context(nc.sbuf_tensor("ffn_" + name, shape, dt))
        return sbuf["ffn"][name]

    X, ident, minus_half, eps, modcol = (sbuf[k] for k in ("X", "ident", "minus_half", "eps", "modcol"))
    scales, out_scale = sbuf["scales"], sbuf["out_scale"]
    weights = sbuf["weights_r"] if split else sbuf["weights"]
    stats, moments, vareps, rstd = sb("stats", [P, FTT, 6]), sb("moments", [P, FTT, 2]), sb("vareps", [P, FTT]), sb("rstd", [P, FTT])
    xhat, unread = sb("xhat", [P, FTT, D]), sb("unread", [P, 1])
    tanh, gated = sb("tanh", [P, 2, FT]), sb("gated", [P, 2, FT])
    y = sb("y", [P, FT])
    full = [sb(f"full{i}", [P, KH if i else 1, FT]) for i in range(4)]
    hi = [sb(f"hi{i}", [P, KH if i else 1, FT], F32R) for i in range(4)]
    lo = [sb(f"lo{i}", [P, KH if i else 1, FT], F32R) for i in range(4)]
    bank = [psum[:, 512 * i:512 * (i + 1)] for i in range(8)]

    stats_done, moments_done, vareps_done, rstd_done, xhat_done, turned = map(
        sem, ("stats", "moments", "vareps", "rstd", "xhat", "turned"))
    full_done = [sem(f"full{i}") for i in range(4)]
    hi_done, lo_done = [sem(f"hi{i}") for i in range(4)], [sem(f"lo{i}") for i in range(4)]
    lo_dve = [sem(f"lo_dve{i}") for i in range(4)]
    tanh_done, gated_done = sem("tanh"), sem("gated")
    psum_done = [sem(f"psum{i}") for i in range(4)]
    y_done, turned_back, x_done = sem("y"), sem("turned_back"), sem("x_done")
    blocks = [1, KH, KH, KH]
    sums = [KH, KH, KH, 1]

    def tile(n, t):
        return X[:, bass.ds(n * FTT + t, 1), :][:, 0, :] if not isinstance(n, int) else X[:, n * FTT + t, :]

    def tiles(n):
        return X[:, bass.ds(n * FTT, FTT), :] if not isinstance(n, int) else X[:, n * FTT:(n + 1) * FTT, :]

    def col(ap, n, i):
        return ap[:, bass.ds(n * FB + i, 1)] if not isinstance(n, int) else ap[:, n * FB + i:n * FB + i + 1]

    def low_on_dve(layer, k):
        return layer >= 2 and k % 2 == 1

    def low_count(layer, n, k):
        return n * 2 + (k // 2 + 1) if layer >= 2 else n * blocks[layer] + (k + 1)

    def make_low(eng, subtract, layer, n, k):
        eng.wait_ge(hi_done[layer], n * blocks[layer] + (k + 1))
        eng.wait_ge(full_done[layer], n * blocks[layer] + (k + 1))
        wait(eng, psum_done[layer], n * sums[layer])
        done = lo_dve if low_on_dve(layer, k) else lo_done
        subtract(lo[layer][:, k, :], full[layer][:, k, :], hi[layer][:, k, :].bitcast(F32), ALU.subtract).then_inc(done[layer], 1)

    def pair(n, m):
        return (4, 0, 2, 4)[m] if isinstance(n, int) and n == 0 else 4

    def is_last(n, back=0):
        return isinstance(n, int) and n >= NT - back

    def sync(sp):
        def store(n):
            sp.wait_ge(x_done, n + 1)
            dst = dram["out"]
            dst = dst[:, bass.ds(n * FTT, FTT), :] if not isinstance(n, int) else dst[:, n * FTT:(n + 1) * FTT, :]
            sp.dma_start(dst, tiles(n)).then_inc(dram["out_stored"], 16)

        store(0)
        with sp.Fori(1, NT - 1) as n:
            store(n)
        store(NT - 1)
        sp.wait_ge(dram["out_stored"], 16 * NT)

    def tensor(pe):
        def value_ready(layer, n, k):
            if split:
                pe.wait_ge(hi_done[layer], n * blocks[layer] + (k + 1))
                pe.wait_ge((lo_dve if low_on_dve(layer, k) else lo_done)[layer], low_count(layer, n, k))
            else:
                pe.wait_ge(full_done[layer], n * blocks[layer] + (k + 1))

        def product(dst, layer, w0, k, first, last):
            parts = (hi, lo) if split else (full,)
            for i, part in enumerate(parts):
                ins = nc.tensor.matmul(dst, weights[:, w0:w0 + P], part[layer][:, k, :],
                                       start=first and i == 0, stop=last and i == len(parts) - 1)
            return ins

        def turn(n):
            pe.wait_ge(xhat_done, n + 1)
            wait(pe, full_done[0], n)
            wait(pe, x_done, n - 2)
            for t in range(FTT):
                last = nc.tensor.transpose(bank[6][:, t * P:(t + 1) * P], xhat[:, t, :], ident[:, :])
            last.then_inc(turned, 1)

        def gates(n, m):
            if m == 0:
                value_ready(0, n, 0)
            wait(pe, full_done[1], (m - 2 if isinstance(n, int) and n == 0 else n * KH + m))
            product(bank[pair(n, m)], 0, W1 + m * P, 0, True, True)
            product(bank[pair(n, m) + 1], 0, W2 + m * P, 0, True, True).then_inc(psum_done[0], 1)

        def last_layer(n):
            wait(pe, y_done, n)
            for k in range(KH):
                value_ready(3, n, k)
                last = product(bank[7], 3, W3 + k * D, k, k == 0, k == KH - 1)
            last.then_inc(psum_done[3], 1)

        def hidden(layer, n, w0, k):
            value_ready(layer, n, k)
            if isinstance(n, int) and n == 0 and layer == 1 and k == 0:
                pe.wait_ge(full_done[1], 3)
            for m in range(KH):
                if k == 0:
                    wait(pe, full_done[3 if layer == 1 else 2], n * KH + (m + 1 - (KH if layer == 1 else 0)))
                ins = product(bank[m], layer, w0 + k * HID + m * P, k, k == 0, k == KH - 1)
                if k == KH - 1:
                    ins.then_inc(psum_done[layer], 1)

        def turn_back(n):
            pe.wait_ge(y_done, n + 1)
            pe.wait_ge(full_done[0], n + 3 if not is_last(n, 2) else NT)
            wait(pe, x_done, n)
            for t in range(FTT):
                last = nc.tensor.transpose(bank[6][:, t * P:(t + 1) * P], y[:, t * P:(t + 1) * P], ident[:, :])
            last.then_inc(turned_back, 1)

        def step(n):
            first, gated_next, norms = isinstance(n, int) and n == 0, not is_last(n, 1), not is_last(n, 2)
            for k in range(KH):
                hidden(1, n, H1, k)
            if gated_next:
                gates(n + 1, 0)
            if not first:
                last_layer(n - 1)
            for k in range(KH):
                hidden(2, n, H2, k)
                if gated_next and k + 1 < KH:
                    gates(n + 1, k + 1)
                if k == 1 and not first:
                    turn_back(n - 1)
            if norms:
                turn(n + 2)

        turn(0)
        for m in range(KH):
            gates(0, m)
        turn(1)
        step(0)
        with pe.Fori(1, NT - 2) as n:
            step(n)
        step(NT - 2)
        step(NT - 1)
        last_layer(NT - 1)
        turn_back(NT - 1)

    def scalar(act):
        def high(layer, n, k):
            act.wait_ge(full_done[layer], n * blocks[layer] + (k + 1))
            wait(act, psum_done[layer], n * sums[layer])
            nc.scalar.copy(hi[layer][:, k, :], full[layer][:, k, :]).then_inc(hi_done[layer], 1)

        def gate(n, m):
            act.wait_ge(psum_done[0], n * KH + (m + 1))
            wait(act, gated_done, n * KH + (m - 1))
            nc.scalar.activation(tanh[:, m % 2, :], bank[pair(n, m)], ACT.Tanh, scale=scales[:, 0, m:m + 1]).then_inc(tanh_done, 1)

        def gelu(layer, n, m):
            act.wait_ge(psum_done[layer], n * KH + (m + 1))
            wait(act, psum_done[layer + 1], n * sums[layer + 1])
            nc.scalar.activation(full[layer + 1][:, m, :], bank[m], ACT.Gelu,
                                 scale=scales[:, 1 + layer, m:m + 1]).then_inc(full_done[layer + 1], 1)

        def gates(n):
            for m in range(KH):
                gate(n, m)
                if split and m >= 1:
                    high(1, n, m - 1)

        def step(n):
            for m in range(KH):
                gelu(1, n, m)
            if not is_last(n, 1):
                gates(n + 1)
            for m in range(KH):
                gelu(2, n, m)
                if m == 1 and split and not is_last(n, 1):
                    high(1, n + 1, KH - 1)

        gates(0)
        if split:
            high(1, 0, KH - 1)
        step(0)
        with act.Fori(1, NT - 2) as n:
            step(n)
        step(NT - 2)
        step(NT - 1)

    def gpsimd(pool):
        def norm(n):
            wait(pool, rstd_done, n)
            pool.wait_ge(moments_done, n + 1)
            nc.gpsimd.tensor_tensor(vareps[:, :], moments[:, :, 1], eps[:, 0:FTT], ALU.add).then_inc(vareps_done, 1)
            pool.wait_ge(vareps_done, n + 1)
            wait(pool, xhat_done, n)
            nc.gpsimd.tensor_tensor(rstd[:, :], vareps[:, :], minus_half[:, 0:FTT], ALU.pow).then_inc(rstd_done, 1)

        def low(layer, n):
            for k in range(blocks[layer]):
                if split and not low_on_dve(layer, k):
                    make_low(pool, nc.gpsimd.tensor_tensor, layer, n, k)

        def step(n):
            if not is_last(n, 2):
                norm(n + 2)
            low(2, n)
            if not is_last(n, 1):
                low(1, n + 1)
            low(3, n)
            if not is_last(n, 2):
                low(0, n + 2)

        norm(0)
        low(0, 0)
        norm(1)
        low(1, 0)
        low(0, 1)
        step(0)
        with pool.Fori(1, NT - 2) as n:
            step(n)
        step(NT - 2)
        step(NT - 1)

    def vector(dve):
        def norm_a(n):
            wait(dve, moments_done, n)
            for t in range(FTT):
                last = nc.vector.bn_stats(stats[:, t, :], tile(n, t))
            last.then_inc(stats_done, 1)
            wait(dve, xhat_done, n)
            dve.wait_ge(stats_done, n + 1)
            nc.vector.memset(unread[:, :], 0.0)
            for t in range(FTT):
                last = nc.vector.bn_aggr(moments[:, t, :], stats[:, t, :])
            last.then_inc(moments_done, 1)

        def norm_b(n):
            dve.wait_ge(rstd_done, n + 1)
            wait(dve, turned, n)
            for t in range(FTT):
                last = nc.vector.tensor_scalar(xhat[:, t, :], tile(n, t), moments[:, t, 0:1], rstd[:, t:t + 1], ALU.subtract, ALU.mult)
            last.then_inc(xhat_done, 1)

        def high(layer, n, k):
            if not split:
                return
            dve.wait_ge(full_done[layer], n * blocks[layer] + (k + 1))
            wait(dve, psum_done[layer], n * sums[layer])
            nc.vector.tensor_copy(hi[layer][:, k, :], full[layer][:, k, :]).then_inc(hi_done[layer], 1)
            if low_on_dve(layer, k):
                make_low(dve, nc.vector.tensor_tensor, layer, n, k)

        def modulate(n):
            dve.wait_ge(turned, n + 1)
            wait(dve, psum_done[0], n * KH)
            for i in range(FB):
                last = nc.vector.tensor_scalar(full[0][:, 0, i * T:(i + 1) * T], bank[6][:, i * T:(i + 1) * T],
                                               col(modcol[:, 2, :], n, i), col(modcol[:, 3, :], n, i), ALU.mult, ALU.add)
            last.then_inc(full_done[0], 1)

        def gate(n, m):
            dve.wait_ge(tanh_done, n * KH + (m + 1))
            wait(dve, full_done[1], n * KH + (m - 1))
            nc.vector.scalar_tensor_tensor(out=gated[:, m % 2, :], in0=tanh[:, m % 2, :], scalar=1.0, in1=bank[pair(n, m)],
                                           op0=ALU.add, op1=ALU.mult).then_inc(gated_done, 1)
            dve.wait_ge(gated_done, n * KH + (m + 1))
            wait(dve, psum_done[1], n * KH)
            nc.vector.scalar_tensor_tensor(out=full[1][:, m, :], in0=bank[pair(n, m) + 1], scalar=scales[:, 1, m:m + 1],
                                           in1=gated[:, m % 2, :], op0=ALU.mult, op1=ALU.mult).then_inc(full_done[1], 1)

        def y_out(n):
            dve.wait_ge(psum_done[3], n + 1)
            wait(dve, turned_back, n)
            for i in range(FB):
                last = nc.vector.tensor_scalar(y[:, i * T:(i + 1) * T], bank[7][:, i * T:(i + 1) * T],
                                               col(out_scale, n, i), None, ALU.mult)
            last.then_inc(y_done, 1)

        def residual(n):
            dve.wait_ge(turned_back, n + 1)
            nc.vector.tensor_tensor(tiles(n), tiles(n), bank[6].rearrange("p (t d) -> p t d", t=FTT), ALU.add).then_inc(x_done, 1)

        def step(n):
            first, gated_next, norms = isinstance(n, int) and n == 0, not is_last(n, 1), not is_last(n, 2)
            if norms:
                norm_a(n + 2)
            for k in range(KH):
                high(2, n, k)
            if gated_next:
                gate(n + 1, 0)
            if not first:
                y_out(n - 1)
            if norms:
                norm_b(n + 2)
            for m in range(1, KH):
                if m == 3 and not first:
                    residual(n - 1)
                if gated_next:
                    gate(n + 1, m)
            for k in range(KH):
                high(3, n, k)
            if norms:
                modulate(n + 2)
                high(0, n + 2, 0)

        norm_a(0)
        norm_b(0)
        modulate(0)
        high(0, 0, 0)
        norm_a(1)
        norm_b(1)
        for m in range(KH):
            gate(0, m)
        modulate(1)
        high(0, 1, 0)
        step(0)
        with dve.Fori(1, NT - 2) as n:
            step(n)
        step(NT - 2)
        step(NT - 1)
        y_out(NT - 1)
        residual(NT - 1)

    return {"sync": sync, "tensor": tensor, "scalar": scalar, "gpsimd": gpsimd, "vector": vector}


def ffn_1_setup(nc, ctx, dram, sbuf, psum):
    def sem(name):
        return dram["semaphores"].enter_context(nc.semaphore("s2_" + name))

    def sb(name, shape, dt=F32):
        return ctx.enter_context(nc.sbuf_tensor("s2_" + name, shape, dt))

    ident, weights, weights_r, scales = (sbuf[k] for k in ("ident", "weights", "weights_r", "scales"))
    w_loaded = dram["ffn_loaded"]
    scales_loaded, rounded, compared, least, moved, scaled = map(sem, ("scales_loaded", "rounded", "compared", "least", "moved", "scaled"))
    taken_off, sizes, piece_sums = sb("taken_off", [P, WEIGHTS]), sb("sizes", [P, WEIGHTS]), sb("piece_sums", [P, PIECES])
    worst, total, raw = sb("worst", [P, 1]), sb("total", [1, 1]), sb("raw", [P, 5, KH])
    worst_done = sem("worst")

    with nc.Block() as block:
        @block.sync
        def _(sp):
            sp.dma_start(raw[:, :, :].rearrange("p i k -> p (i k)"), sbuf["scales_in"]).then_inc(scales_loaded, 16)

        @block.scalar
        def _(act):
            act.wait_ge(w_loaded, 16 * len(dram["ffn_loads"]))
            nc.scalar.copy(weights_r[:, 0:H2], weights[:, 0:H2]).then_inc(rounded, 1)
            for i in range(PIECES):
                part = slice(i * WEIGHTS // PIECES, (i + 1) * WEIGHTS // PIECES)
                act.wait_ge(compared, i + 1)
                last = nc.scalar.activation(sizes[:, part], taken_off[:, part], ACT.Abs, accum_out=piece_sums[:, i:i + 1])
            last.then_inc(least, 1)

        @block.tensor
        def _(pe):
            pe.wait_ge(worst_done, 1)
            nc.tensor.matmul(psum[0:1, 0:P], worst[:, :], ident[:, :], start=True, stop=True).then_inc(moved, 1)

        @block.vector
        def _(dve):
            dve.wait_ge(w_loaded, 16 * len(dram["ffn_loads"]))
            dve.wait_ge(scales_loaded, 16)
            nc.vector.tensor_scalar(scales[:, 0, :], raw[:, 0, :], 0.5, None, ALU.mult)
            nc.vector.scalar_tensor_tensor(out=scales[:, 1, :], in0=raw[:, 0, :], scalar=0.5, in1=raw[:, 1, :], op0=ALU.mult, op1=ALU.mult)
            nc.vector.tensor_copy(scales[:, 2:4, :], raw[:, 2:4, :])
            nc.vector.tensor_scalar(sbuf["out_scale"][:, :], sbuf["modcol"][:, 4, :], raw[:, 4, 0:1], None, ALU.mult)
            nc.vector.tensor_copy(weights_r[:, H2:], weights[:, H2:]).then_inc(scaled, 1)
            dve.wait_ge(scaled, 1)
            dve.wait_ge(rounded, 1)
            for i in range(PIECES):
                part = slice(i * WEIGHTS // PIECES, (i + 1) * WEIGHTS // PIECES)
                nc.vector.tensor_tensor(taken_off[:, part], weights[:, part], weights_r[:, part].bitcast(F32), ALU.subtract).then_inc(compared, 1)
            dve.wait_ge(least, 1)
            nc.vector.tensor_reduce(worst[:, :], piece_sums[:, :], AX.X, ALU.max).then_inc(worst_done, 1)
            dve.wait_ge(moved, 1)
            nc.vector.tensor_reduce(total[:, :], psum[0:1, 0:P], AX.X, ALU.max).then_inc(scaled, 1)
            dve.wait_ge(scaled, 2)
            nc.vector.tensor_scalar(sbuf["exact_weights"][:, :], total[:, :], EXACT_BELOW, None, ALU.is_le)


def adaln_program(nc, ins, out):
    with ExitStack() as ctx:
        def sb(name, shape, dt=F32):
            return ctx.enter_context(nc.sbuf_tensor(name, shape, dt))

        psum_all = ctx.enter_context(nc.psum_tensor("psum_all", [P, 8 * 512], F32))
        psum = psum_all[:, :]
        X = sb("X", [P, B * TT, D])
        sbuf = {
            "X": X, "ident": sb("ident", [P, P]), "ident16": sb("ident16", [P, P], F16),
            "modcol": sb("modcol", [P, 5, B]), "minus_half": sb("minus_half", [P, 8]),
            "eps": sb("eps", [P, 8]), "biases": sb("biases", [P, 3]),
        }
        x_view = ins["x"].rearrange("b (t p) d -> p (b t) d", p=P)
        out_view = out.rearrange("b (t p) d -> p (b t) d", p=P)
        table = nc.dram_tensor("modulation_table", [B, ROWS, D], F32, kind="Internal").ap()
        dram = {
            "x": x_view, "table": table,
            "condT": [ins["c0T"], ins["c1T"]], "wmod": [ins["wmod0"], ins["wmod1"]],
            "bo": [ins["bo0"], ins["bo1"]],
        }
        dram["semaphores"] = ctx
        dram["out"], dram["out_stored"] = out_view, ctx.enter_context(nc.semaphore("out_stored"))
        dram["loads"] = [(sbuf["ident"][:, :], ins["ident"])]
        dram["fills"] = [(sbuf["minus_half"][:, :], -0.5), (sbuf["eps"][:, :], LN_EPS)]
        dram["fills"] += [(sbuf["biases"][:, i:i + 1], v) for i, v in enumerate((-COLLAPSE * SHARPNESS, 0.625, 0.3125))]
        dram["experts_loaded"], dram["ffn_loaded"] = ctx.enter_context(nc.semaphore("experts_loaded")), ctx.enter_context(nc.semaphore("ffn_loaded"))
        sbuf["wqk1"], sbuf["wv1"], sbuf["wo1"] = sb("wqk1", [P, 2 * D]), sb("wv1", [P, D]), sb("wo1", [P, D])
        sbuf["bqk1"], sbuf["bv1"], sbuf["rope"] = sb("bqk1", [P, 2 * D]), sb("bv1", [P, TT * D]), sb("rope", [P, 2, TT, HD])
        dram["loads"] += [
            (sbuf["wqk1"][:, :], ins["wqk1"]), (sbuf["wv1"][:, :], ins["wv1"]), (sbuf["wo1"][:, :], ins["wo1"]),
            (sbuf["bqk1"][:, :], ins["bqk1"].partition_broadcast(P)),
            (sbuf["bv1"][:, :], ins["bv1"].partition_broadcast(P)),
            (sbuf["rope"][:, :, :, :].rearrange("p i t d -> p (i t d)"), ins["rope"])]

        def either(eng, flag, name, with_flag, without_flag):
            value = eng.value_load(flag[0:1, 0:1], min_val=0, max_val=1)
            with eng.If(value == 1):
                with_flag[name](eng)
            with eng.Else():
                without_flag[name](eng)

        with ExitStack() as layer:
            def sbe(name, shape, dt=F32):
                return layer.enter_context(nc.sbuf_tensor(name, shape, dt))
            ctrl, f1, f2 = sbe("ctrl", [P, SLOTS]), sbe("f1", [P, SLOTS, NF]), sbe("f2", [P, NE, D])
            ebias, tie, own = sbe("ebias", [P, NE]), sbe("tie", [P, GT]), sbe("own", [P, TG])
            sbuf["experts"] = ctrl, f1, f2, ebias, tie, own
            dram["experts_loads"] = [
                (ctrl[:, :], ins["ctrl"]), (f1[:, :, :].rearrange("p s f -> p (s f)"), ins["f1"]), (f2[:, :, :], ins["f2"]),
                (ebias[:, :], ins["ebias"]), (tie[:, :], ins["tie"].partition_broadcast(P)), (own[:, :], ins["own"])]
            with ExitStack() as part:
                def sb0(name, shape, dt=F32):
                    return part.enter_context(nc.sbuf_tensor(name, shape, dt))
                sbuf["kmask"] = [sb0(f"kmask{i}", [P, H, T], F16) for i in range(2)]
                sbuf["vpad"] = [sb0(f"vpad{i}", [P, TT, H, 32]) for i in range(2)]
                sbuf["probs"] = sb0("probs", [P, 4, G, UNIT_PAD])
                sbuf["wqk0"], sbuf["wv0"], sbuf["wo0"] = sb0("wqk0", [P, 2 * D]), sb0("wv0", [P, D]), sb0("wo0", [P, D])
                sbuf["gamma"], sbuf["beta"], sbuf["gqk"] = sb0("gammacol", [P, 1]), sb0("betacol", [P, 1]), sb0("gqk", [P, 2, D])
                dram["loads"] += [
                    (sbuf["wqk0"][:, :], ins["wqk0"]), (sbuf["wv0"][:, :], ins["wv0"]), (sbuf["wo0"][:, :], ins["wo0"]),
                    (sbuf["gamma"][:, :], ins["gamma"]), (sbuf["beta"][:, :], ins["beta"]),
                    (sbuf["gqk"][:, :, :].rearrange("p a d -> p (a d)"), ins["gqk"].partition_broadcast(P)),
                    (sbuf["ident16"][:, :], ins["ident16"]),
                ]
                dram["fills"] += [(k[:, :, :], 0.0) for k in sbuf["kmask"]] + [(v[:, :, :, :], 0.0) for v in sbuf["vpad"]]
                dram["fills"] += [(sbuf["probs"][:, :, :, T:UNIT_PAD], 1.0)]
                with ExitStack() as first:
                    setup_phase(nc, first, dram, sbuf, psum)
                with ExitStack() as first:
                    attention_0(nc, first, dram, sbuf, psum)
            with ExitStack() as first:
                experts_0(nc, first, dram, sbuf, psum)
        with ExitStack() as layer:
            def sb2(name, shape, dt=F32):
                return layer.enter_context(nc.sbuf_tensor(name, shape, dt))
            sbuf["weights"] = sb2("weights", [P, WEIGHTS])
            sbuf["scales"], sbuf["out_scale"] = sb2("scales", [P, 4, KH]), sb2("out_scale", [P, B])
            sbuf["exact_weights"], sbuf["scales_in"], sbuf["ffn"] = sb2("exact_weights", [1, 1], I32), ins["scales"], {}
            dram["ffn_loads"] = [(sbuf["weights"][:, lo:hi], ins[k]) for k, lo, hi in (
                ("w1", W1, W2), ("w2", W2, H1), ("h1", H1, H2), ("h2", H2, W3), ("w3", W3, WEIGHTS))]
            with ExitStack() as part:
                def sb1(name, shape, dt=F32):
                    return part.enter_context(nc.sbuf_tensor(name, shape, dt))
                sbuf["kmask1"] = [sb1(f"kmask1_{i}", [P, H, T], F32R) for i in range(2)]
                sbuf["vpad1"] = [sb1(f"vpad1_{i}", [P, TT, H, 32]) for i in range(2)]
                sbuf["sel"], sbuf["sel_loaded"] = sb1("sel", [P, H, P], F32R), sb1("sel_loaded", [P, H, P])
                sbuf["ident_r"] = sb1("ident_r", [P, P], F32R)
                sbuf["small_scores"] = small = sb1("small_scores", [1, 1], I32)
                sbuf["a1"], dram["sel"] = {}, ins["sel"]
                general = attention_1(nc, part, dram, sbuf, psum, True)
                bounded = attention_1(nc, part, dram, sbuf, psum, False)
                with ExitStack() as first:
                    attention_1_setup(nc, first, dram, sbuf, psum)
                with nc.Block() as block:
                    @block.sync
                    def _(sp):
                        either(sp, small, "sync", bounded, general)

                    @block.tensor
                    def _(pe):
                        either(pe, small, "tensor", bounded, general)

                    @block.scalar
                    def _(act):
                        either(act, small, "scalar", bounded, general)

                    @block.gpsimd
                    def _(pool):
                        either(pool, small, "gpsimd", bounded, general)

                    @block.vector
                    def _(dve):
                        either(dve, small, "vector", bounded, general)
            sbuf["weights_r"] = sb2("weights_r", [P, WEIGHTS], F32R)
            with ExitStack() as first:
                ffn_1_setup(nc, first, dram, sbuf, psum)
            with ExitStack() as part:
                general = ffn_1(nc, part, dram, sbuf, psum, False)
                exact = ffn_1(nc, part, dram, sbuf, psum, True)
                fits = sbuf["exact_weights"]
                with nc.Block() as block:
                    @block.sync
                    def _(sp):
                        either(sp, fits, "sync", exact, general)

                    @block.tensor
                    def _(pe):
                        either(pe, fits, "tensor", exact, general)

                    @block.scalar
                    def _(act):
                        either(act, fits, "scalar", exact, general)

                    @block.gpsimd
                    def _(pool):
                        either(pool, fits, "gpsimd", exact, general)

                    @block.vector
                    def _(dve):
                        either(dve, fits, "vector", exact, general)
DEBUG = {}


def kernel(**inputs):
    import concourse.bacc as bacc
    from concourse.bass_utils import run_bass_kernel_spmd

    a = {k: np.asarray(v) for k, v in inputs.items()}
    c = np.ascontiguousarray
    f32 = np.float32
    inv_freq = f32(1.0) / np.power(f32(10000.0), np.arange(0, HD, 2, dtype=f32) / f32(HD))
    angle = (np.arange(T, dtype=f32)[:, None] * inv_freq[None, :].astype(f32)).astype(f32)
    cos, sin = np.cos(angle).astype(f32), np.sin(angle).astype(f32)
    rope = np.stack([np.concatenate([cos, cos], 1), np.concatenate([-sin, sin], 1)])
    sel = np.zeros((P, H, P), f32)
    for head in range(H):
        sel[head, head] = sel[H + head, head] = 1.0
    order = [G * j + 2 * s + i for s in range(2) for j in range(G) for i in range(2)]
    def inputs_first(w):
        return c(w.T.reshape(-1, P, w.shape[0]).transpose(1, 0, 2).reshape(P, -1))

    def by_block(s):
        return s.reshape(KH, P).T

    w3_s = np.repeat(a["L1_ffn_w3_s"][:, None], KH, axis=1)
    arrays = {
        "w1": inputs_first(a["L1_ffn_w1_w"]), "w2": inputs_first(a["L1_ffn_w2_w"]), "h1": inputs_first(a["L1_ffn_h1_w"]),
        "h2": inputs_first(a["L1_ffn_h2_w"]), "w3": inputs_first(a["L1_ffn_w3_w"]),
        "scales": c(np.concatenate([by_block(a["L1_ffn_w1_s"]), by_block(a["L1_ffn_w2_s"]), by_block(a["L1_ffn_h1_s"]),
                                    by_block(a["L1_ffn_h2_s"]), w3_s], axis=1)),
        "wqk1": c(np.concatenate([a["L1_attn_Wq"], a["L1_attn_Wk"]], axis=1)), "wv1": c(a["L1_attn_Wv"]),
        "wo1": c(a["L1_attn_Wo"].reshape(H, HD, D)[order].reshape(D, D)),
        "bqk1": c(np.concatenate([a["L1_attn_bq"], a["L1_attn_bk"]])), "bv1": c(np.tile(a["L1_attn_bv"], TT)),
        "rope": c(rope.reshape(2, TT, P, HD).transpose(2, 0, 1, 3).reshape(P, 2 * TT * HD)),
        "sel": c(sel.reshape(P, H * P)),
        "x": c(a["L0_attn_x"]),
        "c0T": c(a["L0_c"].T), "c1T": c(a["L1_c"].T), "wmod0": c(a["L0_wmod"]), "wmod1": c(a["L1_wmod"]),
        "bo0": c(a["L0_attn_b_o"]), "bo1": c(a["L1_attn_bo"]),
        "wqk0": c(np.concatenate([a["L0_attn_w_q"], a["L0_attn_w_k"]], axis=1)),
        "wv0": c(a["L0_attn_w_v"]), "wo0": c(a["L0_attn_w_o"]),
        "gamma": c(a["L0_attn_gamma"][:, None]), "beta": c(a["L0_attn_beta"][:, None]),
        "gqk": c(np.concatenate([np.tile(a["L0_attn_g_q"], H), np.tile(a["L0_attn_g_k"], H)])),
        "ctrl": c(a["L0_ffn_controller"].reshape(D, SLOTS)), "f1": c(a["L0_ffn_f1"].reshape(D, SLOTS * NF)),
        "f2": c(a["L0_ffn_f2"].transpose(1, 2, 0, 3).reshape(NS_ * NF, NE, D)),
        "ebias": c(a["L0_ffn_bias"].transpose(1, 2, 0).reshape(NS_ * NF, NE)),
        "tie": (np.arange(GT, dtype=f32) * f32(1e-6 / (GT - 1))).astype(f32),
        "own": np.kron(np.eye(TG, dtype=f32), np.ones((GT, 1), f32)),
        "ident": np.eye(P, dtype=f32), "ident16": np.eye(P, dtype=np.float16),
    }
    nc = bacc.Bacc("TRN2", target_bir_lowering=False, num_devices=1)
    ins = {k: nc.dram_tensor(f"in_{k}", v.shape, mybir.dt.from_np(v.dtype), kind="ExternalInput").ap() for k, v in arrays.items()}
    out = nc.dram_tensor("out", a["L0_attn_x"].shape, F32, kind="ExternalOutput").ap()
    adaln_program(nc, ins, out)
    return run_bass_kernel_spmd(nc, [{f"in_{k}": v for k, v in arrays.items()}], core_ids=[0]).results[0]["out"]
```
